# Optimizing a Trainium2 kernel written in Bass

```python
import numpy as np
import jax
import jax.numpy as jnp

def _softmax(x, axis=-1):
    return jax.nn.softmax(x, axis=axis)

def _gelu(x):
    return jax.nn.gelu(x, approximate=True)

def _silu(x):
    return jax.nn.silu(x)

def _sigmoid(x):
    return jax.nn.sigmoid(x)

def _layernorm(x, axis=-1, eps=1e-05):
    m = jnp.mean(x, axis=axis, keepdims=True)
    v = jnp.var(x, axis=axis, keepdims=True)
    return (x - m) / jnp.sqrt(v + eps)

def _scatter_add(tgt, idx, src, axis=0):
    return tgt.at[idx].add(src)

def _segment_sum(src, seg, n):
    return jax.ops.segment_sum(src, seg, n)
kernel_name = 'mk_gnn_ffn_d2_gnn_r16_5592f5'

def setup_inputs(seed: int=0):
    np.random.seed(seed)
    _w = jnp.asarray

    def _rec_inputs():
        import jax
        import jax.numpy as jnp
        _gk = jax.random.key(seed)
        x = -0.0003713 + 1 * jax.random.normal(jax.random.fold_in(_gk, 1), (3125, 256), jnp.float32)
        _s = jax.random.randint(jax.random.fold_in(_gk, 2), (50000,), 0, 3125, jnp.int32)
        _d = jax.random.randint(jax.random.fold_in(_gk, 3), (50000,), 0, 3125, jnp.int32)
        _loop = jnp.arange(3125, dtype=jnp.int32)
        src = jnp.concatenate([_s, _d, _loop])
        dst = jnp.concatenate([_d, _s, _loop])
        _o = jnp.argsort(dst, stable=True)
        src = src[_o]
        dst = dst[_o]
        return (x, src, dst)
    x, src, dst = _rec_inputs()

    def _L0_gnn_setup():
        import jax, jax.numpy as jnp
        import numpy as np
        N = 3125
        E = 50000
        DIN = 256
        DOUT = 64
        H = 4
        NEG_SLOPE = 0.01
        key = jax.random.key(seed)
        k0, k1, k2, k3, k4 = jax.random.split(key, 5)
        h = jax.random.normal(k0, (N, DIN), dtype=jnp.float32)
        src = jax.random.randint(k1, (E,), 0, N)
        dst = jax.random.randint(k2, (E,), 0, N)
        W = jax.random.normal(k3, (H, DOUT, DIN), dtype=jnp.float32) * np.float32(np.sqrt(2.0) * np.sqrt(2.0 / (DIN + DOUT)))
        att = jax.random.normal(k4, (H, 2 * DOUT), dtype=jnp.float32) * np.float32(np.sqrt(2.0) * np.sqrt(2.0 / (2 * DOUT + 1)))
        return {'h': h, 'src': src, 'dst': dst, 'W': W, 'att': att}
    _L0_gnn_all = _L0_gnn_setup()
    _L0_gnn_in = {k: v for k, v in _L0_gnn_all.items() if k in ('W', 'att')}
    del _L0_gnn_all

    def _L0_ffn_setup():
        import jax, jax.numpy as jnp
        import numpy as np
        B, A = (256, 8)
        IN, OUT = (256, 256)
        SH1, SH2 = (256, 128)
        EH1, EH2 = (128, 64)
        E, TOPK = (4, 2)

        def _shared_mlp(x, W1, b1, W2, b2, W3, b3):
            h = jax.nn.relu(x @ W1 + b1)
            h = jax.nn.relu(h @ W2 + b2)
            return h @ W3 + b3

        def _experts_mlp(x, eW1, eb1, eW2, eb2, eW3, eb3):
            h = jax.nn.relu(jnp.einsum('baf,efh->ebah', x, eW1) + eb1[:, None, None, :])
            h = jax.nn.relu(jnp.einsum('ebah,ehg->ebag', h, eW2) + eb2[:, None, None, :])
            o = jnp.einsum('ebag,ego->ebao', h, eW3) + eb3[:, None, None, :]
            return jnp.moveaxis(o, 0, -1)
        key = jax.random.key(seed)
        ks = jax.random.split(key, 16)
        s = 0.05
        return {'x': jax.random.normal(ks[0], (B, A, IN), jnp.float32), 'sW1': jax.random.normal(ks[1], (IN, SH1), jnp.float32) * s, 'sb1': jnp.zeros((SH1,), jnp.float32), 'sW2': jax.random.normal(ks[2], (SH1, SH2), jnp.float32) * s, 'sb2': jnp.zeros((SH2,), jnp.float32), 'sW3': jax.random.normal(ks[3], (SH2, OUT), jnp.float32) * s, 'sb3': jnp.zeros((OUT,), jnp.float32), 'eW1': jax.random.normal(ks[4], (E, IN, EH1), jnp.float32) * s, 'eb1': jnp.zeros((E, EH1), jnp.float32), 'eW2': jax.random.normal(ks[5], (E, EH1, EH2), jnp.float32) * s, 'eb2': jnp.zeros((E, EH2), jnp.float32), 'eW3': jax.random.normal(ks[6], (E, EH2, OUT), jnp.float32) * s, 'eb3': jnp.zeros((E, OUT), jnp.float32), 'gW': jax.random.normal(ks[7], (IN, E), jnp.float32) * s, 'gb': jnp.zeros((E,), jnp.float32)}
    _L0_ffn_all = _L0_ffn_setup()
    _L0_ffn_in = {k: v for k, v in _L0_ffn_all.items() if k in ('sW1', 'sb1', 'sW2', 'sb2', 'sW3', 'sb3', 'eW1', 'eb1', 'eW2', 'eb2', 'eW3', 'eb3', 'gW', 'gb')}
    del _L0_ffn_all

    def _L1_gnn_setup():
        import jax, jax.numpy as jnp
        import numpy as np
        N_NODES = 6250
        F_DIM = 256
        NNZ = 100000

        def _prelu(x, a):
            return jnp.where(x >= 0, x, a * x)

        def _hconv(x, W, b, src, dst, n):
            xt = x @ W
            ones = jnp.ones(src.shape, xt.dtype)
            D = jax.ops.segment_sum(ones, src, num_segments=n)
            B = jax.ops.segment_sum(ones, dst, num_segments=n)
            Dinv = jnp.where(D > 0, 1.0 / D, 0.0)
            Binv = jnp.where(B > 0, 1.0 / B, 0.0)
            m = jax.ops.segment_sum(xt[src], dst, num_segments=n) * Binv[:, None]
            out = jax.ops.segment_sum(m[dst], src, num_segments=n) * Dinv[:, None]
            return out + b
        key = jax.random.key(seed)
        k0, k1, k2, k3 = jax.random.split(key, 4)
        x = jax.random.normal(k0, (N_NODES, F_DIM), dtype=jnp.float32)
        edge_index = jax.random.randint(k1, (2, NNZ), 0, N_NODES, dtype=jnp.int32)
        scale = (2.0 / F_DIM) ** 0.5
        W1 = jax.random.normal(k2, (F_DIM, F_DIM), dtype=jnp.float32) * scale
        W2 = jax.random.normal(k3, (F_DIM, F_DIM), dtype=jnp.float32) * scale
        b1 = jnp.zeros((F_DIM,), jnp.float32)
        b2 = jnp.zeros((F_DIM,), jnp.float32)
        a = jnp.full((1,), 0.25, jnp.float32)
        return {'x': x, 'edge_index': edge_index, 'W1': W1, 'b1': b1, 'W2': W2, 'b2': b2, 'a': a}
    _L1_gnn_all = _L1_gnn_setup()
    _L1_gnn_in = {k: v for k, v in _L1_gnn_all.items() if k in ('W1', 'b1', 'W2', 'b2', 'a')}
    del _L1_gnn_all

    def _L1_ffn_setup():
        import jax, jax.numpy as jnp
        import numpy as np
        B, S, D = (8, 256, 256)
        H = 4 * D
        CAPACITY = 0.5
        key = jax.random.key(seed)
        ks = jax.random.split(key, 6)
        x = jax.random.normal(ks[0], (B, S, D), dtype=jnp.float32)
        attention_mask = jnp.zeros((B, 1, 1, S), dtype=jnp.float32)
        wr = jax.random.normal(ks[1], (D, 1), dtype=jnp.float32) * 0.02
        br = jnp.zeros((1,), dtype=jnp.float32)
        w1 = jax.random.normal(ks[2], (D, H), dtype=jnp.float32) * 0.02
        b1 = jnp.zeros((H,), dtype=jnp.float32)
        w2 = jax.random.normal(ks[3], (H, D), dtype=jnp.float32) * 0.02
        b2 = jnp.zeros((D,), dtype=jnp.float32)
        return {'x': x, 'attention_mask': attention_mask, 'wr': wr, 'br': br, 'w1': w1, 'b1': b1, 'w2': w2, 'b2': b2}
    _L1_ffn_all = _L1_ffn_setup()
    _L1_ffn_in = {k: v for k, v in _L1_ffn_all.items() if k in ('attention_mask', 'wr', 'br', 'w1', 'b1', 'w2', 'b2')}
    del _L1_ffn_all
    return {'x': x, 'src': src, 'dst': dst, 'L0_gnn_W': _L0_gnn_in['W'], 'L0_gnn_att': _L0_gnn_in['att'], 'L0_ffn_sW1': _L0_ffn_in['sW1'], 'L0_ffn_sb1': _L0_ffn_in['sb1'], 'L0_ffn_sW2': _L0_ffn_in['sW2'], 'L0_ffn_sb2': _L0_ffn_in['sb2'], 'L0_ffn_sW3': _L0_ffn_in['sW3'], 'L0_ffn_sb3': _L0_ffn_in['sb3'], 'L0_ffn_eW1': _L0_ffn_in['eW1'], 'L0_ffn_eb1': _L0_ffn_in['eb1'], 'L0_ffn_eW2': _L0_ffn_in['eW2'], 'L0_ffn_eb2': _L0_ffn_in['eb2'], 'L0_ffn_eW3': _L0_ffn_in['eW3'], 'L0_ffn_eb3': _L0_ffn_in['eb3'], 'L0_ffn_gW': _L0_ffn_in['gW'], 'L0_ffn_gb': _L0_ffn_in['gb'], 'L1_gnn_W1': _L1_gnn_in['W1'], 'L1_gnn_b1': _L1_gnn_in['b1'], 'L1_gnn_W2': _L1_gnn_in['W2'], 'L1_gnn_b2': _L1_gnn_in['b2'], 'L1_gnn_a': _L1_gnn_in['a'], 'L1_ffn_attention_mask': _L1_ffn_in['attention_mask'], 'L1_ffn_wr': _L1_ffn_in['wr'], 'L1_ffn_br': _L1_ffn_in['br'], 'L1_ffn_w1': _L1_ffn_in['w1'], 'L1_ffn_b1': _L1_ffn_in['b1'], 'L1_ffn_w2': _L1_ffn_in['w2'], 'L1_ffn_b2': _L1_ffn_in['b2']}

def reference(x, src, dst, L0_gnn_W, L0_gnn_att, L0_ffn_sW1, L0_ffn_sb1, L0_ffn_sW2, L0_ffn_sb2, L0_ffn_sW3, L0_ffn_sb3, L0_ffn_eW1, L0_ffn_eb1, L0_ffn_eW2, L0_ffn_eb2, L0_ffn_eW3, L0_ffn_eb3, L0_ffn_gW, L0_ffn_gb, L1_gnn_W1, L1_gnn_b1, L1_gnn_W2, L1_gnn_b2, L1_gnn_a, L1_ffn_attention_mask, L1_ffn_wr, L1_ffn_br, L1_ffn_w1, L1_ffn_b1, L1_ffn_w2, L1_ffn_b2):
    import jax
    import jax.numpy as jnp

    def _L0_gnn_ref(h, src, dst, W, att):
        import jax, jax.numpy as jnp
        import numpy as np
        N = 3125
        E = 50000
        DIN = 256
        DOUT = 64
        H = 4
        NEG_SLOPE = 0.01
        z = jnp.einsum('ni,hoi->hno', h, W)
        a_src, a_dst = (att[:, :DOUT], att[:, DOUT:])
        e_src = jnp.einsum('hno,ho->hn', z, a_src)
        e_dst = jnp.einsum('hno,ho->hn', z, a_dst)
        e = e_src[:, src] + e_dst[:, dst]
        e = jnp.where(e > 0, e, NEG_SLOPE * e)

        def per_head(e_h, z_h):
            m = jax.ops.segment_max(e_h, dst, num_segments=N)
            m = jnp.where(jnp.isfinite(m), m, 0.0)
            ex = jnp.exp(e_h - m[dst])
            den = jax.ops.segment_sum(ex, dst, num_segments=N)
            alpha = ex / jnp.maximum(den[dst], jnp.float32(1e-16))
            return jax.ops.segment_sum(alpha[:, None] * z_h[src], dst, num_segments=N)
        out = jax.vmap(per_head)(e, z)
        return jnp.transpose(out, (1, 0, 2)).reshape(N, H * DOUT)

    def _L0_ffn_ref(x, sW1, sb1, sW2, sb2, sW3, sb3, eW1, eb1, eW2, eb2, eW3, eb3, gW, gb):
        import jax, jax.numpy as jnp
        import numpy as np
        B, A = (256, 8)
        IN, OUT = (256, 256)
        SH1, SH2 = (256, 128)
        EH1, EH2 = (128, 64)
        E, TOPK = (4, 2)

        def _shared_mlp(x, W1, b1, W2, b2, W3, b3):
            h = jax.nn.relu(x @ W1 + b1)
            h = jax.nn.relu(h @ W2 + b2)
            return h @ W3 + b3

        def _experts_mlp(x, eW1, eb1, eW2, eb2, eW3, eb3):
            h = jax.nn.relu(jnp.einsum('baf,efh->ebah', x, eW1) + eb1[:, None, None, :])
            h = jax.nn.relu(jnp.einsum('ebah,ehg->ebag', h, eW2) + eb2[:, None, None, :])
            o = jnp.einsum('ebag,ego->ebao', h, eW3) + eb3[:, None, None, :]
            return jnp.moveaxis(o, 0, -1)
        all_out = _experts_mlp(x, eW1, eb1, eW2, eb2, eW3, eb3)
        shared = _shared_mlp(x, sW1, sb1, sW2, sb2, sW3, sb3)
        gates = jax.nn.softmax(x @ gW + gb, axis=-1)
        topv, topi = jax.lax.top_k(gates, TOPK)
        topw = jax.nn.softmax(topv, axis=-1)
        sel = jnp.take_along_axis(all_out, topi[:, :, None, :], axis=-1)
        gated = jnp.sum(sel * topw[:, :, None, :], axis=-1)
        return shared + gated

    def _L1_gnn_ref(x, edge_index, W1, b1, W2, b2, a):
        import jax, jax.numpy as jnp
        import numpy as np
        N_NODES = 6250
        F_DIM = 256
        NNZ = 100000

        def _prelu(x, a):
            return jnp.where(x >= 0, x, a * x)

        def _hconv(x, W, b, src, dst, n):
            xt = x @ W
            ones = jnp.ones(src.shape, xt.dtype)
            D = jax.ops.segment_sum(ones, src, num_segments=n)
            B = jax.ops.segment_sum(ones, dst, num_segments=n)
            Dinv = jnp.where(D > 0, 1.0 / D, 0.0)
            Binv = jnp.where(B > 0, 1.0 / B, 0.0)
            m = jax.ops.segment_sum(xt[src], dst, num_segments=n) * Binv[:, None]
            out = jax.ops.segment_sum(m[dst], src, num_segments=n) * Dinv[:, None]
            return out + b
        src, dst = (edge_index[0], edge_index[1])
        n = x.shape[0]
        h = _prelu(_hconv(x, W1, b1, src, dst, n), a)
        h = _hconv(h, W2, b2, src, dst, n) + x
        return _prelu(h, a)

    def _L1_ffn_ref(x, attention_mask, wr, br, w1, b1, w2, b2):
        import jax, jax.numpy as jnp
        import numpy as np
        B, S, D = (8, 256, 256)
        H = 4 * D
        CAPACITY = 0.5
        b, s, d = x.shape
        weights = (jnp.einsum('bsd,do->bso', x, wr) + br)[..., 0]
        k = max(1, int(CAPACITY * s))
        kk = k - 1 if k > 1 else 1
        _, idx = jax.lax.top_k(weights, k)
        sel_idx = idx[:, :kk]
        sel = jnp.take_along_axis(x, sel_idx[:, :, None], axis=1)
        h = jax.nn.gelu(jnp.einsum('bkd,dh->bkh', sel, w1) + b1)
        y = jnp.einsum('bkh,hd->bkd', h, w2) + b2
        w_sel = jnp.take_along_axis(weights, sel_idx, axis=1)
        y = y * w_sel[..., None]
        batch_idx = jnp.arange(b)[:, None]
        processed = jnp.zeros_like(x).at[batch_idx, sel_idx].set(y)
        return processed + x
    edge_index = jnp.stack([src, dst])
    x = x + _L0_gnn_ref(_layernorm(x, axis=-1), src, dst, L0_gnn_W, L0_gnn_att)
    x = x + _L0_ffn_ref(_layernorm(x, axis=-1)[None], L0_ffn_sW1, L0_ffn_sb1, L0_ffn_sW2, L0_ffn_sb2, L0_ffn_sW3, L0_ffn_sb3, L0_ffn_eW1, L0_ffn_eb1, L0_ffn_eW2, L0_ffn_eb2, L0_ffn_eW3, L0_ffn_eb3, L0_ffn_gW, L0_ffn_gb)[0]
    x = x + _L1_gnn_ref(_layernorm(x, axis=-1), edge_index, L1_gnn_W1, L1_gnn_b1, L1_gnn_W2, L1_gnn_b2, L1_gnn_a)
    x = x + _L1_ffn_ref(_layernorm(x, axis=-1)[None], L1_ffn_attention_mask, L1_ffn_wr, L1_ffn_br, L1_ffn_w1, L1_ffn_b1, L1_ffn_w2, L1_ffn_b2)[0]
    return x

_drawn_inputs = setup_inputs


def setup_inputs(seed=0):
    import zlib

    import numpy as np

    out = dict(_drawn_inputs(seed))
    spreads = {'L0_ffn_sb1': (0.0, 0.522),
     'L0_ffn_sb2': (0.0, 0.1),
     'L0_ffn_sb3': (0.0, 0.1),
     'L0_ffn_eb1': (0.0, 0.8),
     'L0_ffn_eb2': (0.0, 0.606),
     'L0_ffn_eb3': (0.0, 0.1),
     'L0_ffn_gb': (0.0, 0.518),
     'L1_gnn_b1': (0.0, 0.1),
     'L1_gnn_b2': (0.0, 0.1),
     'L1_ffn_b1': (0.0, 0.8),
     'L1_ffn_b2': (0.0, 0.8)}
    factors = {'L1_ffn_wr': 7.147, 'L1_ffn_w1': 8.0, 'L1_ffn_w2': 8.0}
    for name, (base, spread) in spreads.items():
        noise = np.random.default_rng([zlib.crc32(name.encode()), seed]).standard_normal(out[name].shape)
        drawn = base * np.exp(spread * noise) if base else spread * noise
        out[name] = jnp.asarray(drawn.astype(out[name].dtype))
    for name, factor in factors.items():
        out[name] = (out[name] * factor).astype(out[name].dtype)
    return out
```

```python
import concourse.bass as bass
from concourse import mybir
from contextlib import ExitStack, contextmanager

FP32 = mybir.dt.float32
BF16 = mybir.dt.bfloat16
I32 = mybir.dt.int32
ALU = mybir.AluOpType
ACT = mybir.ActivationFunctionType
AXX = mybir.AxisListType.X

N = 3125
P = 125
T = N // P
U = 5
F = 256
KF = F // 128
HEADS = 4
DH = F // HEADS
E = 103125
ROW = E // P
G = U
NG = N // G
SEG = 32
WIN = 256
NSEG = WIN // SEG
SROWS = 3240
PAD_KEY = 16000000.0
EPS = 1e-5
BIG = 1e30
BANKS = [(0, 1), (2, 3), (4,)]
QB = U * P
X3 = 770
PART = [(0, 257), (258, 256), (514, 256)]
D1 = DH + 1
W3 = 3 * D1
ARENA = T * HEADS * 2 * W3
WIDE = 30.0
MASK_SCALE = 2.0 ** 80


class Env:
    pass


@contextmanager
def scope(nc):
    with ExitStack() as ctx:
        sems = []

        def sb(name, shape, dt):
            return ctx.enter_context(nc.sbuf_tensor(name, shape, dt))

        def pb(name, shape, dt):
            return ctx.enter_context(nc.psum_tensor(name, shape, dt))

        def sem(name):
            sems.append(ctx.enter_context(nc.semaphore(name)))
            return sems[-1]

        yield sb, pb, sem
        if sems:
            with nc.Block() as block:
                @block.sync
                def _(sp):
                    for s in sems:
                        sp.sem_clear(s)


def layernorm_stats(nc, dve, v, X, st, mv, MV):
    with dve.Fori(0, U) as i:
        for u in range(U):
            v.bn_stats(out=st[:, u, :], in_=X[:, bass.ds(i * U + u, 1), :].rearrange("p a f -> p (a f)"))
        v.drain()
        for u in range(U):
            v.bn_aggr(out=mv[:, u, :], in_=st[:, u, :])
        v.drain()
        v.tensor_copy(MV[:, bass.ds(i * U, U), :], mv[:, :, :])
        v.drain()


def normalize_batch(v, X, H, MV, rstd, i, hready, t_ready, dve, first):
    for u in range(U):
        t = i * U + u
        if not first:
            dve.wait_ge(t_ready, 3 * (i - 1) + u // 2 + 1)
        v.tensor_scalar(H[:, u, :], X[:, bass.ds(t, 1), :].rearrange("p a f -> p (a f)"),
                        MV[:, bass.ds(t, 1), 0:1].rearrange("p a b -> p (a b)"),
                        rstd[:, bass.ds(t, 1)], ALU.subtract, ALU.mult).then_inc(hready, 1)


def setup_phase(k):
    nc = k.nc
    with scope(nc) as (sb, pb, sem):
        const_written = sem("const_written")
        iota_int = sb("iota_int", [128, P], I32)
        with nc.Block() as block:
            @block.gpsimd
            def _(pool):
                g = nc.gpsimd
                g.memset(k.ident[:, :], 0.0)
                g.memset(k.ones[:, :], 1.0)
                g.iota(iota_int[:, :], pattern=[[1, P]], base=0, channel_multiplier=0)
                g.drain()
                g.affine_select(out=k.ident[:, :], in_=k.ident[:, :], compare_op=ALU.not_equal, fill=1.0,
                                base=0, pattern=[[-1, 128]], channel_multiplier=1)
                g.tensor_copy(k.iota_row[:, :], iota_int[:, :])
                g.drain()
                g.tensor_copy(k.ident_bf[:, :], k.ident[:, :])
                g.drain()


def copy_transposed(act, a, ps_t, HT, t_ready, product_ready, ht_ready):
    def batch(i, first):
        for b, tiles in enumerate(BANKS):
            act.wait_ge(t_ready, 3 * i + b + 1)
            if not first:
                act.wait_ge(product_ready, 3 * (i - 1) + b + 1)
            n = len(tiles)
            a.activation(HT[:, :, tiles[0] * P:(tiles[0] + n) * P].rearrange("p q (u c) -> p u q c", c=P),
                         ps_t[:, b, 0:n * KF * P].rearrange("p (u q c) -> p u q c", u=n, c=P), ACT.Copy).then_inc(ht_ready, 1)

    batch(0, True)
    with act.Fori(1, U) as i:
        batch(i, False)


def transpose_batch(pe, t_, k, H, ps_t, h_ready, ht_ready, t_ready, i, first):
    for b, tiles in enumerate(BANKS):
        if not first:
            pe.wait_ge(ht_ready, 3 * (i - 1) + b + 1)
        pe.wait_ge(h_ready, U * i + tiles[-1] + 1)
        for s, u in enumerate(tiles):
            for q in range(KF):
                last = t_.transpose(ps_t[:, b, (s * KF + q) * P:(s * KF + q + 1) * P],
                                    H[:, u, q * 128:(q + 1) * 128], k.ident[0:P, 0:P])
        last.then_inc(t_ready, 1)


def gat_project_phase(k):
    nc = k.nc
    v, a, t_ = nc.vector, nc.scalar, nc.tensor
    with scope(nc) as (sb, pb, sem):
        X = sb("x_in", [P, T, F], FP32)
        H = sb("h_batch", [P, U, F], FP32)
        HT = sb("hT_batch", [128, KF, QB], FP32)
        w_rows = sb("w_rows", [128, KF, F], FP32)
        wT = sb("wT", [128, KF, F], FP32)
        att_b = sb("att_b", [P, 2, HEADS, DH], FP32)
        st = sb("bn_st", [P, U, 6], FP32)
        mv = sb("bn_mv", [P, U, 2], FP32)
        MV = sb("bn_all", [P, T, 2], FP32)
        std = sb("std", [P, T], FP32)
        rstd = sb("rstd", [P, T], FP32)
        eps = sb("eps", [P, 1], FP32)
        z = sb("z_batch", [P, U, HEADS, DH + 1], FP32)
        prod = sb("prod", [P, U, 2, HEADS, DH], FP32)
        ered = sb("ered", [P, U, 2, HEADS], FP32)
        esT = sb("esT", [HEADS * T, 2, P], FP32)
        ends = sb("es_ends", [P, 2, HEADS], FP32)
        ends8 = sb("es_ends8", [2 * HEADS, 1], FP32)
        diag8 = sb("es_diag8", [2 * HEADS, 2 * HEADS], FP32)
        limits = sb("es_limits", [P, 2, HEADS], FP32)
        wide = sb("es_wide", [P, HEADS], FP32)
        wide1 = sb("es_wide1", [P, 1], FP32)
        ps_t = pb("ps_t", [128, 3, 512], FP32)
        ps_z = pb("ps_z", [128, 3, 512], FP32)
        ps_w = pb("ps_w", [128, KF, F], FP32)
        x_loaded, w_loaded, att_loaded = sem("x_loaded"), sem("w_loaded"), sem("att_loaded")
        wt_psum, wt_ready = sem("wt_psum"), sem("wt_ready")
        stats_done, std_done = sem("stats_done"), sem("std_done")
        h_ready, t_ready, ht_ready = sem("h_ready"), sem("t_ready"), sem("ht_ready")
        z_ready, z_free = sem("z_ready"), sem("z_free")
        zs_ready, zs_free = sem("zs_ready"), sem("zs_free")
        es_done, esT_psum, esT_done, es_stored = sem("es_done"), sem("esT_psum"), sem("esT_done"), sem("es_stored")
        ends_done, ends_psum, diag_done, limits_psum = sem("ends_done"), sem("ends_psum"), sem("diag_done"), sem("limits_psum")
        with nc.Block() as block:
            @block.sync
            def _(sp):
                sp.dma_start(X[:, :, :], k.x.rearrange("(t p) f -> p t f", p=P)).then_inc(x_loaded, 16)
                sp.dma_start(w_rows[:, :, :],
                             k.L0_gnn_W.rearrange("h o i -> (h o) i").rearrange("(q r) i -> r q i", r=128)).then_inc(w_loaded, 16)
                for j in range(2):
                    sp.dma_start(att_b[:, j, :, :],
                                 k.L0_gnn_att[:, j * DH:(j + 1) * DH].unsqueeze(0).to_broadcast([P, HEADS, DH])).then_inc(att_loaded, 16)
                with sp.Fori(0, U) as i:
                    sp.wait_ge(zs_ready, i + 1)
                    for u in range(U):
                        sp.dma_start(k.z_dram[:, bass.ds(i * U + u, 1), :, :].rearrange("h a p c -> p (a h) c"),
                                     z[:, u, :, :]).then_inc(zs_free, 16)
                sp.wait_ge(zs_free, 16 * (T + U))
                sp.wait_ge(esT_done, 1)
                for j, rows in enumerate((k.es_dram, k.ed_dram)):
                    sp.dma_start(rows.rearrange("t h p -> (t h) p"), esT[:, j, :]).then_inc(es_stored, 16)
                sp.wait_ge(es_stored, 32)

            @block.vector
            def _(dve):
                v.memset(eps[:, :], EPS)
                v.memset(z[:, :, :, :], 1.0)
                dve.sem_inc(z_free, 3)
                dve.wait_ge(x_loaded, 16)
                layernorm_stats(nc, dve, v, X, st, mv, MV)
                v.nop().then_inc(stats_done, 1)
                dve.wait_ge(std_done, 1)
                v.reciprocal(rstd[:, :], std[:, :])
                v.drain()
                dve.wait_ge(att_loaded, 32)

                def logits(i):
                    for b, tiles in enumerate(BANKS):
                        dve.wait_ge(z_ready, 3 * i + b + 1)
                        if b == 0:
                            dve.wait_ge(zs_free, 16 * U * (i + 1))
                        for s, u in enumerate(tiles):
                            v.tensor_copy(z[:, u, :, 0:DH],
                                          ps_z[0:P, b, s * F:(s + 1) * F].rearrange("p (h o) -> p h o", h=HEADS))
                        v.drain().then_inc(z_free, 1)
                    v.nop().then_inc(zs_ready, 1)
                    for u in range(U):
                        for j in range(2):
                            v.tensor_tensor(out=prod[:, u, j, :, :], in0=z[:, u, :, 0:DH], in1=att_b[:, j, :, :], op=ALU.mult)
                    v.drain()
                    v.tensor_reduce(out=ered[:, :, :, :].rearrange("p u j h -> p (u j h)"),
                                    in_=prod[:, :, :, :, :].rearrange("p u j h o -> p (u j h) o"), axis=AXX, op=ALU.add)
                    v.drain()
                    v.tensor_copy(k.es[:, bass.ds(i * U, U), :], ered[:, :, 0, :])
                    v.tensor_copy(k.ed[:, bass.ds(i * U, U), :], ered[:, :, 1, :])
                    v.drain()

                normalize_batch(v, X, H, MV, rstd, 0, h_ready, t_ready, dve, True)
                with dve.Fori(1, U) as i:
                    normalize_batch(v, X, H, MV, rstd, i, h_ready, t_ready, dve, False)
                    logits(i - 1)
                logits(U - 1)
                v.nop().then_inc(es_done, 1)
                v.tensor_reduce(out=ends[:, 0, :], in_=k.es[:, :, :].rearrange("p t h -> p h t"), axis=AXX, op=ALU.max)
                v.tensor_reduce(out=ends[:, 1, :], in_=k.es[:, :, :].rearrange("p t h -> p h t"), axis=AXX, op=ALU.min)
                v.drain()
                v.tensor_scalar(ends[:, 1, :], ends[:, 1, :], -1.0, None, ALU.mult)
                v.drain().then_inc(ends_done, 1)
                dve.wait_ge(ends_psum, 1)
                v.tensor_reduce(out=ends8[:, :], in_=ps_w[0:2 * HEADS, 0, 0:P], axis=AXX, op=ALU.max)
                v.drain()
                v.tensor_scalar(diag8[:, :], k.ident[0:2 * HEADS, 0:2 * HEADS], ends8[:, 0:1], None, ALU.mult)
                v.drain().then_inc(diag_done, 1)
                dve.wait_ge(limits_psum, 1)
                v.tensor_copy(limits[:, :, :].rearrange("p j h -> p (j h)"), ps_w[0:P, 0, 0:2 * HEADS])
                v.drain()
                v.tensor_copy(k.top[:, :], limits[:, 0, :])
                v.tensor_tensor(out=wide[:, :], in0=limits[:, 0, :], in1=limits[:, 1, :], op=ALU.add)
                v.drain()
                v.tensor_reduce(out=wide1[:, :], in_=wide[:, :], axis=AXX, op=ALU.max)
                v.drain()
                v.tensor_scalar(wide1[:, :], wide1[:, :], WIDE, 2.0, ALU.is_gt, ALU.mult)
                v.drain()
                v.tensor_tensor(out=k.rounds[0:1, :], in0=k.rounds[0:1, :], in1=wide1[0:1, :], op=ALU.max)
                v.drain()

            @block.scalar
            def _(act):
                act.sem_inc(zs_free, 16 * U)
                act.wait_ge(wt_psum, 1)
                a.activation(wT[:, :, :], ps_w[:, :, :], ACT.Copy)
                a.drain().then_inc(wt_ready, 1)
                act.wait_ge(stats_done, 1)
                a.activation(std[:, :], MV[:, :, 1], ACT.Sqrt, bias=eps[:, 0:1])
                a.drain().then_inc(std_done, 1)
                copy_transposed(act, a, ps_t, HT, t_ready, z_ready, ht_ready)
                act.wait_ge(esT_psum, 1)
                a.activation(esT[:, :, :].rearrange("r j p -> r (j p)"), ps_t[0:HEADS * T, 0, 0:2 * P], ACT.Copy)
                a.drain().then_inc(esT_done, 1)

            @block.tensor
            def _(pe):
                pe.wait_ge(w_loaded, 16)
                for q in range(KF):
                    for r in range(KF):
                        t_.transpose(ps_w[:, q, r * 128:(r + 1) * 128], w_rows[:, r, q * 128:(q + 1) * 128], k.ident[:, :])
                t_.drain().then_inc(wt_psum, 1)
                pe.wait_ge(wt_ready, 1)

                def products(i):
                    for b, tiles in enumerate(BANKS):
                        pe.wait_ge(ht_ready, 3 * i + b + 1)
                        pe.wait_ge(z_free, 3 * i + b + 1)
                        for s, u in enumerate(tiles):
                            for q in range(KF):
                                last = t_.matmul(ps_z[0:P, b, s * F:(s + 1) * F], HT[:, q, u * P:(u + 1) * P], wT[:, q, :],
                                                 start=(q == 0), stop=(q == KF - 1))
                        last.then_inc(z_ready, 1)

                transpose_batch(pe, t_, k, H, ps_t, h_ready, ht_ready, t_ready, 0, True)
                with pe.Fori(1, U) as i:
                    transpose_batch(pe, t_, k, H, ps_t, h_ready, ht_ready, t_ready, i, False)
                    products(i - 1)
                products(U - 1)
                pe.wait_ge(es_done, 1)
                t_.transpose(ps_t[0:HEADS * T, 0, 0:P], k.es[:, :, :].rearrange("p t h -> p (t h)"), k.ident[0:P, 0:P])
                t_.transpose(ps_t[0:HEADS * T, 0, P:2 * P], k.ed[:, :, :].rearrange("p t h -> p (t h)"), k.ident[0:P, 0:P]).then_inc(esT_psum, 1)
                pe.wait_ge(ends_done, 1)
                t_.transpose(ps_w[0:2 * HEADS, 0, 0:P], ends[:, :, :].rearrange("p j h -> p (j h)"), k.ident[0:P, 0:P])
                t_.drain().then_inc(ends_psum, 1)
                pe.wait_ge(diag_done, 1)
                t_.matmul(ps_w[0:P, 0, 0:2 * HEADS], k.ones[0:2 * HEADS, 0:P], diag8[:, :], start=True, stop=True)
                t_.drain().then_inc(limits_psum, 1)


def edge_windows_phase(k):
    nc = k.nc
    v, a, t_, g = nc.vector, nc.scalar, nc.tensor, nc.gpsimd
    NB = 2 * U
    with scope(nc) as (sb, pb, sem):
        src_i = sb("src_i", [P, ROW], I32)
        dst_i = sb("dst_i", [P, ROW], I32)
        nxt_i = sb("nxt_i", [P, ROW], I32)
        key = sb("key", [P, ROW], FP32)
        down = sb("down", [P, ROW], FP32)
        pad = sb("pad", [1, SROWS * SEG - E], FP32)
        thr_i = sb("thr_i", [P, NB], I32)
        thr = sb("thr", [P, NB], FP32)
        low_i = sb("low_i", [P, U], I32)
        low = sb("low", [P, U], FP32)
        off_i = sb("off_i", [P, U, NSEG], I32)
        off = sb("off", [P, U, NSEG], FP32)
        head = sb("head", [P, 1], FP32)
        nd = sb("nd", [P, 1], FP32)
        diag = sb("diag", [P, P], FP32)
        heads = sb("heads", [P, P + 1], FP32)
        junk = sb("junk", [P, ROW], FP32)
        below = sb("below", [P, NB], FP32)
        row_f = sb("row_f", [P, NB], FP32)
        row_i = sb("row_i", [P, NB], I32)
        rows = sb("rows", [P, NB, ROW], I32)
        within = sb("within", [P, NB], FP32)
        edge = sb("edge", [P, NB], FP32)
        is_sorted = sb("is_sorted", [P, 1], FP32)
        base_i = sb("base_i", [P, U], I32)
        base = sb("base", [P, U], FP32)
        seg_f = sb("seg_f", [P, U, NSEG], FP32)
        seg_i = sb("seg_i", [P, U, NSEG], I32)
        span = sb("span", [P, U], FP32)
        span1 = sb("span1", [P, 1], FP32)
        spanT = sb("spanT", [1, P], FP32)
        win = sb("win", [P, U, WIN], FP32)
        rel = sb("rel", [P, U, WIN], FP32)
        rq_i = sb("rq_i", [P, U, WIN], I32)
        rq = sb("rq", [P, U, WIN], FP32)
        lo = sb("lo", [P, U, WIN], FP32)
        ps_h = pb("ps_h", [128, 512], FP32)
        ps_q = pb("ps_q", [128, 3, 512], FP32)
        ps_l = pb("ps_l", [128, 3, 512], FP32)
        loaded, consts = sem("loaded"), sem("consts")
        heads_in, heads_psum, row_ready = sem("heads_in"), sem("heads_psum"), sem("row_ready")
        key_ready, key_stored = sem("key_ready"), sem("key_stored")
        rows_in, win_in = k.rows_in, k.win_in
        seg_ready, cut_ready, cut_psum, span_ready, span_psum = (
            sem("seg_ready"), sem("cut_ready"), sem("cut_psum"), sem("span_ready"), sem("span_psum"))
        with nc.Block() as block:
            @block.sync
            def _(sp):
                sp.dma_start(dst_i[:, :], k.dst.rearrange("(p c) -> p c", p=P)).then_inc(loaded, 16)
                sp.dma_start(src_i[:, :], k.src.rearrange("(p c) -> p c", p=P)).then_inc(loaded, 16)
                sp.dma_start(nxt_i[0:P - 1, :], k.dst[1:1 + (P - 1) * ROW].rearrange("(p c) -> p c", c=ROW)).then_inc(loaded, 16)
                sp.dma_start(nxt_i[P - 1:P, 0:ROW - 1], k.dst[E - ROW + 1:E].rearrange("(p c) -> p c", p=1)).then_inc(loaded, 16)
                sp.dma_start(nxt_i[P - 1:P, ROW - 1:ROW], k.dst[E - 1:E].rearrange("(p c) -> p c", p=1)).then_inc(loaded, 16)
                sp.wait_ge(key_ready, 1)
                sp.wait_ge(consts, 1)
                flat = k.key_dram.rearrange("r c -> (r c)")
                sp.dma_start(flat[0:E].rearrange("(p c) -> p c", p=P), key[:, :]).then_inc(key_stored, 16)
                sp.dma_start(flat[E:SROWS * SEG].rearrange("(p c) -> p c", p=1), pad[:, :]).then_inc(key_stored, 16)
                sp.wait_ge(key_stored, 32)

            @block.gpsimd
            def _(pool):
                g.iota(thr_i[:, 0:U], pattern=[[G * P, U]], base=0, channel_multiplier=G)
                g.iota(thr_i[:, U:NB], pattern=[[G * P, U]], base=G, channel_multiplier=G)
                g.iota(low_i[:, :], pattern=[[P, U]], base=0, channel_multiplier=1)
                g.iota(off_i[:, :, :], pattern=[[0, U], [1, NSEG]], base=0, channel_multiplier=0)
                g.memset(pad[:, :], PAD_KEY)
                g.drain()
                g.tensor_copy(thr[:, :], thr_i[:, :])
                g.tensor_copy(low[:, :], low_i[:, :])
                g.tensor_copy(off[:, :, :], off_i[:, :, :])
                g.drain().then_inc(consts, 1)
                pool.wait_ge(row_ready, 1)
                for j in range(NB):
                    g.indirect_dma_start(out=rows[:, j, :], out_offset=None, in_=k.dst.rearrange("(p c) -> p c", p=P),
                                         in_offset=bass.IndirectOffsetOnAxis(ap=row_i[:, j:j + 1], axis=0)).then_inc(rows_in, 16)
                pool.wait_ge(seg_ready, 1)
                pool.wait_ge(key_stored, 32)
                for j in range(U):
                    for s in range(NSEG):
                        g.indirect_dma_start(out=win[:, j, s * SEG:(s + 1) * SEG], out_offset=None, in_=k.key_dram,
                                             in_offset=bass.IndirectOffsetOnAxis(ap=seg_i[:, j, s:s + 1], axis=0)).then_inc(win_in, 16)

            @block.vector
            def _(dve):
                dve.wait_ge(loaded, 80)
                v.tensor_copy(head[:, :], dst_i[:, 0:1])
                v.scalar_tensor_tensor(out=key[:, :], in0=dst_i[:, :], scalar=float(N), in1=src_i[:, :], op0=ALU.mult, op1=ALU.add)
                v.tensor_tensor(out=down[:, :], in0=nxt_i[:, :], in1=dst_i[:, :], op=ALU.is_lt)
                v.drain()
                v.tensor_reduce(out=nd[:, :], in_=down[:, :], axis=AXX, op=ALU.add)
                v.tensor_scalar(diag[:, :], k.ident[0:P, 0:P], head[:, 0:1], None, ALU.mult)
                v.drain().then_inc(heads_in, 1)
                v.nop().then_inc(key_ready, 1)
                dve.wait_ge(heads_psum, 1)
                v.tensor_copy(heads[:, :], ps_h[0:P, 0:P + 1])
                v.drain()
                v.tensor_scalar(is_sorted[:, :], heads[:, P:P + 1], 0.0, None, ALU.is_equal)
                dve.wait_ge(consts, 1)
                for j in range(NB):
                    v.tensor_scalar(junk[:, 0:P], heads[:, 0:P], thr[:, j:j + 1], 0.0,
                                    ALU.is_lt, ALU.add, accum_out=below[:, j:j + 1])
                    v.drain()
                v.tensor_scalar(row_f[:, :], below[:, :], -1.0, 0.0, ALU.add, ALU.max)
                v.drain()
                v.tensor_copy(row_i[:, :], row_f[:, :])
                v.drain().then_inc(row_ready, 1)
                dve.wait_ge(rows_in, 16 * NB)
                for j in range(NB):
                    v.tensor_scalar(junk[:, :], rows[:, j, :], thr[:, j:j + 1], 0.0, ALU.is_lt, ALU.add,
                                    accum_out=within[:, j:j + 1])
                    v.drain()
                v.scalar_tensor_tensor(out=edge[:, :], in0=row_f[:, :], scalar=float(ROW), in1=within[:, :], op0=ALU.mult, op1=ALU.add)
                v.drain()
                v.tensor_scalar(edge[:, 0:U], edge[:, 0:U], is_sorted[:, 0:1], None, ALU.mult)
                v.tensor_scalar(edge[:, U:NB], edge[:, U:NB], -float(E), is_sorted[:, 0:1], ALU.add, ALU.mult)
                v.drain()
                v.tensor_scalar(edge[:, U:NB], edge[:, U:NB], float(E), None, ALU.add)
                v.tensor_scalar(base_i[:, :], edge[:, 0:U], 1.0 / SEG, 0.5 / SEG - 0.5, ALU.mult, ALU.add)
                v.drain()
                v.tensor_copy(base[:, :], base_i[:, :])
                v.drain()
                v.tensor_copy(k.base[:, :], base[:, :])
                v.tensor_tensor(out=seg_f[:, :, :], in0=off[:, :, :], in1=base[:, :].unsqueeze(2).to_broadcast([P, U, NSEG]), op=ALU.add)
                v.scalar_tensor_tensor(out=span[:, :], in0=base[:, :], scalar=-float(SEG), in1=edge[:, U:NB], op0=ALU.mult, op1=ALU.add)
                v.drain()
                v.tensor_copy(seg_i[:, :, :], seg_f[:, :, :])
                v.tensor_reduce(out=span1[:, :], in_=span[:, :], axis=AXX, op=ALU.max)
                v.drain().then_inc(seg_ready, 1)
                dve.wait_ge(span_psum, 1)
                v.tensor_copy(spanT[:, :], ps_h[0:1, 0:P])
                v.drain()
                v.tensor_reduce(out=span1[0:1, :], in_=spanT[:, :], axis=AXX, op=ALU.max)
                v.drain()
                v.tensor_scalar(k.rounds[0:1, :], span1[0:1, :], 1.0 / WIN, 0.5 - 0.5 / WIN, ALU.mult, ALU.add)
                dve.wait_ge(win_in, 16 * U * NSEG)
                cut_keys(nc, v, low, win, rel, rq_i, rq, lo)
                v.nop().then_inc(cut_ready, 1)
                dve.wait_ge(cut_psum, 1)
                copy_cuts(v, k, ps_q, ps_l)

            @block.tensor
            def _(pe):
                pe.wait_ge(heads_in, 1)
                t_.matmul(ps_h[0:P, 0:P], k.ones[0:P, 0:P], diag[:, :], start=True, stop=True)
                t_.matmul(ps_h[0:P, P:P + 1], k.ones[0:P, 0:P], nd[:, :], start=True, stop=True)
                t_.drain().then_inc(heads_psum, 1)
                pe.wait_ge(seg_ready, 1)
                t_.transpose(ps_h[0:1, 0:P], span1[:, :], k.ident[0:P, 0:P])
                t_.drain().then_inc(span_psum, 1)
                pe.wait_ge(cut_ready, 1)
                transpose_cuts(t_, k, rq, lo, ps_q, ps_l)
                t_.drain().then_inc(cut_psum, 1)


def cut_keys(nc, v, low, win, rel, rq_i, rq, lo):
    for j in range(U):
        v.scalar_tensor_tensor(out=rel[:, j, :], in0=low[:, j:j + 1].to_broadcast([P, WIN]), scalar=-float(G * N),
                               in1=win[:, j, :], op0=ALU.mult, op1=ALU.add)
    v.drain()
    v.tensor_scalar(rq_i[:, :, :], rel[:, :, :], 1.0 / P, 0.5 / P - 0.5, ALU.mult, ALU.add)
    v.drain()
    v.tensor_copy(rq[:, :, :], rq_i[:, :, :])
    v.drain()
    v.scalar_tensor_tensor(out=lo[:, :, :], in0=rq[:, :, :], scalar=-float(P), in1=rel[:, :, :], op0=ALU.mult, op1=ALU.add)
    v.drain()
    v.tensor_scalar(rq[:, :, :], rq[:, :, :], -1.0, float(P), ALU.max, ALU.min)
    v.drain()


def transpose_cuts(t_, k, rq, lo, ps_q, ps_l):
    for j in range(U):
        for c in range(2):
            n = 2 * j + c
            for cut, ps in ((rq, ps_q), (lo, ps_l)):
                t_.transpose(ps[:, n // 4, (n % 4) * P:(n % 4 + 1) * P], cut[:, j, c * 128:(c + 1) * 128], k.ident[0:P, 0:P])


def copy_cuts(v, k, ps_q, ps_l):
    for cut, ps in ((k.rowG, ps_q), (k.colG, ps_l)):
        for j in range(U):
            for c in range(2):
                n = 2 * j + c
                v.tensor_copy(cut[:, j * T:(j + 1) * T, c * U:(c + 1) * U],
                              ps[:, n // 4, (n % 4) * P:(n % 4 + 1) * P].rearrange("p (b g) -> p b g", g=U))
    v.drain()


HB = [(0, 1, 2), (3, 4)]
PAIR = [0, 1, 2, 0, 1]
BACK = [2, 2, 5, 3, 3]
TQ = 4
TR_AFTER = [(0, 1), (2,), (3, 4), (5,), (6,)]
NTB = (T + TQ - 1) // TQ


def zparts(k):
    return k.arena[:, :].rearrange("p (t h e c d) -> p t h e c d", t=T, h=HEADS, e=2, c=3)


def count_phase(k):
    nc = k.nc
    v, a, t_ = nc.vector, nc.scalar, nc.tensor
    with scope(nc) as (sb, pb, sem):
        M = 2 * U
        iota_rep = sb("iota_rep", [128, P, M], BF16)
        row_hot = sb("row_hot", [128, U, P, M], BF16)
        col_hot = sb("col_hot", [128, U, P, M], BF16)
        blk = sb("blk", [P, 2, T, QB], BF16)
        tr = sb("tr", [P, 2, N], BF16)
        u_dst = sb("u_dst", [P, T, HEADS], FP32)
        m_dst = sb("m_dst", [P, T, HEADS], FP32)
        src_exp = sb("src_exp", [P, T, HEADS, 2], FP32)
        z = sb("z_tile_in", [P, HEADS, D1], FP32)
        ex = sb("src_exp_now", [P, HEADS, 2], FP32)
        full = sb("z_full", [P, HEADS, 2, D1], FP32)
        rest = sb("z_rest", [P, HEADS, 2, D1], FP32)
        ps = pb("ps_hist", [128, 3, 2, 512], FP32)
        ps_tr = pb("ps_tr", [128, 2, 512], FP32)
        hot_done, hist_done, blk_done = sem("hot_done"), sem("hist_done"), sem("blk_done")
        tr_psum, tr_done = sem("tr_psum"), sem("tr_done")
        blk_stored, tr_stored = sem("blk_stored"), sem("tr_stored")
        terms_done, exps_done, z_in, z_read = sem("terms_done"), sem("exps_done"), sem("z_in"), sem("z_read")
        with nc.Block() as block:
            @block.vector
            def _(dve):
                v.tensor_copy(iota_rep[:, :, :], k.iota_row[:, :].unsqueeze(2).to_broadcast([128, P, M]))
                v.drain()

                top_b = k.top[:, :].unsqueeze(1).to_broadcast([P, T, HEADS])
                v.tensor_tensor(out=src_exp[:, :, :, 0], in0=k.es[:, :, :], in1=top_b, op=ALU.subtract)
                v.tensor_tensor(out=u_dst[:, :, :], in0=k.ed[:, :, :], in1=top_b, op=ALU.add)
                v.tensor_scalar(k.es_mask[:, :, :], k.es[:, :, :], MASK_SCALE, None, ALU.mult)
                v.drain()
                v.tensor_scalar(src_exp[:, :, :, 1], src_exp[:, :, :, 0], 0.01, None, ALU.mult)
                v.tensor_scalar(k.dst_exp[:, :, :, 1], u_dst[:, :, :], 0.01, None, ALU.mult)
                v.drain()
                v.tensor_tensor(out=m_dst[:, :, :], in0=u_dst[:, :, :], in1=k.dst_exp[:, :, :, 1], op=ALU.max)
                v.drain()
                v.tensor_tensor(out=k.dst_exp[:, :, :, 0], in0=u_dst[:, :, :], in1=m_dst[:, :, :], op=ALU.subtract)
                v.tensor_tensor(out=k.dst_exp[:, :, :, 1], in0=k.dst_exp[:, :, :, 1], in1=m_dst[:, :, :], op=ALU.subtract)
                v.drain().then_inc(terms_done, 1)

                def hots(i, first):
                    for u in range(U):
                        if not first:
                            dve.wait_ge(hist_done, U * (i - 1) + u + 1)
                        for cut, hot in ((k.rowG, row_hot), (k.colG, col_hot)):
                            v.tensor_tensor(out=hot[:, u, :, :], in0=iota_rep[:, :, :],
                                            in1=cut[:, bass.ds(i * U + u, 1), :].to_broadcast([128, P, M]),
                                            op=ALU.is_equal).then_inc(hot_done, 1)

                hots(0, True)
                with dve.Fori(1, T) as i:
                    hots(i, False)

            @block.gpsimd
            def _(pool):
                g = nc.gpsimd
                pool.wait_ge(exps_done, 1)
                with pool.Fori(0, T) as t:
                    g.tensor_copy(ex[:, :, :], src_exp[:, bass.ds(t, 1), :, :].rearrange("p a h e -> p (a h) e"))
                    g.drain()
                    pool.wait_ge(z_in, 16 * (t + 1))
                    for e in range(2):
                        g.tensor_tensor(out=full[:, :, e, :], in0=z[:, :, :], in1=ex[:, :, e:e + 1].to_broadcast([P, HEADS, D1]), op=ALU.mult)
                    g.drain().then_inc(z_read, 1)
                    part = [zparts(k)[:, bass.ds(t, 1), :, :, c, :].rearrange("p a h e c -> p (a h) e c") for c in range(3)]
                    g.tensor_copy(part[0], full[:, :, :, :])
                    g.drain()
                    g.tensor_tensor(out=rest[:, :, :, :], in0=full[:, :, :, :], in1=part[0], op=ALU.subtract)
                    g.drain()
                    g.tensor_copy(part[1], rest[:, :, :, :])
                    g.drain()
                    g.tensor_tensor(out=part[2], in0=rest[:, :, :, :], in1=part[1], op=ALU.subtract)
                    g.drain()

            @block.scalar
            def _(act):
                act.sem_inc(tr_done, 2)
                act.sem_inc(blk_done, U)
                act.wait_ge(terms_done, 1)
                a.activation(src_exp[:, :, :, :], src_exp[:, :, :, :], ACT.Exp)
                a.activation(k.dst_exp[:, :, :, :], k.dst_exp[:, :, :, :], ACT.Exp)
                a.drain().then_inc(exps_done, 1)

                def hist_out(i, u):
                    act.wait_ge(hist_done, U * i + u + 1)
                    for b, groups in enumerate(HB):
                        n = len(groups) * G
                        last = a.activation(
                            blk[:, bass.ds((i // U) % 2, 1), :, bass.ds((i % U) * P + u * G * U + groups[0] * G, n)].rearrange("p a t d -> p (a t) d"),
                            ps[0:P, PAIR[u], b, 0:n * T].rearrange("p (d t) -> p t d", t=T), ACT.Copy)
                    last.then_inc(blk_done, 1)

                def tr_out(i, banks):
                    for r in banks:
                        n = min(TQ, T - r * TQ)
                        act.wait_ge(tr_psum, NTB * i + r + 1)
                        a.activation(tr[:, bass.ds(i % 2, 1), r * TQ * P:(r * TQ + n) * P].rearrange("p a c -> p (a c)"),
                                     ps_tr[0:P, r % 2, 0:n * P], ACT.Copy).then_inc(tr_done, 1)

                act.wait_ge(blk_stored, 16)
                for u in range(U):
                    hist_out(0, u)
                with act.Fori(1, T) as i:
                    act.wait_ge(blk_stored, 16 * (i // U + 1))
                    act.wait_ge(tr_stored, 16 * i)
                    for u in range(U):
                        hist_out(i, u)
                        tr_out(i - 1, TR_AFTER[u])
                act.wait_ge(tr_stored, 16 * T)
                tr_out(T - 1, range(NTB))

            @block.tensor
            def _(pe):
                def histogram(i, u):
                    pe.wait_ge(hot_done, 2 * (U * i + u + 1))
                    pe.wait_ge(blk_done, U * i + u + 1 - BACK[u] + U)
                    for b, groups in enumerate(HB):
                        for s, gg in enumerate(groups):
                            for c in range(2):
                                last = t_.matmul(ps[0:P, PAIR[u], b, s * P:(s + 1) * P],
                                                 col_hot[:, u, :, c * U + gg], row_hot[:, u, :, c * U + gg],
                                                 start=(c == 0), stop=(c == 1))
                    last.then_inc(hist_done, 1)

                def transposes(i, banks):
                    for r in banks:
                        pe.wait_ge(tr_done, NTB * i + r + 1 + (1 if r == 0 else 0))
                        for s in range(min(TQ, T - r * TQ)):
                            last = t_.matmul(ps_tr[0:P, r % 2, s * P:(s + 1) * P],
                                             blk[:, bass.ds((i // U) % 2, 1), r * TQ + s, bass.ds((i % U) * P, P)].rearrange("p a d -> p (a d)"),
                                             k.ident_bf[0:P, 0:P], start=True, stop=True)
                        last.then_inc(tr_psum, 1)

                for u in range(U):
                    histogram(0, u)
                with pe.Fori(1, T) as i:
                    for u in range(U):
                        histogram(i, u)
                        if u == 0:
                            pe.wait_ge(blk_done, U * i + U)
                        transposes(i - 1, TR_AFTER[u])
                pe.wait_ge(blk_done, U * T + U)
                transposes(T - 1, range(NTB))

            @block.sync
            def _(sp):
                sp.sem_inc(blk_stored, 32)
                sp.sem_inc(tr_stored, 32)
                sp.sem_inc(z_read, 1)
                with sp.Fori(0, U) as j:
                    with sp.Fori(0, U) as w:
                        i = j * U + w
                        sp.wait_ge(z_read, i + 1)
                        sp.dma_start(z[:, :, :],
                                     k.z_dram[:, bass.ds(i, 1), :, :].rearrange("h a p c -> p (a h) c")).then_inc(z_in, 16)
                        sp.wait_ge(tr_done, NTB * (i + 1) + 2)
                        sp.wait_ge(tr_stored, 16 * i + 32)
                        sp.dma_start(k.countsT.rearrange("(t p) s -> t p s", p=P)[bass.ds(i, 1), :, :].rearrange("a p s -> (a p) s"),
                                     tr[:, bass.ds(i % 2, 1), :].rearrange("p a s -> p (a s)")).then_inc(tr_stored, 16)
                    sp.wait_ge(blk_stored, 16 * j + 32)
                    sp.dma_start(k.counts[:, bass.ds(j * QB, QB)].rearrange("(t p) d -> p t d", p=P),
                                 blk[:, bass.ds(j % 2, 1), :, :].rearrange("p a t d -> p (a t) d")).then_inc(blk_stored, 16)
                sp.wait_ge(blk_stored, 16 * U + 32)
                sp.wait_ge(tr_stored, 16 * T + 32)


def more_windows_phase(k, r):
    nc = k.nc
    v, t_, g = nc.vector, nc.tensor, nc.gpsimd
    with scope(nc) as (sb, pb, sem):
        low_i = sb("w_low_i", [P, U], I32)
        low = sb("w_low", [P, U], FP32)
        off_i = sb("w_off_i", [P, U, NSEG], I32)
        off = sb("w_off", [P, U, NSEG], FP32)
        seg_f = sb("w_seg_f", [P, U, NSEG], FP32)
        seg_i = sb("w_seg_i", [P, U, NSEG], I32)
        win = sb("w_win", [P, U, WIN], FP32)
        rel = sb("w_rel", [P, U, WIN], FP32)
        rq_i = sb("w_rq_i", [P, U, WIN], I32)
        rq = sb("w_rq", [P, U, WIN], FP32)
        lo = sb("w_lo", [P, U, WIN], FP32)
        ps_q = pb("w_ps_q", [128, 3, 512], FP32)
        ps_l = pb("w_ps_l", [128, 3, 512], FP32)
        consts, seg_ready, cut_ready, cut_psum = sem("w_consts"), sem("w_seg"), sem("w_cut"), sem("w_cut_psum")
        with nc.Block() as block:
            @block.gpsimd
            def _(pool):
                g.iota(low_i[:, :], pattern=[[P, U]], base=0, channel_multiplier=1)
                g.iota(off_i[:, :, :], pattern=[[0, U], [1, NSEG]], base=0, channel_multiplier=0)
                g.drain()
                g.tensor_copy(low[:, :], low_i[:, :])
                g.tensor_copy(off[:, :, :], off_i[:, :, :])
                g.drain().then_inc(consts, 1)
                pool.wait_ge(seg_ready, 1)
                for j in range(U):
                    for s in range(NSEG):
                        g.indirect_dma_start(out=win[:, j, s * SEG:(s + 1) * SEG], out_offset=None, in_=k.key_dram,
                                             in_offset=bass.IndirectOffsetOnAxis(ap=seg_i[:, j, s:s + 1], axis=0)).then_inc(k.more_in, 16)

            @block.vector
            def _(dve):
                dve.wait_ge(consts, 1)
                v.tensor_scalar(k.base[:, :], k.base[:, :], float(NSEG), None, ALU.add)
                v.drain()
                v.tensor_tensor(out=seg_f[:, :, :], in0=off[:, :, :], in1=k.base[:, :].unsqueeze(2).to_broadcast([P, U, NSEG]), op=ALU.add)
                v.drain()
                v.tensor_scalar(seg_i[:, :, :], seg_f[:, :, :], float(SROWS - 1), None, ALU.min)
                v.drain().then_inc(seg_ready, 1)
                dve.wait_ge(k.more_in, 16 * U * NSEG * r)
                cut_keys(nc, v, low, win, rel, rq_i, rq, lo)
                v.nop().then_inc(cut_ready, 1)
                dve.wait_ge(cut_psum, 1)
                copy_cuts(v, k, ps_q, ps_l)

            @block.tensor
            def _(pe):
                pe.wait_ge(cut_ready, 1)
                transpose_cuts(t_, k, rq, lo, ps_q, ps_l)
                t_.drain().then_inc(cut_psum, 1)


def clear_low_phase(k):
    nc = k.nc
    with scope(nc) as (sb, pb, sem):
        zero = sb("zero_rows", [P, N], BF16)
        zero_set, cleared = sem("zero_set"), sem("cleared")
        with nc.Block() as block:
            @block.vector
            def _(dve):
                nc.vector.memset(zero[:, :], 0.0)
                nc.vector.drain().then_inc(zero_set, 1)

            @block.sync
            def _(sp):
                sp.wait_ge(zero_set, 1)
                with sp.Fori(0, T) as t:
                    sp.dma_start(k.counts_low[bass.ds(t * P, P), :], zero[:, :]).then_inc(cleared, 16)
                sp.wait_ge(cleared, 16 * T)


def more_counts_phase(k):
    nc = k.nc
    v, t_ = nc.vector, nc.tensor
    M = 2 * U
    with scope(nc) as (sb, pb, sem):
        iota_rep = sb("m_iota", [128, P, M], BF16)
        row_hot = sb("m_row_hot", [128, P, M], BF16)
        col_hot = sb("m_col_hot", [128, P, M], BF16)
        high = sb("m_high", [P, T, P], BF16)
        low = sb("m_low", [P, T, P], BF16)
        acc = sb("m_acc", [P, T, P], FP32)
        ps = pb("m_ps", [128, 2, 512], FP32)
        in_done, hot_done, hist_done, sum_done, stored = sem("m_in"), sem("m_hot"), sem("m_hist"), sem("m_sum"), sem("m_stored")

        def tile(counts, i):
            return counts.rearrange("(t p) d -> p t d", p=P)[:, :, bass.ds(i * P, P)]

        with nc.Block() as block:
            @block.sync
            def _(sp):
                sp.sem_inc(stored, 32)
                with sp.Fori(0, T) as i:
                    sp.wait_ge(stored, 32 * (i + 1))
                    sp.dma_start(high[:, :, :], tile(k.counts, i)).then_inc(in_done, 16)
                    sp.dma_start(low[:, :, :], tile(k.counts_low, i)).then_inc(in_done, 16)
                    sp.wait_ge(sum_done, i + 1)
                    sp.dma_start(tile(k.counts, i), high[:, :, :]).then_inc(stored, 16)
                    sp.dma_start(tile(k.counts_low, i), low[:, :, :]).then_inc(stored, 16)
                sp.wait_ge(stored, 32 * (T + 1))

            @block.vector
            def _(dve):
                v.tensor_copy(iota_rep[:, :, :], k.iota_row[:, :].unsqueeze(2).to_broadcast([128, P, M]))
                v.drain()
                with dve.Fori(0, T) as i:
                    for u in range(U):
                        for cut, hot in ((k.rowG, row_hot), (k.colG, col_hot)):
                            v.tensor_tensor(out=hot[:, :, :], in0=iota_rep[:, :, :],
                                            in1=cut[:, bass.ds(i * U + u, 1), :].to_broadcast([128, P, M]), op=ALU.is_equal)
                        v.drain().then_inc(hot_done, 1)
                        dve.wait_ge(hist_done, U * i + u + 1)
                        for b, groups in enumerate(HB):
                            n = len(groups) * G
                            d0 = u * G * U + groups[0] * G
                            v.tensor_copy(acc[:, :, d0:d0 + n], ps[0:P, b, 0:n * T].rearrange("p (d t) -> p t d", t=T))
                        v.drain()
                    dve.wait_ge(in_done, 32 * (i + 1))
                    for part in (high, low):
                        v.tensor_tensor(out=acc[:, :, :], in0=acc[:, :, :], in1=part[:, :, :], op=ALU.add)
                        v.drain()
                    v.tensor_copy(high[:, :, :], acc[:, :, :])
                    v.drain()
                    v.tensor_tensor(out=low[:, :, :], in0=acc[:, :, :], in1=high[:, :, :], op=ALU.subtract)
                    v.drain().then_inc(sum_done, 1)

            @block.tensor
            def _(pe):
                with pe.Fori(0, T) as i:
                    for u in range(U):
                        pe.wait_ge(hot_done, U * i + u + 1)
                        for b, groups in enumerate(HB):
                            for s, gg in enumerate(groups):
                                for c in range(2):
                                    last = t_.matmul(ps[0:P, b, s * P:(s + 1) * P], col_hot[:, :, c * U + gg], row_hot[:, :, c * U + gg],
                                                     start=(c == 0), stop=(c == 1))
                        last.then_inc(hist_done, 1)


def transpose_counts_phase(k, name, counts, countsT, with_max):
    nc = k.nc
    v, t_ = nc.vector, nc.tensor
    with scope(nc) as (sb, pb, sem):
        tile = sb(name + "tile", [P, T, P], BF16)
        tr = sb(name + "tr", [P, N], BF16)
        absent = sb(name + "absent", [P, N], BF16)
        junk = sb(name + "junk", [P, N], BF16)
        mx1 = sb(name + "mx1", [P, HEADS], FP32)
        ps = pb(name + "ps", [128, NTB, 512], FP32)
        es_row = k.arena[0:P, 0:2 * HEADS * N].bitcast(FP32).rearrange("p (h n) -> p h n", h=HEADS)
        tile_in, tr_psum, tr_done, stored = sem(name + "tile_in"), sem(name + "psum"), sem(name + "done"), sem(name + "stored")
        es_loaded = sem(name + "es_loaded")
        with nc.Block() as block:
            @block.sync
            def _(sp):
                sp.sem_inc(stored, 16)
                if with_max:
                    for h in range(HEADS):
                        sp.dma_start(es_row[:, h, :].rearrange("q (t p) -> q t p", p=P),
                                     k.es_dram[:, h, :].unsqueeze(0).to_broadcast([P, T, P])).then_inc(es_loaded, 16)
                with sp.Fori(0, T) as i:
                    sp.wait_ge(stored, 16 * (i + 1))
                    sp.dma_start(tile[:, :, :], counts.rearrange("(t p) d -> p t d", p=P)[:, :, bass.ds(i * P, P)]).then_inc(tile_in, 16)
                    sp.wait_ge(tr_done, i + 1)
                    sp.dma_start(countsT[bass.ds(i * P, P), :], tr[:, :]).then_inc(stored, 16)
                sp.wait_ge(stored, 16 * (T + 1))

            @block.tensor
            def _(pe):
                with pe.Fori(0, T) as i:
                    pe.wait_ge(tile_in, 16 * (i + 1))
                    for t in range(T):
                        last = t_.matmul(ps[0:P, t // TQ, (t % TQ) * P:(t % TQ + 1) * P], tile[:, t, :], k.ident_bf[0:P, 0:P],
                                         start=True, stop=True)
                    last.then_inc(tr_psum, 1)

            @block.vector
            def _(dve):
                if with_max:
                    dve.wait_ge(es_loaded, 16 * HEADS)
                with dve.Fori(0, T) as i:
                    dve.wait_ge(tr_psum, i + 1)
                    for b in range(NTB):
                        n = min(TQ, T - b * TQ)
                        v.tensor_copy(tr[:, b * TQ * P:(b * TQ + n) * P], ps[0:P, b, 0:n * P])
                    v.drain()
                    if with_max:
                        v.tensor_scalar(absent[:, :], tr[:, :], 0.0, -BIG, ALU.is_equal, ALU.mult)
                        v.drain()
                        for h in range(HEADS):
                            v.tensor_tensor_reduce(out=junk[:, :], in0=es_row[:, h, :], in1=absent[:, :], scale=1.0,
                                                   scalar=-3e38, op0=ALU.add, op1=ALU.max, accum_out=mx1[:, h:h + 1])
                            v.drain()
                        v.tensor_copy(k.mx[:, bass.ds(i, 1), :].rearrange("p a h -> p (a h)"), mx1[:, :])
                        v.drain()
                    v.nop().then_inc(tr_done, 1)


def last_use(u, ring, period):
    if u >= ring:
        return ring
    return period + u - max(x for x in range(period) if x % ring == u % ring)


def gat_attend_phase(k, name, planes):
    nc = k.nc
    v, a, t_ = nc.vector, nc.scalar, nc.tensor
    TT = T * len(planes)
    RC, R1, R2 = 2, 3, 2
    NC = (N + 511) // 512
    NR = (T + 6) // 7
    with scope(nc) as (sb, pb, sem):
        ec = sb(name + "edge_max", [P, T, HEADS], FP32)
        has = sb(name + "has_edge", [P, T, HEADS], FP32)
        rows = sb(name + "row_terms", [P, 2, HEADS, T], FP32)
        rowsT = sb(name + "row_termsT", [HEADS * T, 2, P], FP32)
        es_now = sb(name + "es_now", [P, 2, T], FP32)
        row_b = k.arena[0:P, 0:8 * N].bitcast(FP32).rearrange("p (r j n) -> p r j n", r=2, j=2)
        cnt = k.arena[0:P, 10 * N:(10 + RC) * N].rearrange("p (r n) -> p r n", r=RC)
        zt = sb(name + "z_tile", [P, RC, D1], FP32)
        e1 = sb(name + "exp_full", [P, R1, N], FP32)
        e2 = sb(name + "exp_slope", [P, R2, N], FP32)
        sums = k.arena[0:D1, 8 * N:10 * N].bitcast(FP32)
        ps = pb(name + "ps_sums", [128, NC, 512], FP32)
        ps_t = pb(name + "ps_back", [128, 512], FP32)
        rows_ready, rows_psum, rowsT_ready, rows_stored = sem(name + "rows_ready"), sem(name + "rows_psum"), sem(name + "rowsT_ready"), sem(name + "rows_stored")
        row_in = sem(name + "row_in")
        cz_in = [sem(name + f"cz_in{s}") for s in range(RC)]
        exp_done, e2_free, w_done, pv_done = sem(name + "exp_done"), sem(name + "e2_free"), sem(name + "w_done"), sem(name + "pv_done")
        head_out, back_psum, back_out = sem(name + "head_out"), sem(name + "back_psum"), sem(name + "back_out")
        act_passed = sem(name + "act_passed")
        uses = [sum(1 for x in range(TT) if x % RC == s) for s in range(RC)]

        with nc.Block() as block:
            @block.sync
            def _(sp):
                sp.wait_ge(rowsT_ready, 1)
                for j in range(2):
                    sp.dma_start(k.rows_dram[j].rearrange("h t p -> (h t) p"), rowsT[:, j, :]).then_inc(rows_stored, 16)
                sp.wait_ge(rows_stored, 32)
                with sp.Fori(0, HEADS) as h:
                    sp.wait_ge(exp_done, 2 * TT * h + 2)
                    for j in range(2):
                        sp.dma_start(row_b[:, bass.ds(h % 2, 1), j, :].rearrange("p a n -> p (a n)"),
                                     k.rows_dram[j, bass.ds(h, 1)].rearrange("a t p -> a (t p)").to_broadcast([P, N])).then_inc(row_in, 16)
                    for t in range(TT):
                        sp.wait_ge(pv_done, TT * h + t + 1 - last_use(t, RC, TT) + TT)
                        sp.dma_start(cnt[:, t % RC, :], planes[t // T][(t % T) * P:(t % T + 1) * P, :]).then_inc(cz_in[t % RC], 16)
                        sp.dma_start(zt[:, t % RC, :], k.z_dram[bass.ds(h, 1), t % T].rearrange("a p c -> (a p) c")).then_inc(cz_in[t % RC], 16)

            @block.vector
            def _(dve):
                v.tensor_scalar(has[:, :, :], k.mx[:, :, :], -0.5 * BIG, None, ALU.is_gt)
                v.drain()
                v.tensor_tensor(out=ec[:, :, :], in0=k.mx[:, :, :], in1=has[:, :, :], op=ALU.mult)
                v.drain()
                v.tensor_tensor(out=ec[:, :, :], in0=ec[:, :, :], in1=k.ed[:, :, :], op=ALU.add)
                v.drain()
                v.tensor_tensor(out=ec[:, :, :], in0=ec[:, :, :], in1=has[:, :, :], op=ALU.mult)
                v.drain()
                v.scalar_tensor_tensor(out=ec[:, :, :], in0=ec[:, :, :], scalar=0.01, in1=ec[:, :, :], op0=ALU.mult, op1=ALU.max)
                v.drain()
                v.tensor_tensor(out=rows[:, 0, :, :].rearrange("p h t -> p t h"), in0=k.ed[:, :, :], in1=ec[:, :, :], op=ALU.subtract)
                v.scalar_tensor_tensor(out=rows[:, 1, :, :].rearrange("p h t -> p t h"), in0=k.ed[:, :, :], scalar=0.01,
                                       in1=ec[:, :, :], op0=ALU.mult, op1=ALU.subtract)
                v.drain().then_inc(rows_ready, 1)

                def back(h, r):
                    n = min(7, T - 7 * r)
                    dve.wait_ge(back_psum, NR * h + r + 2)
                    v.tensor_copy(k.acc[:, bass.ds(h, 1), 7 * r:7 * r + n, :].rearrange("p a t c -> p (a t c)"),
                                  ps_t[0:P, 0:n * D1]).then_inc(back_out, 1)

                def head(h, first):
                    for t in range(TT):
                        dve.wait_ge(exp_done, 2 * (TT * h + t + 1) + 2 * TT + 2)
                        v.tensor_tensor(out=e1[:, t % R1, :], in0=e1[:, t % R1, :], in1=e2[:, t % R2, :], op=ALU.max)
                        v.drain().then_inc(e2_free, 1)
                        dve.wait_ge(cz_in[t % RC], 32 * (uses[t % RC] * h + t // RC + 1))
                        v.scalar_tensor_tensor(out=e1[:, t % R1, :], in0=e1[:, t % R1, :], scalar=1.0, in1=cnt[:, t % RC, :],
                                               op0=ALU.min, op1=ALU.mult).then_inc(w_done, 1)
                        if not first and t >= 3 and (t - 3) % 2 == 0 and (t - 3) // 2 < NR:
                            back(h - 1, (t - 3) // 2)

                head(0, True)
                with dve.Fori(1, HEADS) as h:
                    head(h, False)
                for r in range(NR):
                    back(HEADS - 1, r)

            @block.scalar
            def _(act):
                act.sem_inc(exp_done, 2 * TT + 2)
                act.sem_inc(e2_free, TT)
                act.sem_inc(pv_done, TT)
                act.sem_inc(head_out, NC)
                act.sem_inc(back_psum, 1)
                act.wait_ge(rows_psum, 1)
                a.activation(rowsT[:, :, :], ps[0:HEADS * T, 0:2, 0:P], ACT.Copy)
                a.drain().then_inc(rowsT_ready, 1)

                def head_sums(h):
                    for c in range(NC):
                        if c == 0:
                            act.wait_ge(pv_done, TT * (h + 1) + TT)
                            act.wait_ge(back_psum, NR * h + 1)
                        n = min(512, N - 512 * c)
                        a.activation(sums[:, 512 * c:512 * c + n], ps[0:D1, c, 0:n], ACT.Copy).then_inc(head_out, 1)

                def head(h, first):
                    if not first:
                        a.drain()
                    a.activation(es_now[:, 0, :], k.es[:, :, bass.ds(h, 1)].rearrange("p t a -> p (t a)"), ACT.Copy)
                    a.activation(es_now[:, 1, :], k.es[:, :, bass.ds(h, 1)].rearrange("p t a -> p (t a)"), ACT.Copy, scale=0.01)
                    a.drain()
                    act.wait_ge(row_in, 32 * (h + 1))
                    act.sem_inc(act_passed, 1)
                    for t in range(TT):
                        if t == 2 and not first:
                            head_sums(h - 1)
                        act.wait_ge(pv_done, TT * h + t + 1 - last_use(t, R1, TT) + TT)
                        act.sem_inc(act_passed, 1)
                        a.activation(e1[:, t % R1, :], row_b[:, bass.ds(h % 2, 1), 0, :].rearrange("p a n -> p (a n)"), ACT.Exp,
                                     bias=es_now[:, 0, t % T:t % T + 1]).then_inc(exp_done, 1)
                        act.wait_ge(e2_free, TT * h + t + 1 - last_use(t, R2, TT) + TT)
                        act.sem_inc(act_passed, 1)
                        a.activation(e2[:, t % R2, :], row_b[:, bass.ds(h % 2, 1), 1, :].rearrange("p a n -> p (a n)"), ACT.Exp,
                                     bias=es_now[:, 1, t % T:t % T + 1]).then_inc(exp_done, 1)

                head(0, True)
                with act.Fori(1, HEADS) as h:
                    head(h, False)
                head_sums(HEADS - 1)

            @block.tensor
            def _(pe):
                pe.wait_ge(rows_ready, 1)
                for j in range(2):
                    t_.transpose(ps[0:HEADS * T, j, 0:P], rows[:, j, :, :].rearrange("p h t -> p (h t)"), k.ident[0:P, 0:P])
                t_.drain().then_inc(rows_psum, 1)

                def back(h, r):
                    pe.wait_ge(head_out, NC * (h + 1) + NC)
                    if r > 0:
                        pe.wait_ge(back_out, NR * h + r)
                    for s in range(min(7, T - 7 * r)):
                        t = 7 * r + s
                        last = t_.transpose(ps_t[0:P, s * D1:(s + 1) * D1], sums[:, t * P:(t + 1) * P], k.ident[0:D1, 0:D1])
                    last.then_inc(back_psum, 1)

                def head(h, first):
                    for t in range(TT):
                        pe.wait_ge(w_done, TT * h + t + 1)
                        if first and t == 0:
                            pe.wait_ge(rowsT_ready, 1)
                        for c in range(NC):
                            n = min(512, N - 512 * c)
                            if t == 0:
                                pe.wait_ge(head_out, NC * h + c + 1)
                            last = t_.matmul(ps[0:D1, c, 0:n], zt[:, t % RC, :], e1[:, t % R1, 512 * c:512 * c + n],
                                             start=(t == 0), stop=(t == TT - 1))
                        last.then_inc(pv_done, 1)
                        if not first and t >= 2 and t % 2 == 0 and (t - 2) // 2 < NR:
                            back(h - 1, (t - 2) // 2)

                head(0, True)
                with pe.Fori(1, HEADS) as h:
                    head(h, False)
                for r in range(NR):
                    back(HEADS - 1, r)


def gat_finish_phase(k):
    nc = k.nc
    v = nc.vector
    with scope(nc) as (sb, pb, sem):
        den = sb("den", [P, HEADS, T], FP32)
        x_in = sem("x_in_again")
        with nc.Block() as block:
            @block.sync
            def _(sp):
                sp.dma_start(k.X[:, :, :], k.x.rearrange("(t p) f -> p t f", p=P)).then_inc(x_in, 16)

            @block.vector
            def _(dve):
                v.tensor_scalar(den[:, :, :], k.acc[:, :, :, DH], 1e-16, None, ALU.max)
                v.drain()
                v.reciprocal(den[:, :, :], den[:, :, :])
                v.drain()
                for h in range(HEADS):
                    v.tensor_tensor(out=k.acc[:, h, :, 0:DH], in0=k.acc[:, h, :, 0:DH],
                                    in1=den[:, h, :].unsqueeze(2).to_broadcast([P, T, DH]), op=ALU.mult)
                v.drain()
                dve.wait_ge(x_in, 16)
                for h in range(HEADS):
                    v.tensor_tensor(out=k.X[:, :, h * DH:(h + 1) * DH], in0=k.X[:, :, h * DH:(h + 1) * DH],
                                    in1=k.acc[:, h, :, 0:DH], op=ALU.add)
                v.drain()


def gat_separable_phase(k):
    nc = k.nc
    v, a, t_, g = nc.vector, nc.scalar, nc.tensor, nc.gpsimd
    R = U
    BANK = ((0, 1, 2, 3, 4), (5, 6, 7, 3, 4))
    OUT = (3, 4, 0, 1, 2)
    with scope(nc) as (sb, pb, sem):
        cnt = sb("cnt_block", [P, T, QB], BF16)
        ed_b = sb("ed_rows", [P, 2, HEADS, QB], FP32)
        kinds = sb("kinds", [P, R, 2, QB], BF16)
        sums = sb("set_sums", [P, U, 2, 3, D1], FP32)
        tot = sb("set_tot", [P, U, 2, D1], FP32)
        dst_now = sb("dst_now", [P, U, 2], FP32)
        num = sb("set_num", [P, U, D1], FP32)
        x_now = sb("set_x", [P, U, DH], FP32)
        den = sb("set_den", [P, U, 1], FP32)
        ps = pb("ps_sets", [128, 8, 512], FP32)
        x_in = sem("x_in_again")
        cnt_in = [sem(f"cnt_in{i}") for i in range(U)]
        ed_in = sem("ed_in")
        mask_done, kinds_done, pv_done = sem("mask_done"), sem("kinds_done"), sem("pv_done")
        copied, combined, act_passed = sem("set_copied"), sem("set_combined"), sem("act_passed")
        num_done, den_done = sem("num_done"), sem("den_done")
        SETS = U * HEADS
        with nc.Block() as block:
            @block.sync
            def _(sp):
                sp.sem_inc(pv_done, U * R)
                sp.sem_inc(copied, 2 * U)
                sp.sem_inc(combined, 1)
                sp.sem_inc(kinds_done, T)
                sp.sem_inc(ed_in, 16)
                sp.dma_start(k.X[:, :, :], k.x.rearrange("(t p) f -> p t f", p=P)).then_inc(x_in, 16)
                with sp.Fori(0, U) as j:
                    sp.wait_ge(ed_in, 16 * HEADS * j + 16)
                    for h in range(HEADS):
                        sp.dma_start(ed_b[:, bass.ds(j % 2, 1), h, :].rearrange("q a (t p) -> q (a t) p", p=P),
                                     k.ed_dram[bass.ds(j * U, U), h, :].unsqueeze(0).to_broadcast([P, U, P])).then_inc(ed_in, 16)
                    for i in range(U):
                        sp.wait_ge(kinds_done, HEADS * T * j + (i + 1) * U)
                        sp.dma_start(cnt[:, i * U:(i + 1) * U, :],
                                     k.counts.rearrange("(t p) d -> p t d", p=P)[:, i * U:(i + 1) * U, bass.ds(j * QB, QB)]).then_inc(cnt_in[i], 16)

            @block.scalar
            def _(act):
                def mask(q, i, s):
                    act.wait_ge(pv_done, U * (T * q + U * i + s + 1))
                    act.sem_inc(act_passed, 1)
                    a.activation(kinds[:, s, 0, :], ed_b[:, bass.ds((q // HEADS) % 2, 1), bass.ds(q % HEADS, 1), :].rearrange("p a h d -> p (a h d)"),
                                 ACT.Relu, scale=MASK_SCALE,
                                 bias=k.es_mask[:, bass.ds(U * i + s, 1), bass.ds(q % HEADS, 1)].rearrange("p a h -> p (a h)")).then_inc(mask_done, 1)

                def copies(q, half):
                    act.wait_ge(combined, q + 1)
                    for u in OUT:
                        act.wait_ge(pv_done, U * (T * (q + 1) - 1) + u + 1 + U * R)
                        a.activation(sums[:, u, :, :, :].rearrange("p e c d -> p (e c d)"), ps[0:P, BANK[half][u], 0:2 * W3],
                                     ACT.Copy).then_inc(copied, 1)

                def masks(q, half, first):
                    act.wait_ge(ed_in, 16 * HEADS * (q // HEADS + 1) + 16)
                    for s in range(U):
                        if s == U - 1 and not first:
                            copies(q - 1, 1 - half)
                        mask(q, 0, s)
                    with act.Fori(1, U) as i:
                        for s in range(U):
                            mask(q, i, s)

                masks(0, 0, True)
                with act.Fori(0, SETS // 2 - 1) as r:
                    masks(2 * r + 1, 1, False)
                    masks(2 * r + 2, 0, False)
                masks(SETS - 1, 1, False)
                copies(SETS - 1, 1)

            @block.vector
            def _(dve):
                def set_kinds(q, first):
                    for i in range(U):
                        dve.wait_ge(cnt_in[i], 16 * (q // HEADS + 1))
                        if i == 3 and not first:
                            reciprocals(q - 1)
                        for slots in ((0, 1), (2, 3), (4,)):
                            for s in slots:
                                dve.wait_ge(mask_done, T * q + U * i + s + 1)
                                v.tensor_tensor(out=kinds[:, s, 0, :], in0=kinds[:, s, 0, :], in1=cnt[:, U * i + s, :], op=ALU.min)
                            v.drain()
                            for s in slots:
                                v.tensor_tensor(out=kinds[:, s, 1, :], in0=cnt[:, U * i + s, :], in1=kinds[:, s, 0, :],
                                                op=ALU.subtract).then_inc(kinds_done, 1)

                def reciprocals(q):
                    dve.wait_ge(num_done, q + 1)
                    v.tensor_scalar(den[:, :, :], num[:, :, DH:D1], 1e-16, None, ALU.max)
                    v.drain()
                    v.reciprocal(den[:, :, :], den[:, :, :])
                    v.drain().then_inc(den_done, 1)

                set_kinds(0, True)
                with dve.Fori(1, SETS) as q:
                    set_kinds(q, False)
                reciprocals(SETS - 1)

            @block.tensor
            def _(pe):
                parts = zparts(k)

                def group(q, h, half, i, first, final):
                    for s in range(U):
                        pe.wait_ge(kinds_done, T * q + U * i + s + 1 + T)
                        for u in range(U):
                            if first and s == 0:
                                pe.wait_ge(copied, 5 * q + OUT.index(u) + 1 + (U if u >= 3 else 0))
                            for e in range(2):
                                last = t_.matmul(ps[0:P, BANK[half][u], e * W3:(e + 1) * W3], kinds[:, s, e, u * P:(u + 1) * P],
                                                 parts[:, bass.ds(U * i + s, 1), bass.ds(h, 1), e, :, :].rearrange("p a h c d -> p (a h c d)"),
                                                 start=(first and s == 0 and e == 0), stop=(final and s == U - 1 and e == 1))
                            last.then_inc(pv_done, 1)

                with pe.Fori(0, U) as j:
                    with pe.Fori(0, HEADS // 2) as r:
                        for half in range(2):
                            h = 2 * r + half
                            q = HEADS * j + h
                            group(q, h, half, 0, True, False)
                            with pe.Fori(1, U - 1) as i:
                                group(q, h, half, i, False, False)
                            group(q, h, half, U - 1, False, True)

            @block.gpsimd
            def _(pool):
                pool.wait_ge(x_in, 16)
                with pool.Fori(0, U) as j:
                    with pool.Fori(0, HEADS) as h:
                        pool.wait_ge(copied, U * (HEADS * j + h + 1) + 2 * U)
                        g.tensor_tensor(out=tot[:, :, :, :], in0=sums[:, :, :, 1, :], in1=sums[:, :, :, 2, :], op=ALU.add)
                        g.tensor_copy(dst_now[:, :, :], k.dst_exp[:, bass.ds(U * j, U), bass.ds(h, 1), :].rearrange("p t h e -> p t (h e)"))
                        g.drain()
                        g.tensor_tensor(out=tot[:, :, :, :], in0=tot[:, :, :, :], in1=sums[:, :, :, 0, :], op=ALU.add)
                        g.drain().then_inc(combined, 1)
                        g.tensor_tensor(out=tot[:, :, :, :], in0=tot[:, :, :, :], in1=dst_now[:, :, :].unsqueeze(3).to_broadcast([P, U, 2, D1]), op=ALU.mult)
                        g.drain()
                        g.tensor_tensor(out=num[:, :, :], in0=tot[:, :, 0, :], in1=tot[:, :, 1, :], op=ALU.add)
                        g.drain().then_inc(num_done, 1)
                        pool.wait_ge(den_done, HEADS * j + h + 1)
                        g.tensor_tensor(out=num[:, :, 0:DH], in0=num[:, :, 0:DH], in1=den[:, :, :].to_broadcast([P, U, DH]), op=ALU.mult)
                        g.drain()
                        g.tensor_copy(x_now[:, :, :], k.X[:, bass.ds(U * j, U), bass.ds(h * DH, DH)])
                        g.drain()
                        g.tensor_tensor(out=num[:, :, 0:DH], in0=num[:, :, 0:DH], in1=x_now[:, :, :], op=ALU.add)
                        g.drain()
                        g.tensor_copy(k.X[:, bass.ds(U * j, U), bass.ds(h * DH, DH)], num[:, :, 0:DH])
                        g.drain()


HALF = (QB + 1) // 2
HALVES = [(0, HALF), (HALF, QB - HALF)]


def column(ap):
    return ap.rearrange("(p a) -> p a", a=1)


def moe_phase(k):
    nc = k.nc
    v, a, t_ = nc.vector, nc.scalar, nc.tensor
    X = k.X
    EX, H2 = 4, 64
    NB1 = 6
    I1, I2 = 2 * NB1, 2 * (EX + 1)
    IT = I1 + I2
    with scope(nc) as (sb, pb, sem):
        H = sb("h_moe", [P, U, F], FP32)
        HT = sb("hT_moe", [128, KF, QB], FP32)
        st = sb("bn_st_m", [P, U, 6], FP32)
        mv = sb("bn_mv_m", [P, U, 2], FP32)
        MV = sb("bn_all_m", [P, T, 2], FP32)
        std = sb("std_m", [P, T], FP32)
        rstd = sb("rstd_m", [P, T], FP32)
        eps = sb("eps_m", [P, 1], FP32)
        w1 = sb("moe_w1", [128, KF, NB1, 128], FP32)
        w2e = sb("moe_w2e", [128, EX, H2], FP32)
        w2s = sb("moe_w2s", [128, KF, 128], FP32)
        w3e = sb("moe_w3e", [H2, EX, F], FP32)
        w3s = sb("moe_w3s", [128, F], FP32)
        b3 = sb("moe_b3", [EX + 1, F], FP32)
        b1 = sb("moe_b1", [128, NB1], FP32)
        b2e = sb("moe_b2e", [H2, EX], FP32)
        b2s = sb("moe_b2s", [128, 1], FP32)
        gw = sb("gate_w", [128, KF, EX], FP32)
        gb = sb("gate_b", [P, EX], FP32)
        A1 = sb("moe_a1", [128, NB1, QB], FP32)
        A2e = sb("moe_a2e", [H2, EX, QB], FP32)
        A2s = sb("moe_a2s", [128, QB], FP32)
        lg = sb("gate_logits", [P, U, EX], FP32)
        ge = sb("gate_exp", [P, U, EX], FP32)
        m1 = sb("gate_m1", [P, U, EX], FP32)
        m2 = sb("gate_m2", [P, U, EX], FP32)
        prio = sb("gate_prio", [P, U, EX], FP32)
        g1 = sb("gate_s1", [P, U], FP32)
        g2 = sb("gate_s2", [P, U], FP32)
        g3 = sb("gate_s3", [P, U], FP32)
        g5 = sb("gate_weights", [P, U, EX + 1], FP32)
        gT = sb("gate_weightsT", [EX + 1, QB], FP32)
        ps_t = pb("ps_tm", [128, 3, 512], FP32)
        ps_f = pb("ps_fm", [128, 2, 512], FP32)
        ps_o = pb("ps_om", [128, 3, 512], FP32)
        w_in, stats_done, std_done = sem("m_w_in"), sem("m_stats"), sem("m_std")
        h_ready, t_ready, ht_ready = sem("m_h_ready"), sem("m_t_ready"), sem("m_ht_ready")
        f_done, f_out, o_done, o_out = sem("m_f_done"), sem("m_f_out"), sem("m_o_done"), sem("m_o_out")
        lg_psum, lg_max, lg_exp, top_done, top_exp = sem("m_lg_psum"), sem("m_lg_max"), sem("m_lg_exp"), sem("m_top"), sem("m_top_exp")
        g_ready, gt_psum, gt_ready, wr = sem("m_g_ready"), sem("m_gt_psum"), sem("m_gt_ready"), k.args
        with nc.Block() as block:
            @block.sync
            def _(sp):
                loads = [
                    (w1[:, :, 0:EX, :], wr["L0_ffn_eW1"].rearrange("e (q i) o -> q i e o", i=128)),
                    (w1[:, :, EX:NB1, :], wr["L0_ffn_sW1"].rearrange("(q i) (b o) -> q i b o", i=128, o=128)),
                ]
                for dst, src in loads:
                    for q in range(KF):
                        sp.dma_start(dst[:, q], src[q]).then_inc(w_in, 16)
                rest = [
                    (w2e[:, :, :], wr["L0_ffn_eW2"].rearrange("e i o -> i e o")),
                    (w2s[:, :, :], wr["L0_ffn_sW2"].rearrange("(q i) o -> i q o", i=128)),
                    (w3e[:, :, :], wr["L0_ffn_eW3"].rearrange("e i o -> i e o")),
                    (w3s[:, :], wr["L0_ffn_sW3"]),
                    (b3[0:EX, :], wr["L0_ffn_eb3"]),
                    (b3[EX:EX + 1, :], wr["L0_ffn_sb3"].rearrange("(a f) -> a f", a=1)),
                    (b2s[:, :], column(wr["L0_ffn_sb2"])),
                    (gw[:, :, :], wr["L0_ffn_gW"].rearrange("(q i) e -> i q e", i=128)),
                    (gb[:, :], wr["L0_ffn_gb"].unsqueeze(0).to_broadcast([P, EX])),
                ]
                for e in range(EX):
                    rest.append((b1[:, e:e + 1], column(wr["L0_ffn_eb1"][e])))
                    rest.append((b2e[:, e:e + 1], column(wr["L0_ffn_eb2"][e])))
                for b in range(2):
                    rest.append((b1[:, EX + b:EX + b + 1], column(wr["L0_ffn_sb1"][b * 128:(b + 1) * 128])))
                for dst, src in rest:
                    sp.dma_start(dst, src).then_inc(w_in, 16)
                k.moe_loads = 2 * KF + len(rest)

            @block.vector
            def _(dve):
                v.memset(eps[:, :], EPS)
                v.memset(g5[:, :, :], 1.0)
                for e in range(EX):
                    v.memset(prio[:, :, e], float(EX - e))
                layernorm_stats(nc, dve, v, X, st, mv, MV)
                v.nop().then_inc(stats_done, 1)
                dve.wait_ge(std_done, 1)
                v.reciprocal(rstd[:, :], std[:, :])
                v.drain()
                dve.wait_ge(w_in, 16 * k.moe_loads)

                def bc(s):
                    return s[:, :].unsqueeze(2).to_broadcast([P, U, EX])

                def first_largest(mask, values):
                    v.tensor_reduce(out=g1[:, :], in_=values[:, :, :], axis=AXX, op=ALU.max)
                    v.drain()
                    v.tensor_tensor(out=mask[:, :, :], in0=values[:, :, :], in1=bc(g1), op=ALU.is_equal)
                    v.drain()
                    v.tensor_tensor(out=mask[:, :, :], in0=mask[:, :, :], in1=prio[:, :, :], op=ALU.mult)
                    v.drain()
                    v.tensor_reduce(out=g2[:, :], in_=mask[:, :, :], axis=AXX, op=ALU.max)
                    v.drain()
                    v.tensor_tensor(out=mask[:, :, :], in0=mask[:, :, :], in1=bc(g2), op=ALU.is_equal)
                    v.drain()

                def gates(i):
                    dve.wait_ge(lg_psum, i + 1)
                    v.tensor_tensor(out=lg[:, :, :], in0=ps_t[0:P, 2, 256:256 + U * EX].rearrange("p (u e) -> p u e", e=EX),
                                    in1=gb[:, :].unsqueeze(1).to_broadcast([P, U, EX]), op=ALU.add)
                    v.drain()
                    v.tensor_reduce(out=g1[:, :], in_=lg[:, :, :], axis=AXX, op=ALU.max)
                    v.drain()
                    v.tensor_tensor(out=lg[:, :, :], in0=lg[:, :, :], in1=bc(g1), op=ALU.subtract)
                    v.drain().then_inc(lg_max, 1)
                    dve.wait_ge(lg_exp, i + 1)
                    v.tensor_reduce(out=g1[:, :], in_=ge[:, :, :], axis=AXX, op=ALU.add)
                    v.drain()
                    v.reciprocal(g1[:, :], g1[:, :])
                    v.drain()
                    v.tensor_tensor(out=ge[:, :, :], in0=ge[:, :, :], in1=bc(g1), op=ALU.mult)
                    v.drain()
                    first_largest(m1, ge)
                    v.tensor_copy(g3[:, :], g1[:, :])
                    v.scalar_tensor_tensor(out=ge[:, :, :], in0=m1[:, :, :], scalar=-4.0, in1=ge[:, :, :], op0=ALU.mult, op1=ALU.add)
                    v.drain()
                    first_largest(m2, ge)
                    v.tensor_tensor(out=g3[:, :], in0=g1[:, :], in1=g3[:, :], op=ALU.subtract)
                    v.drain().then_inc(top_done, 1)
                    dve.wait_ge(top_exp, i + 1)
                    v.tensor_scalar(g1[:, :], g3[:, :], 1.0, None, ALU.add)
                    v.drain()
                    v.reciprocal(g1[:, :], g1[:, :])
                    v.drain()
                    v.tensor_tensor(out=g2[:, :], in0=g3[:, :], in1=g1[:, :], op=ALU.mult)
                    v.tensor_tensor(out=m1[:, :, :], in0=m1[:, :, :], in1=bc(g1), op=ALU.mult)
                    v.drain()
                    v.tensor_tensor(out=m2[:, :, :], in0=m2[:, :, :], in1=bc(g2), op=ALU.mult)
                    v.drain()
                    v.tensor_tensor(out=g5[:, :, 0:EX], in0=m1[:, :, :], in1=m2[:, :, :], op=ALU.add)
                    v.drain().then_inc(g_ready, 1)

                def combine(i):
                    for u in range(U):
                        xt = X[:, bass.ds(i * U + u, 1), :].rearrange("p a f -> p (a f)")
                        for b, parts in enumerate([(None, 0), (1, 2), (3,)]):
                            dve.wait_ge(o_done, 3 * (U * i + u) + b + 1)
                            for s, e in enumerate(parts):
                                src = ps_o[0:P, b, s * F:(s + 1) * F]
                                if e is None:
                                    v.tensor_tensor(out=xt, in0=src, in1=xt, op=ALU.add)
                                else:
                                    v.scalar_tensor_tensor(out=xt, in0=src, scalar=g5[:, u, e:e + 1], in1=xt, op0=ALU.mult, op1=ALU.add)
                                d = v.drain()
                            d.then_inc(o_out, 1)

                normalize_batch(v, X, H, MV, rstd, 0, h_ready, t_ready, dve, True)
                with dve.Fori(1, U) as i:
                    normalize_batch(v, X, H, MV, rstd, i, h_ready, t_ready, dve, False)
                    gates(i - 1)
                    combine(i - 1)
                gates(U - 1)
                combine(U - 1)

            @block.scalar
            def _(act):
                act.sem_inc(f_out, 2)
                act.wait_ge(stats_done, 1)
                a.activation(std[:, :], MV[:, :, 1], ACT.Sqrt, bias=eps[:, 0:1])
                a.drain().then_inc(std_done, 1)

                def copies(i):
                    for b, tiles in enumerate(BANKS):
                        act.wait_ge(t_ready, 3 * i + b + 1)
                        n = len(tiles)
                        a.activation(HT[:, :, tiles[0] * P:(tiles[0] + n) * P].rearrange("p q (u c) -> p u q c", c=P),
                                     ps_t[:, b, 0:n * KF * P].rearrange("p (u q c) -> p u q c", u=n, c=P), ACT.Copy).then_inc(ht_ready, 1)

                def layers(i):
                    m = 0
                    for o in range(NB1):
                        for lo, n in HALVES:
                            act.wait_ge(f_done, IT * i + m + 1)
                            a.activation(A1[:, o, lo:lo + n], ps_f[:, m % 2, 0:n], ACT.Relu, bias=b1[:, o:o + 1]).then_inc(f_out, 1)
                            m += 1
                        if o == 0:
                            act.wait_ge(lg_max, i + 1)
                            a.activation(ge[:, :, :], lg[:, :, :], ACT.Exp).then_inc(lg_exp, 1)
                        if o == 2:
                            act.wait_ge(top_done, i + 1)
                            a.activation(g3[:, :], g3[:, :], ACT.Exp).then_inc(top_exp, 1)
                    for e in range(EX + 1):
                        for lo, n in HALVES:
                            act.wait_ge(f_done, IT * i + m + 1)
                            if e < EX:
                                a.activation(A2e[:, e, lo:lo + n], ps_f[0:H2, m % 2, 0:n], ACT.Relu, bias=b2e[:, e:e + 1]).then_inc(f_out, 1)
                            else:
                                a.activation(A2s[:, lo:lo + n], ps_f[:, m % 2, 0:n], ACT.Relu, bias=b2s[:, 0:1]).then_inc(f_out, 1)
                            m += 1
                    act.wait_ge(gt_psum, i + 1)
                    a.activation(gT[:, 0:4 * P], ps_t[0:EX + 1, 0, 0:4 * P], ACT.Copy)
                    a.activation(gT[:, 4 * P:QB], ps_t[0:EX + 1, 1, 0:P], ACT.Copy)
                    a.drain().then_inc(gt_ready, 1)

                copies(0)
                act.wait_ge(w_in, 16 * k.moe_loads)
                with act.Fori(1, U) as i:
                    layers(i - 1)
                    copies(i)
                layers(U - 1)

            @block.tensor
            def _(pe):
                def transposes(i, first):
                    for b, tiles in enumerate(BANKS):
                        if not first and b == 0:
                            pe.wait_ge(gt_ready, i)
                        pe.wait_ge(h_ready, U * i + tiles[-1] + 1)
                        for s, u in enumerate(tiles):
                            for q in range(KF):
                                last = t_.transpose(ps_t[:, b, (s * KF + q) * P:(s * KF + q + 1) * P],
                                                    H[:, u, q * 128:(q + 1) * 128], k.ident[0:P, 0:P])
                        last.then_inc(t_ready, 1)

                def layers(i):
                    pe.wait_ge(ht_ready, 3 * (i + 1))
                    for u in range(U):
                        for q in range(KF):
                            last = t_.matmul(ps_t[0:P, 2, 256 + u * EX:256 + (u + 1) * EX], HT[:, q, u * P:(u + 1) * P], gw[:, q, :],
                                             start=(q == 0), stop=(q == KF - 1))
                    last.then_inc(lg_psum, 1)
                    m = 0
                    for o in range(NB1):
                        for lo, n in HALVES:
                            pe.wait_ge(f_out, IT * i + m + 1)
                            for q in range(KF):
                                last = t_.matmul(ps_f[:, m % 2, 0:n], w1[:, q, o, :], HT[:, q, lo:lo + n], start=(q == 0), stop=(q == KF - 1))
                            last.then_inc(f_done, 1)
                            m += 1
                    for e in range(EX + 1):
                        for lo, n in HALVES:
                            pe.wait_ge(f_out, IT * i + m + 1)
                            if e < EX:
                                last = t_.matmul(ps_f[0:H2, m % 2, 0:n], w2e[:, e, :], A1[:, e, lo:lo + n], start=True, stop=True)
                            else:
                                for q in range(KF):
                                    last = t_.matmul(ps_f[:, m % 2, 0:n], w2s[:, q, :], A1[:, EX + q, lo:lo + n],
                                                     start=(q == 0), stop=(q == KF - 1))
                            last.then_inc(f_done, 1)
                            m += 1
                    pe.wait_ge(g_ready, i + 1)
                    for u in range(U):
                        last = t_.transpose(ps_t[0:EX + 1, u // 4, (u % 4) * P:(u % 4 + 1) * P], g5[:, u, :], k.ident[0:P, 0:P])
                    last.then_inc(gt_psum, 1)

                def outputs(i):
                    pe.wait_ge(f_out, IT * (i + 1) + 2)
                    pe.wait_ge(gt_ready, i + 1)
                    for u in range(U):
                        cols = slice(u * P, (u + 1) * P)
                        for b, parts in enumerate([(None, 0), (1, 2), (3,)]):
                            pe.wait_ge(o_out, 3 * (U * i + u) + b + 1)
                            for s, e in enumerate(parts):
                                dst = ps_o[0:P, b, s * F:(s + 1) * F]
                                if e is None:
                                    t_.matmul(dst, A2s[:, cols], w3s[:, :], start=True, stop=False)
                                    last = t_.matmul(dst, gT[:, cols], b3[:, :], start=False, stop=True)
                                else:
                                    last = t_.matmul(dst, A2e[:, e, cols], w3e[:, e, :], start=True, stop=True)
                            last.then_inc(o_done, 1)

                pe.sem_inc(o_out, 3)
                pe.wait_ge(w_in, 16 * k.moe_loads)
                transposes(0, True)
                with pe.Fori(1, U) as i:
                    layers(i - 1)
                    transposes(i, False)
                    outputs(i - 1)
                layers(U - 1)
                outputs(U - 1)


def row_of(X, t):
    return X[:, bass.ds(t, 1), 0:F].rearrange("p a f -> p (a f)")


def split_rest_dve(dve, v, full, rest, R3, hi_done, rest_done, mid_done, i):
    rows = R3[:, bass.ds(i * U, U), :]
    dve.wait_ge(hi_done, i + 1)
    v.tensor_tensor(out=rest[:, :, :], in0=full[:, :, :], in1=rows[:, :, 0:F], op=ALU.subtract)
    v.drain().then_inc(rest_done, 1)
    dve.wait_ge(mid_done, i + 1)
    v.tensor_tensor(out=rows[:, :, PART[2][0]:X3], in0=rest[:, :, :], in1=rows[:, :, PART[1][0]:PART[1][0] + F], op=ALU.subtract)
    v.drain()


def split_parts_act(act, a, full, rest, R3, full_done, hi_done, rest_done, mid_done):
    with act.Fori(0, U) as i:
        act.wait_ge(full_done, i + 1)
        a.activation(R3[:, bass.ds(i * U, U), 0:F], full[:, :, :], ACT.Copy).then_inc(hi_done, 1)
        act.wait_ge(rest_done, i + 1)
        a.activation(R3[:, bass.ds(i * U, U), PART[1][0]:PART[1][0] + F], rest[:, :, :], ACT.Copy).then_inc(mid_done, 1)


def conv_input_phase(k, name, weights, source, R3):
    nc = k.nc
    v, a, t_, g = nc.vector, nc.scalar, nc.tensor, nc.gpsimd
    X = k.X
    with scope(nc) as (sb, pb, sem):
        H = sb(name + "h", [P, U, F], FP32)
        HT = sb(name + "hT", [128, KF, QB], FP32)
        W = sb(name + "w", [128, KF, F], FP32)
        full = sb(name + "full", [P, U, F], FP32)
        rest = sb(name + "rest", [P, U, F], FP32)
        st = sb(name + "st", [P, U, 6], FP32)
        mv = sb(name + "mv", [P, U, 2], FP32)
        MV = sb(name + "MV", [P, T, 2], FP32)
        std = sb(name + "std", [P, T], FP32)
        rstd = sb(name + "rstd", [P, T], FP32)
        eps = sb(name + "eps", [P, 1], FP32)
        ps_t = pb(name + "ps_t", [128, 3, 512], FP32)
        ps_z = pb(name + "ps_z", [128, 3, 512], FP32)
        w_in, stats_done, std_done = sem(name + "w_in"), sem(name + "stats"), sem(name + "std_done")
        h_ready, t_ready, ht_ready = sem(name + "h_ready"), sem(name + "t_ready"), sem(name + "ht_ready")
        z_ready, z_free = sem(name + "z_ready"), sem(name + "z_free")
        kept = sem(name + "kept")
        full_done, hi_done, rest_done, mid_done = sem(name + "full"), sem(name + "hi"), sem(name + "rest_d"), sem(name + "mid")
        with nc.Block() as block:
            @block.sync
            def _(sp):
                sp.dma_start(W[:, :, :], weights.rearrange("(q i) o -> i q o", i=128)).then_inc(w_in, 16)

            @block.vector
            def _(dve):
                dve.sem_inc(z_free, 3)
                v.memset(R3[:, :, F:F + 1], 1.0)

                def split(i):
                    for b, tiles in enumerate(BANKS):
                        dve.wait_ge(z_ready, 3 * i + b + 1)
                        n = len(tiles)
                        v.tensor_copy(full[:, tiles[0]:tiles[0] + n, :].rearrange("p u f -> p (u f)"),
                                      ps_z[0:P, b, 0:n * F])
                        v.drain().then_inc(z_free, 1)
                    v.nop().then_inc(full_done, 1)
                    split_rest_dve(dve, v, full, rest, R3, hi_done, rest_done, mid_done, i)

                if source is None:
                    v.memset(eps[:, :], EPS)
                    layernorm_stats(nc, dve, v, X, st, mv, MV)
                    v.nop().then_inc(stats_done, 1)
                    dve.wait_ge(std_done, 1)
                    v.reciprocal(rstd[:, :], std[:, :])
                    v.drain()
                    normalize_batch(v, X, H, MV, rstd, 0, h_ready, t_ready, dve, True)
                    with dve.Fori(1, U) as i:
                        dve.wait_ge(kept, i)
                        normalize_batch(v, X, H, MV, rstd, i, h_ready, t_ready, dve, False)
                        split(i - 1)
                    split(U - 1)
                else:
                    with dve.Fori(0, U) as i:
                        split(i)

            @block.gpsimd
            def _(pool):
                if source is None:
                    with pool.Fori(0, U) as i:
                        pool.wait_ge(h_ready, U * (i + 1))
                        g.tensor_copy(k.LNX[:, bass.ds(i * U, U), :], H[:, :, :])
                        g.drain().then_inc(kept, 1)
                else:
                    def stage(i, first):
                        for u in range(U):
                            if not first:
                                pool.wait_ge(t_ready, 3 * (i - 1) + u // 2 + 1)
                            g.tensor_copy(H[:, u, :], row_of(source, i * U + u)).then_inc(h_ready, 1)
                    stage(0, True)
                    with pool.Fori(1, U) as i:
                        stage(i, False)

            @block.scalar
            def _(act):
                if source is None:
                    act.wait_ge(stats_done, 1)
                    a.activation(std[:, :], MV[:, :, 1], ACT.Sqrt, bias=eps[:, 0:1])
                    a.drain().then_inc(std_done, 1)

                def copies(i, first):
                    for b, tiles in enumerate(BANKS):
                        act.wait_ge(t_ready, 3 * i + b + 1)
                        if not first:
                            act.wait_ge(z_ready, 3 * (i - 1) + b + 1)
                        n = len(tiles)
                        a.activation(HT[:, :, tiles[0] * P:(tiles[0] + n) * P].rearrange("p q (u c) -> p u q c", c=P),
                                     ps_t[:, b, 0:n * KF * P].rearrange("p (u q c) -> p u q c", u=n, c=P), ACT.Copy).then_inc(ht_ready, 1)

                def parts(i):
                    act.wait_ge(full_done, i + 1)
                    a.activation(R3[:, bass.ds(i * U, U), 0:F], full[:, :, :], ACT.Copy).then_inc(hi_done, 1)
                    act.wait_ge(rest_done, i + 1)
                    a.activation(R3[:, bass.ds(i * U, U), PART[1][0]:PART[1][0] + F], rest[:, :, :], ACT.Copy).then_inc(mid_done, 1)

                copies(0, True)
                with act.Fori(1, U) as i:
                    copies(i, False)
                    parts(i - 1)
                parts(U - 1)

            @block.tensor
            def _(pe):
                def products(i):
                    for b, tiles in enumerate(BANKS):
                        pe.wait_ge(ht_ready, 3 * i + b + 1)
                        pe.wait_ge(z_free, 3 * i + b + 1)
                        for s, u in enumerate(tiles):
                            for q in range(KF):
                                last = t_.matmul(ps_z[0:P, b, s * F:(s + 1) * F], HT[:, q, u * P:(u + 1) * P], W[:, q, :],
                                                 start=(q == 0), stop=(q == KF - 1))
                        last.then_inc(z_ready, 1)

                pe.wait_ge(w_in, 16)
                transpose_batch(pe, t_, k, H, ps_t, h_ready, ht_ready, t_ready, 0, True)
                with pe.Fori(1, U) as i:
                    transpose_batch(pe, t_, k, H, ps_t, h_ready, ht_ready, t_ready, i, False)
                    products(i - 1)
                products(U - 1)


def conv_step_phase(k, name, planes, R3, kind, out3=None, bias=None, target=None):
    nc = k.nc
    v, a, t_ = nc.vector, nc.scalar, nc.tensor
    X = k.X
    NS = U * len(planes)
    with scope(nc) as (sb, pb, sem):
        ring = sb(name + "ring", [P, U, U, QB], BF16)
        full = sb(name + "full", [P, U, F], FP32)
        rest = sb(name + "rest", [P, U, F], FP32)
        num = sb(name + "num", [P, U], FP32)
        one = sb(name + "one", [P, U], FP32)
        inv = sb(name + "inv", [P, U], FP32)
        bias_b = sb(name + "bias", [P, F], FP32)
        slope = sb(name + "slope", [P, 1], FP32)
        ps = pb(name + "ps", [128, U, 512], FP32)
        c_in = [sem(name + f"c_in{s}") for s in range(U)]
        c_used, c_out, b_in = sem(name + "c_used"), sem(name + "c_out"), sem(name + "b_in")
        full_done, hi_done, rest_done, mid_done = sem(name + "full_d"), sem(name + "hi"), sem(name + "rest_d"), sem(name + "mid")
        with nc.Block() as block:
            @block.sync
            def _(sp):
                if kind != "edges":
                    sp.dma_start(bias_b[:, :], bias.unsqueeze(0).to_broadcast([P, F])).then_inc(b_in, 16)
                    sp.dma_start(slope[:, :], k.args["L1_gnn_a"].unsqueeze(0).to_broadcast([P, 1])).then_inc(b_in, 16)
                with sp.Fori(0, U) as i:
                    for s in range(NS):
                        sp.wait_ge(c_used, NS * i + s + 1)
                        sp.dma_start(ring[:, s % U, :, :],
                                     planes[s // U][(s % U) * QB:(s % U + 1) * QB, bass.ds(i * QB, QB)].rearrange("(t p) d -> p t d", p=P))\
                            .then_inc(c_in[s % U], 16)

            @block.tensor
            def _(pe):
                with pe.Fori(0, U) as i:
                    for s in range(NS):
                        pe.wait_ge(c_in[s % U], 16 * (len(planes) * i + s // U + 1))
                        for w in range(U):
                            t = s * U + w
                            for kk in range(U):
                                if t == 0:
                                    pe.wait_ge(c_out, U * i + kk + 1)
                                for j, (off, n) in enumerate(PART):
                                    last = t_.matmul(ps[0:P, kk, 0:n], ring[:, s % U, w, kk * P:(kk + 1) * P], R3[:, t % T, off:off + n],
                                                     start=(t == 0 and j == 0), stop=(t == NS * U - 1 and j == 2))
                        last.then_inc(c_used, 1)

            @block.vector
            def _(dve):
                dve.sem_inc(c_out, U)
                dve.sem_inc(c_used, U)
                if kind == "edges":
                    v.memset(out3[:, :, F:F + 1], 1.0)
                else:
                    dve.wait_ge(b_in, 32)
                with dve.Fori(0, U) as i:
                    dve.wait_ge(c_used, NS * (i + 1) + U)
                    v.tensor_scalar(num[:, :], ps[0:P, :, F], 1.0, None, ALU.max)
                    v.tensor_scalar(one[:, :], ps[0:P, :, F], 1.0, None, ALU.min)
                    v.drain()
                    v.reciprocal(num[:, :], num[:, :])
                    v.drain()
                    v.tensor_tensor(out=inv[:, :], in0=num[:, :], in1=one[:, :], op=ALU.mult)
                    v.drain()
                    for kk in range(U):
                        if kind == "edges":
                            v.tensor_scalar(full[:, kk, :], ps[0:P, kk, 0:F], inv[:, kk:kk + 1], None, ALU.mult).then_inc(c_out, 1)
                        else:
                            v.scalar_tensor_tensor(out=full[:, kk, :], in0=ps[0:P, kk, 0:F], scalar=inv[:, kk:kk + 1], in1=bias_b[:, :],
                                                   op0=ALU.mult, op1=ALU.add).then_inc(c_out, 1)
                    v.drain()
                    if kind == "edges":
                        v.nop().then_inc(full_done, 1)
                        split_rest_dve(dve, v, full, rest, out3, hi_done, rest_done, mid_done, i)
                    else:
                        rows = bass.ds(i * U, U)
                        if kind == "last":
                            v.tensor_tensor(out=full[:, :, :], in0=full[:, :, :], in1=k.LNX[:, rows, :], op=ALU.add)
                            v.drain()
                        v.tensor_scalar(rest[:, :, :], full[:, :, :], 0.0, slope[:, 0:1], ALU.min, ALU.mult)
                        v.drain()
                        if kind == "hidden":
                            v.scalar_tensor_tensor(out=target[:, rows, 0:F], in0=full[:, :, :], scalar=0.0, in1=rest[:, :, :],
                                                   op0=ALU.max, op1=ALU.add)
                        else:
                            v.scalar_tensor_tensor(out=full[:, :, :], in0=full[:, :, :], scalar=0.0, in1=rest[:, :, :],
                                                   op0=ALU.max, op1=ALU.add)
                            v.drain()
                            v.tensor_tensor(out=X[:, rows, :], in0=X[:, rows, :], in1=full[:, :, :], op=ALU.add)
                        v.drain()

            @block.scalar
            def _(act):
                if kind == "edges":
                    split_parts_act(act, a, full, rest, out3, full_done, hi_done, rest_done, mid_done)


def ffn_phase(k):
    nc = k.nc
    v, a, t_ = nc.vector, nc.scalar, nc.tensor
    X, wr = k.X, k.args
    HB8 = 1024 // 128
    I1 = 2 * HB8
    TOPK = N // 2 - 1
    with scope(nc) as (sb, pb, sem):
        H = sb("f_h", [P, U, F], FP32)
        HT = sb("f_hT", [128, KF, QB], FP32)
        st = sb("f_st", [P, U, 6], FP32)
        mv = sb("f_mv", [P, U, 2], FP32)
        MV = sb("f_MV", [P, T, 2], FP32)
        std = sb("f_std", [P, T], FP32)
        rstd = sb("f_rstd", [P, T], FP32)
        eps = sb("f_eps", [P, 1], FP32)
        w1 = sb("f_w1", [128, KF, HB8 * 128], FP32)
        w2 = sb("f_w2", [128, HB8, F], FP32)
        b1 = sb("f_b1", [128, HB8], FP32)
        b2 = sb("f_b2", [P, F], FP32)
        wr_b = sb("f_wr", [P, F], FP32)
        br_b = sb("f_br", [P, 1], FP32)
        A = sb("f_a", [128, HB8, QB], FP32)
        Y = k.arena[0:P, 0:2 * T * F].bitcast(FP32).rearrange("p (t f) -> p t f", t=T)
        wt5 = sb("f_wt5", [P, U], FP32)
        wt = sb("f_wt", [P, T], FP32)
        wtT = sb("f_wtT", [T, P], FP32)
        w_row = sb("f_w_row", [P, N], FP32)
        junk = sb("f_junk", [P, N], BF16)
        prod = sb("f_prod", [P, U, F], FP32)
        before = sb("f_before", [P, P], FP32)
        gt = sb("f_gt", [P, T], FP32)
        ge = sb("f_ge", [P, T], FP32)
        tie = sb("f_tie", [P, T], FP32)
        ws = sb("f_ws", [P, T], FP32)
        ps_t = pb("f_ps_t", [128, 3, 512], FP32)
        ps_f = pb("f_ps_f", [128, 2, 512], FP32)
        ps_o = pb("f_ps_o", [128, 3, 512], FP32)
        w_in, s_in, stats_done, std_done = sem("f_w_in"), sem("f_s_in"), sem("f_stats"), sem("f_std_done")
        h_ready, t_ready, ht_ready = sem("f_h_ready"), sem("f_t_ready"), sem("f_ht_ready")
        f_done, f_out, o_done, y_done = sem("f_done"), sem("f_out"), sem("f_o_done"), sem("f_y_done")
        wt_done, wt_psum, wt_copied, wt_stored, row_in, tri_done = (sem("f_wt_done"), sem("f_wt_psum"), sem("f_wt_copied"),
                                                                    sem("f_wt_stored"), sem("f_row_in"), sem("f_tri"))
        out_ready, out_stored = sem("f_out_ready"), sem("f_out_stored")
        with nc.Block() as block:
            @block.sync
            def _(sp):
                sp.dma_start(wr_b[:, :], wr["L1_ffn_wr"].rearrange("f a -> a f").to_broadcast([P, F])).then_inc(s_in, 16)
                sp.dma_start(br_b[:, :], wr["L1_ffn_br"].unsqueeze(0).to_broadcast([P, 1])).then_inc(s_in, 16)
                sp.dma_start(b2[:, :], wr["L1_ffn_b2"].unsqueeze(0).to_broadcast([P, F])).then_inc(s_in, 16)
                sp.dma_start(w1[:, :, :], wr["L1_ffn_w1"].rearrange("(q i) o -> i q o", i=128)).then_inc(w_in, 16)
                for o in range(HB8):
                    sp.dma_start(b1[:, o:o + 1], column(wr["L1_ffn_b1"][o * 128:(o + 1) * 128])).then_inc(w_in, 16)
                sp.dma_start(w2[:, :, :], wr["L1_ffn_w2"].rearrange("(q i) o -> i q o", i=128)).then_inc(w_in, 16)
                sp.wait_ge(wt_copied, 1)
                sp.dma_start(k.wt_dram, wtT[:, :]).then_inc(wt_stored, 16)
                sp.wait_ge(wt_stored, 16)
                sp.dma_start(w_row[:, :], k.wt_dram.rearrange("(a t) p -> a (t p)", a=1).to_broadcast([P, N])).then_inc(row_in, 16)
                for i in range(U):
                    sp.wait_ge(out_ready, i + 1)
                    sp.dma_start(k.out.rearrange("(t p) f -> p t f", p=P)[:, i * U:(i + 1) * U, :], X[:, i * U:(i + 1) * U, :]).then_inc(out_stored, 16)
                sp.wait_ge(out_stored, 16 * U)

            @block.gpsimd
            def _(pool):
                nc.gpsimd.affine_select(out=before[:, :], in_=k.ones[0:P, 0:P], compare_op=ALU.is_gt, fill=0.0, base=0,
                                        pattern=[[-1, P]], channel_multiplier=1)
                nc.gpsimd.drain().then_inc(tri_done, 1)

            @block.vector
            def _(dve):
                v.memset(eps[:, :], EPS)
                layernorm_stats(nc, dve, v, X, st, mv, MV)
                v.nop().then_inc(stats_done, 1)
                dve.wait_ge(std_done, 1)
                v.reciprocal(rstd[:, :], std[:, :])
                v.drain()
                dve.wait_ge(s_in, 48)
                with dve.Fori(0, U) as i:
                    for u in range(U):
                        t = i * U + u
                        v.tensor_scalar(prod[:, u, :], row_of(X, t), MV[:, bass.ds(t, 1), 0:1].rearrange("p a b -> p (a b)"),
                                        rstd[:, bass.ds(t, 1)], ALU.subtract, ALU.mult)
                    v.drain()
                    v.tensor_tensor(out=prod[:, :, :], in0=prod[:, :, :], in1=wr_b[:, :].unsqueeze(1).to_broadcast([P, U, F]), op=ALU.mult)
                    v.drain()
                    v.tensor_reduce(out=wt5[:, :], in_=prod[:, :, :], axis=AXX, op=ALU.add)
                    v.drain()
                    v.tensor_scalar(wt[:, bass.ds(i * U, U)], wt5[:, :], br_b[:, 0:1], None, ALU.add)
                    v.drain()
                v.nop().then_inc(wt_done, 1)

                for i in range(U):
                    normalize_batch(v, X, H, MV, rstd, i, h_ready, t_ready, dve, i == 0)
                    if i == 0:
                        dve.wait_ge(row_in, 16)
                        dve.wait_ge(tri_done, 1)
                        v.memset(ge[:, 0:1], 0.0)
                    for t in range(i * U, (i + 1) * U):
                        c = t * P
                        if t:
                            v.tensor_scalar(junk[:, 0:c], w_row[:, 0:c], wt[:, t:t + 1], 0.0, ALU.is_ge, ALU.add, accum_out=ge[:, t:t + 1])
                            v.drain()
                        v.tensor_scalar(junk[:, c:N], w_row[:, c:N], wt[:, t:t + 1], 0.0, ALU.is_gt, ALU.add, accum_out=gt[:, t:t + 1])
                        v.drain()
                        v.scalar_tensor_tensor(out=junk[:, c:c + P], in0=w_row[:, c:c + P], scalar=wt[:, t:t + 1], in1=before[:, :],
                                               op0=ALU.is_equal, op1=ALU.mult, accum_out=tie[:, t:t + 1])
                        v.drain()
                v.tensor_tensor(out=gt[:, :], in0=gt[:, :], in1=ge[:, :], op=ALU.add)
                v.drain()
                v.tensor_tensor(out=gt[:, :], in0=gt[:, :], in1=tie[:, :], op=ALU.add)
                v.drain()
                v.scalar_tensor_tensor(out=ws[:, :], in0=gt[:, :], scalar=float(TOPK), in1=wt[:, :], op0=ALU.is_lt, op1=ALU.mult)
                v.drain()

                with dve.Fori(0, U) as i:
                    rows = bass.ds(i * U, U)
                    dve.wait_ge(y_done, 3 * (i + 1))
                    v.tensor_tensor(out=Y[:, rows, :], in0=Y[:, rows, :], in1=b2[:, :].unsqueeze(1).to_broadcast([P, U, F]), op=ALU.add)
                    for u in range(U):
                        t = i * U + u
                        v.tensor_scalar(prod[:, u, :], row_of(X, t), MV[:, bass.ds(t, 1), 0:1].rearrange("p a b -> p (a b)"),
                                        rstd[:, bass.ds(t, 1)], ALU.subtract, ALU.mult)
                    v.drain()
                    v.tensor_tensor(out=X[:, rows, :], in0=X[:, rows, :], in1=prod[:, :, :], op=ALU.add)
                    v.drain()
                    for u in range(U):
                        t = i * U + u
                        v.scalar_tensor_tensor(out=row_of(X, t), in0=row_of(Y, t), scalar=ws[:, bass.ds(t, 1)], in1=row_of(X, t),
                                               op0=ALU.mult, op1=ALU.add)
                    v.drain().then_inc(out_ready, 1)

            @block.scalar
            def _(act):
                act.sem_inc(f_out, 2)
                act.wait_ge(stats_done, 1)
                a.activation(std[:, :], MV[:, :, 1], ACT.Sqrt, bias=eps[:, 0:1])
                a.drain().then_inc(std_done, 1)
                act.wait_ge(wt_psum, 1)
                a.activation(wtT[:, :], ps_o[0:T, 0, 0:P], ACT.Copy)
                a.drain().then_inc(wt_copied, 1)

                def copies(i):
                    for b, tiles in enumerate(BANKS):
                        act.wait_ge(t_ready, 3 * i + b + 1)
                        n = len(tiles)
                        a.activation(HT[:, :, tiles[0] * P:(tiles[0] + n) * P].rearrange("p q (u c) -> p u q c", c=P),
                                     ps_t[:, b, 0:n * KF * P].rearrange("p (u q c) -> p u q c", u=n, c=P), ACT.Copy).then_inc(ht_ready, 1)

                def hidden(i):
                    m = 0
                    for o in range(HB8):
                        for lo, n in HALVES:
                            act.wait_ge(f_done, I1 * i + m + 1)
                            a.activation(A[:, o, lo:lo + n], ps_f[:, m % 2, 0:n], ACT.Gelu_apprx_tanh, bias=b1[:, o:o + 1]).then_inc(f_out, 1)
                            m += 1

                def results(i):
                    for b, tiles in enumerate(BANKS):
                        act.wait_ge(o_done, 3 * i + b + 1)
                        n = len(tiles)
                        a.activation(Y[:, bass.ds(i * U + tiles[0], n), :].rearrange("p t f -> p (t f)"), ps_o[0:P, b, 0:n * F], ACT.Copy)
                        a.drain().then_inc(y_done, 1)

                copies(0)
                act.wait_ge(w_in, 16 * (2 + HB8))
                with act.Fori(1, U) as i:
                    hidden(i - 1)
                    copies(i)
                    results(i - 1)
                hidden(U - 1)
                results(U - 1)

            @block.tensor
            def _(pe):
                def hidden(i):
                    pe.wait_ge(ht_ready, 3 * (i + 1))
                    m = 0
                    for o in range(HB8):
                        for lo, n in HALVES:
                            pe.wait_ge(f_out, I1 * i + m + 1)
                            for q in range(KF):
                                last = t_.matmul(ps_f[:, m % 2, 0:n], w1[:, q, o * 128:(o + 1) * 128], HT[:, q, lo:lo + n],
                                                 start=(q == 0), stop=(q == KF - 1))
                            last.then_inc(f_done, 1)
                            m += 1

                def results(i, first):
                    pe.wait_ge(f_out, I1 * (i + 1) + 2)
                    for b, tiles in enumerate(BANKS):
                        if not first:
                            pe.wait_ge(y_done, 3 * (i - 1) + b + 1)
                        for s, u in enumerate(tiles):
                            for o in range(HB8):
                                last = t_.matmul(ps_o[0:P, b, s * F:(s + 1) * F], A[:, o, u * P:(u + 1) * P], w2[:, o, :],
                                                 start=(o == 0), stop=(o == HB8 - 1))
                        last.then_inc(o_done, 1)

                pe.wait_ge(wt_done, 1)
                t_.transpose(ps_o[0:T, 0, 0:P], wt[:, :], k.ident[0:P, 0:P]).then_inc(wt_psum, 1)
                transpose_batch(pe, t_, k, H, ps_t, h_ready, ht_ready, t_ready, 0, True)
                pe.wait_ge(w_in, 16 * (2 + HB8))
                pe.wait_ge(wt_copied, 1)
                hidden(0)
                transpose_batch(pe, t_, k, H, ps_t, h_ready, ht_ready, t_ready, 1, False)
                results(0, True)
                with pe.Fori(2, U) as i:
                    hidden(i - 1)
                    transpose_batch(pe, t_, k, H, ps_t, h_ready, ht_ready, t_ready, i, False)
                    results(i - 1, False)
                hidden(U - 1)
                results(U - 1, False)


def enter_branch(nc):
    for engine in (nc.sync, nc.gpsimd, nc.vector, nc.scalar, nc.tensor):
        engine.nop()


def program(nc, **args):
    k = Env()
    k.nc = nc
    (k.x, k.src, k.dst, k.L0_gnn_W, k.L0_gnn_att) = (args[n] for n in ("x", "src", "dst", "L0_gnn_W", "L0_gnn_att"))
    k.args = args
    k.out = args["out"]

    def dram(name, shape, dt):
        return nc.dram_tensor(name, shape, dt, kind="Internal").ap()

    k.z_dram = dram("z_dram", [HEADS, T, P, DH + 1], FP32)
    k.es_dram = dram("es_dram", [T, HEADS, P], FP32)
    k.ed_dram = dram("ed_dram", [T, HEADS, P], FP32)
    k.key_dram = dram("key_dram", [SROWS, SEG], FP32)
    k.rows_dram = dram("rows_dram", [2, HEADS, T, P], FP32)
    k.wt_dram = dram("wt_dram", [T, P], FP32)
    k.counts = dram("counts", [N, N], BF16)
    k.countsT = dram("countsT", [N, N], BF16)
    k.counts_low = dram("counts_low", [N, N], BF16)
    k.countsT_low = dram("countsT_low", [N, N], BF16)
    with scope(nc) as (sb, pb, sem):
        k.rows_in, k.win_in, k.more_in = sem("rows_in"), sem("win_in"), sem("more_in")
        k.ident = sb("ident", [128, 128], FP32)
        k.ident_bf = sb("ident_bf", [128, 128], BF16)
        k.ones = sb("ones", [128, 128], FP32)
        k.iota_row = sb("iota_row", [128, P], BF16)
        k.es = sb("es", [P, T, HEADS], FP32)
        k.ed = sb("ed", [P, T, HEADS], FP32)
        k.mx = sb("mx", [P, T, HEADS], FP32)
        k.base = sb("base_seg", [P, U], FP32)
        k.rounds = sb("rounds", [1, 1], I32)
        k.rowG = sb("rowG", [128, NG // U, 2 * U], BF16)
        k.colG = sb("colG", [128, NG // U, 2 * U], BF16)
        k.top = sb("es_top", [P, HEADS], FP32)
        k.es_mask = sb("es_mask", [P, T, HEADS], FP32)
        k.dst_exp = sb("dst_exp", [P, T, HEADS, 2], FP32)
        k.arena = sb("arena", [P, ARENA], BF16)
        setup_phase(k)
        edge_windows_phase(k)
        gat_project_phase(k)
        rounds = nc.values_load(k.rounds[0:1, 0:1], min_val=1, max_val=(SROWS * SEG) // WIN)
        count_phase(k)

        def convolutions(name, counts, countsT):
            hidden = k.pa[:, :, :].bitcast(FP32)
            conv_input_phase(k, name + "1i_", k.args["L1_gnn_W1"], None, k.pa)
            conv_step_phase(k, name + "1e_", counts, k.pa, "edges", out3=k.pb)
            conv_step_phase(k, name + "1n_", countsT, k.pb, "hidden", bias=k.args["L1_gnn_b1"], target=hidden)
            conv_input_phase(k, name + "2i_", k.args["L1_gnn_W2"], hidden, k.pb)
            conv_step_phase(k, name + "2e_", counts, k.pb, "edges", out3=k.pa)
            conv_step_phase(k, name + "2n_", countsT, k.pa, "last", bias=k.args["L1_gnn_b2"])

        k.X = sb("X", [P, T, F], FP32)
        with nc.If_cmp(rounds.val, 2, "IS_GE"):
            enter_branch(nc)
            clear_low_phase(k)
            with nc.Fori(1, rounds) as r:
                more_windows_phase(k, r)
                more_counts_phase(k)
            transpose_counts_phase(k, "th_", k.counts, k.countsT, True)
            transpose_counts_phase(k, "tl_", k.counts_low, k.countsT_low, False)
            with nc.sbuf_tensor("gat_sums", [P, HEADS, T, DH + 1], FP32) as acc:
                k.acc = acc
                gat_attend_phase(k, "two_", [k.counts, k.counts_low])
                gat_finish_phase(k)
        with nc.Else():
            enter_branch(nc)
            gat_separable_phase(k)
        nc.end_all_ifs()
        moe_phase(k)
        k.pa, k.pb = (k.arena[:, n * T * X3:(n + 1) * T * X3].rearrange("p (t c) -> p t c", t=T) for n in range(2))
        with nc.sbuf_tensor("LNX", [P, T, F], FP32) as k.LNX:
            with nc.If_cmp(rounds.val, 2, "IS_GE"):
                enter_branch(nc)
                convolutions("two", [k.counts, k.counts_low], [k.countsT, k.countsT_low])
            with nc.Else():
                enter_branch(nc)
                convolutions("one", [k.counts], [k.countsT])
            nc.end_all_ifs()
        ffn_phase(k)


_INS = ['x', 'src', 'dst', 'L0_gnn_W', 'L0_gnn_att', 'L0_ffn_sW1', 'L0_ffn_sb1', 'L0_ffn_sW2', 'L0_ffn_sb2', 'L0_ffn_sW3',
        'L0_ffn_sb3', 'L0_ffn_eW1', 'L0_ffn_eb1', 'L0_ffn_eW2', 'L0_ffn_eb2', 'L0_ffn_eW3', 'L0_ffn_eb3', 'L0_ffn_gW',
        'L0_ffn_gb', 'L1_gnn_W1', 'L1_gnn_b1', 'L1_gnn_W2', 'L1_gnn_b2', 'L1_gnn_a', 'L1_ffn_wr', 'L1_ffn_br', 'L1_ffn_w1',
        'L1_ffn_b1', 'L1_ffn_w2', 'L1_ffn_b2']


def kernel(**inputs):
    import numpy as _np
    import concourse.bacc as _bacc
    from concourse import mybir as _mybir
    from concourse.bass_utils import run_bass_kernel_spmd as _run

    nc = _bacc.Bacc("TRN2", target_bir_lowering=False, num_devices=1)
    arrays, args = {}, {}
    for name in _INS:
        a = _np.ascontiguousarray(inputs[name])
        arrays[f"in_{name}_dram"] = a
        args[name] = nc.dram_tensor(f"in_{name}_dram", a.shape, _mybir.dt.from_np(a.dtype), kind="ExternalInput").ap()
    args["out"] = nc.dram_tensor("out_0_dram", (3125, 256), _mybir.dt.float32, kind="ExternalOutput").ap()
    program(nc, **args)
    r = _run(nc, [arrays], core_ids=[0])
    return r.results[0]["out_0_dram"]
```

```python
import concourse.bass as bass
from concourse import mybir
from contextlib import ExitStack, contextmanager

FP32 = mybir.dt.float32
BF16 = mybir.dt.bfloat16
I32 = mybir.dt.int32
ALU = mybir.AluOpType
ACT = mybir.ActivationFunctionType
AXX = mybir.AxisListType.X

N = 3125
P = 125
T = N // P
U = 5
F = 256
KF = F // 128
HEADS = 4
DH = F // HEADS
E = 103125
ROW = E // P
G = U
NG = N // G
SEG = 32
WIN = 256
NSEG = WIN // SEG
SROWS = 3240
PAD_KEY = 16000000.0
EPS = 1e-5
BIG = 1e30
BANKS = [(0, 1), (2, 3), (4,)]
QB = U * P
X3 = 770
PART = [(0, 257), (258, 256), (514, 256)]
D1 = DH + 1
W3 = 3 * D1
ARENA = T * HEADS * 2 * W3
HIDDEN = 1024
WIDE = 30.0
MASK_SCALE = 2.0 ** 80


class Env:
    pass


@contextmanager
def scope(nc):
    with ExitStack() as ctx:
        sems = []

        def sb(name, shape, dt):
            return ctx.enter_context(nc.sbuf_tensor(name, shape, dt))

        def pb(name, shape, dt):
            return ctx.enter_context(nc.psum_tensor(name, shape, dt))

        def sem(name):
            sems.append(ctx.enter_context(nc.semaphore(name)))
            return sems[-1]

        yield sb, pb, sem
        if sems:
            with nc.Block() as block:
                @block.sync
                def _(sp):
                    for s in sems:
                        sp.sem_clear(s)


def batch_stats(v, X, st, mv, MV, i):
    for u in range(U):
        v.bn_stats(out=st[:, u, :], in_=X[:, bass.ds(i * U + u, 1), :].rearrange("p a f -> p (a f)"))
    v.drain()
    for u in range(U):
        v.bn_aggr(out=mv[:, u, :], in_=st[:, u, :])
    v.drain()
    v.tensor_copy(MV[:, bass.ds(i * U, U), :], mv[:, :, :])
    v.drain()


def layernorm_stats(nc, dve, v, X, st, mv, MV):
    with dve.Fori(0, U) as i:
        batch_stats(v, X, st, mv, MV, i)


def normalize_batch(v, X, H, MV, rstd, i, hready, t_ready, dve, first):
    for u in range(U):
        t = i * U + u
        if not first:
            dve.wait_ge(t_ready, 3 * (i - 1) + u // 2 + 1)
        v.tensor_scalar(H[:, u, :], X[:, bass.ds(t, 1), :].rearrange("p a f -> p (a f)"),
                        MV[:, bass.ds(t, 1), 0:1].rearrange("p a b -> p (a b)"),
                        rstd[:, bass.ds(t, 1)], ALU.subtract, ALU.mult).then_inc(hready, 1)


def setup_phase(k):
    nc = k.nc
    with scope(nc) as (sb, pb, sem):
        iota_int = sb("iota_int", [128, P], I32)
        with nc.Block() as block:
            @block.gpsimd
            def _(pool):
                g = nc.gpsimd
                g.memset(k.ident[:, :], 0.0)
                g.memset(k.ones[:, :], 1.0)
                g.iota(iota_int[:, :], pattern=[[1, P]], base=0, channel_multiplier=0)
                g.drain()
                g.affine_select(out=k.ident[:, :], in_=k.ident[:, :], compare_op=ALU.not_equal, fill=1.0,
                                base=0, pattern=[[-1, 128]], channel_multiplier=1)
                g.tensor_copy(k.iota_row[:, :], iota_int[:, :])
                g.drain()
                g.tensor_copy(k.ident_bf[:, :], k.ident[:, :])
                g.drain()


def copy_transposed(act, a, ps_t, HT, t_ready, product_ready, ht_ready):
    def batch(i, first):
        for b, tiles in enumerate(BANKS):
            act.wait_ge(t_ready, 3 * i + b + 1)
            if not first:
                act.wait_ge(product_ready, 3 * (i - 1) + b + 1)
            n = len(tiles)
            a.activation(HT[:, :, tiles[0] * P:(tiles[0] + n) * P].rearrange("p q (u c) -> p u q c", c=P),
                         ps_t[:, b, 0:n * KF * P].rearrange("p (u q c) -> p u q c", u=n, c=P), ACT.Copy).then_inc(ht_ready, 1)

    batch(0, True)
    with act.Fori(1, U) as i:
        batch(i, False)


def transpose_batch(pe, t_, k, H, ps_t, h_ready, ht_ready, t_ready, i, first):
    for b, tiles in enumerate(BANKS):
        if not first:
            pe.wait_ge(ht_ready, 3 * (i - 1) + b + 1)
        pe.wait_ge(h_ready, U * i + tiles[-1] + 1)
        for s, u in enumerate(tiles):
            for q in range(KF):
                last = t_.transpose(ps_t[:, b, (s * KF + q) * P:(s * KF + q + 1) * P],
                                    H[:, u, q * 128:(q + 1) * 128], k.ident[0:P, 0:P])
        last.then_inc(t_ready, 1)


def edges_and_projection_phase(k):
    nc = k.nc
    v, a, t_, g = nc.vector, nc.scalar, nc.tensor, nc.gpsimd
    NB = 2 * U
    with scope(nc) as (sb, pb, sem):
        X = k.arena[0:P, 2 * NB * ROW:2 * NB * ROW + 2 * T * F].bitcast(FP32).rearrange("p (t f) -> p t f", t=T)
        H = sb("h_batch", [P, U, F], FP32)
        HT = sb("hT_batch", [128, KF, QB], FP32)
        w_rows = sb("w_rows", [128, KF, F], FP32)
        wT = sb("wT", [128, KF, F], FP32)
        att_b = sb("att_b", [P, 2, HEADS, DH], FP32)
        st = sb("bn_st", [P, U, 6], FP32)
        mv = sb("bn_mv", [P, U, 2], FP32)
        MV = sb("bn_all", [P, T, 2], FP32)
        std = sb("std", [P, T], FP32)
        rstd = sb("rstd", [P, T], FP32)
        eps = sb("eps", [P, 1], FP32)
        z = sb("z_batch", [P, U, HEADS, DH + 1], FP32)
        prod = sb("prod", [P, U, 2, HEADS, DH], FP32)
        ered = sb("ered", [P, U, 2, HEADS], FP32)
        esT = sb("esT", [HEADS * T, 2, P], FP32)
        ends = sb("es_ends", [P, 2, HEADS], FP32)
        ends8 = sb("es_ends8", [2 * HEADS, 1], FP32)
        diag8 = sb("es_diag8", [2 * HEADS, 2 * HEADS], FP32)
        limits = sb("es_limits", [P, 2, HEADS], FP32)
        wide = sb("es_wide", [P, HEADS], FP32)
        wide1 = sb("es_wide1", [P, 1], FP32)
        ps_t = pb("ps_t", [128, 3, 512], FP32)
        ps_z = pb("ps_z", [128, 3, 512], FP32)
        ps_w = pb("ps_w", [128, KF, F], FP32)
        x_loaded, w_loaded, att_loaded = sem("x_loaded"), sem("w_loaded"), sem("att_loaded")
        wt_psum, wt_ready = sem("wt_psum"), sem("wt_ready")
        stats_done, std_done = sem("stats_done"), sem("std_done")
        h_ready, t_ready, ht_ready = sem("h_ready"), sem("t_ready"), sem("ht_ready")
        z_ready, z_free = sem("z_ready"), sem("z_free")
        zs_ready, zs_free = sem("zs_ready"), sem("zs_free")
        es_done, esT_psum, esT_done, es_stored = sem("es_done"), sem("esT_psum"), sem("esT_done"), sem("es_stored")
        ends_done, ends_psum, diag_done, limits_psum = sem("ends_done"), sem("ends_psum"), sem("diag_done"), sem("limits_psum")
        src_i = sb("src_i", [P, ROW], I32)
        dst_i = sb("dst_i", [P, ROW], I32)
        nxt_i = sb("nxt_i", [P, ROW], I32)
        key = sb("key", [P, ROW], FP32)
        down = sb("down", [P, ROW], FP32)
        pad = sb("pad", [1, SROWS * SEG - E], FP32)
        thr_i = sb("thr_i", [P, NB], I32)
        thr = sb("thr", [P, NB], FP32)
        low_i = sb("low_i", [P, U], I32)
        low = sb("low", [P, U], FP32)
        off_i = sb("off_i", [P, U, NSEG], I32)
        off = sb("off", [P, U, NSEG], FP32)
        head = sb("head", [P, 1], FP32)
        nd = sb("nd", [P, 1], FP32)
        diag = sb("diag", [P, P], FP32)
        heads = sb("heads", [P, P + 1], FP32)
        junk = sb("junk", [P, ROW], FP32)
        below = sb("below", [P, NB], FP32)
        row_f = sb("row_f", [P, NB], FP32)
        row_i = sb("row_i", [P, NB], I32)
        rows = k.arena[0:P, 0:2 * NB * ROW].bitcast(I32).rearrange("p (n c) -> p n c", n=NB)
        within = sb("within", [P, NB], FP32)
        edge = sb("edge", [P, NB], FP32)
        is_sorted = sb("is_sorted", [P, 1], FP32)
        base_i = sb("base_i", [P, U], I32)
        base = sb("base", [P, U], FP32)
        seg_f = sb("seg_f", [P, U, NSEG], FP32)
        seg_i = sb("seg_i", [P, U, NSEG], I32)
        span = sb("span", [P, U], FP32)
        span1 = sb("span1", [P, 1], FP32)
        spanT = sb("spanT", [1, P], FP32)
        win = sb("win", [P, U, WIN], FP32)
        rel = sb("rel", [P, U, WIN], FP32)
        rq_i = sb("rq_i", [P, U, WIN], I32)
        rq = sb("rq", [P, U, WIN], FP32)
        lo = sb("lo", [P, U, WIN], FP32)
        ps_h = pb("ps_h", [128, 512], FP32)
        ps_q, ps_l = ps_t, ps_z
        loaded, consts = sem("loaded"), sem("consts")
        heads_in, heads_psum, row_ready = sem("heads_in"), sem("heads_psum"), sem("row_ready")
        key_ready, key_stored = sem("key_ready"), sem("key_stored")
        rows_in, win_in = k.rows_in, k.win_in
        seg_ready, cut_ready, cut_psum, span_psum = (
            sem("seg_ready"), sem("cut_ready"), sem("cut_psum"), sem("span_psum"))
        with nc.Block() as block:
            @block.sync
            def _(sp):
                sp.dma_start(dst_i[:, :], k.dst.rearrange("(p c) -> p c", p=P)).then_inc(loaded, 16)
                sp.dma_start(src_i[:, :], k.src.rearrange("(p c) -> p c", p=P)).then_inc(loaded, 16)
                sp.dma_start(nxt_i[0:P - 1, :], k.dst[1:1 + (P - 1) * ROW].rearrange("(p c) -> p c", c=ROW)).then_inc(loaded, 16)
                sp.dma_start(nxt_i[P - 1:P, 0:ROW - 1], k.dst[E - ROW + 1:E].rearrange("(p c) -> p c", p=1)).then_inc(loaded, 16)
                sp.dma_start(nxt_i[P - 1:P, ROW - 1:ROW], k.dst[E - 1:E].rearrange("(p c) -> p c", p=1)).then_inc(loaded, 16)
                sp.dma_start(X[:, :, :], k.x.rearrange("(t p) f -> p t f", p=P)).then_inc(x_loaded, 16)
                sp.dma_start(w_rows[:, :, :],
                             k.L0_gnn_W.rearrange("h o i -> (h o) i").rearrange("(q r) i -> r q i", r=128)).then_inc(w_loaded, 16)
                for j in range(2):
                    sp.dma_start(att_b[:, j, :, :],
                                 k.L0_gnn_att[:, j * DH:(j + 1) * DH].unsqueeze(0).to_broadcast([P, HEADS, DH])).then_inc(att_loaded, 16)
                sp.wait_ge(key_ready, 1)
                sp.wait_ge(consts, 1)
                flat = k.key_dram.rearrange("r c -> (r c)")
                sp.dma_start(flat[0:E].rearrange("(p c) -> p c", p=P), key[:, :]).then_inc(key_stored, 16)
                sp.dma_start(flat[E:SROWS * SEG].rearrange("(p c) -> p c", p=1), pad[:, :]).then_inc(key_stored, 16)
                with sp.Fori(0, U) as i:
                    sp.wait_ge(zs_ready, i + 1)
                    for u in range(U):
                        sp.dma_start(k.z_dram[:, bass.ds(i * U + u, 1), :, :].rearrange("h a p c -> p (a h) c"),
                                     z[:, u, :, :]).then_inc(zs_free, 16)
                sp.wait_ge(zs_free, 16 * (T + U))
                sp.wait_ge(esT_done, 1)
                for j, rows in enumerate((k.es_dram, k.ed_dram)):
                    sp.dma_start(rows.rearrange("t h p -> (t h) p"), esT[:, j, :]).then_inc(es_stored, 16)
                sp.wait_ge(es_stored, 32)
                sp.wait_ge(key_stored, 32)

            @block.gpsimd
            def _(pool):
                g.iota(thr_i[:, 0:U], pattern=[[G * P, U]], base=0, channel_multiplier=G)
                g.iota(thr_i[:, U:NB], pattern=[[G * P, U]], base=G, channel_multiplier=G)
                g.iota(low_i[:, :], pattern=[[P, U]], base=0, channel_multiplier=1)
                g.iota(off_i[:, :, :], pattern=[[0, U], [1, NSEG]], base=0, channel_multiplier=0)
                g.memset(pad[:, :], PAD_KEY)
                g.drain()
                g.tensor_copy(thr[:, :], thr_i[:, :])
                g.tensor_copy(low[:, :], low_i[:, :])
                g.tensor_copy(off[:, :, :], off_i[:, :, :])
                g.drain().then_inc(consts, 1)
                pool.wait_ge(row_ready, 1)
                for j in range(NB):
                    g.indirect_dma_start(out=rows[:, j, :], out_offset=None, in_=k.dst.rearrange("(p c) -> p c", p=P),
                                         in_offset=bass.IndirectOffsetOnAxis(ap=row_i[:, j:j + 1], axis=0)).then_inc(rows_in, 16)
                pool.wait_ge(seg_ready, 1)
                pool.wait_ge(key_stored, 32)
                for j in range(U):
                    for s in range(NSEG):
                        g.indirect_dma_start(out=win[:, j, s * SEG:(s + 1) * SEG], out_offset=None, in_=k.key_dram,
                                             in_offset=bass.IndirectOffsetOnAxis(ap=seg_i[:, j, s:s + 1], axis=0)).then_inc(win_in, 16)

            @block.vector
            def _(dve):
                dve.wait_ge(loaded, 80)
                v.tensor_copy(head[:, :], dst_i[:, 0:1])
                v.scalar_tensor_tensor(out=key[:, :], in0=dst_i[:, :], scalar=float(N), in1=src_i[:, :], op0=ALU.mult, op1=ALU.add)
                v.tensor_tensor(out=down[:, :], in0=nxt_i[:, :], in1=dst_i[:, :], op=ALU.is_lt)
                v.drain()
                v.tensor_reduce(out=nd[:, :], in_=down[:, :], axis=AXX, op=ALU.add)
                v.tensor_scalar(diag[:, :], k.ident[0:P, 0:P], head[:, 0:1], None, ALU.mult)
                v.drain().then_inc(heads_in, 1)
                v.nop().then_inc(key_ready, 1)
                dve.wait_ge(heads_psum, 1)
                v.tensor_copy(heads[:, :], ps_h[0:P, 0:P + 1])
                v.drain()
                v.tensor_scalar(is_sorted[:, :], heads[:, P:P + 1], 0.0, None, ALU.is_equal)
                dve.wait_ge(consts, 1)
                for j in range(NB):
                    v.tensor_scalar(junk[:, 0:P], heads[:, 0:P], thr[:, j:j + 1], 0.0,
                                    ALU.is_lt, ALU.add, accum_out=below[:, j:j + 1])
                    v.drain()
                v.tensor_scalar(row_f[:, :], below[:, :], -1.0, 0.0, ALU.add, ALU.max)
                v.drain()
                v.tensor_copy(row_i[:, :], row_f[:, :])
                v.drain().then_inc(row_ready, 1)

                v.memset(eps[:, :], EPS)
                v.memset(z[:, :, :, :], 1.0)
                dve.sem_inc(z_free, 3)
                dve.wait_ge(x_loaded, 16)
                layernorm_stats(nc, dve, v, X, st, mv, MV)
                v.nop().then_inc(stats_done, 1)

                dve.wait_ge(rows_in, 16 * NB)
                for j in range(NB):
                    v.tensor_scalar(junk[:, :], rows[:, j, :], thr[:, j:j + 1], 0.0, ALU.is_lt, ALU.add,
                                    accum_out=within[:, j:j + 1])
                    v.drain()
                v.scalar_tensor_tensor(out=edge[:, :], in0=row_f[:, :], scalar=float(ROW), in1=within[:, :], op0=ALU.mult, op1=ALU.add)
                v.drain()
                v.tensor_scalar(edge[:, 0:U], edge[:, 0:U], is_sorted[:, 0:1], None, ALU.mult)
                v.tensor_scalar(edge[:, U:NB], edge[:, U:NB], -float(E), is_sorted[:, 0:1], ALU.add, ALU.mult)
                v.drain()
                v.tensor_scalar(edge[:, U:NB], edge[:, U:NB], float(E), None, ALU.add)
                v.tensor_scalar(base_i[:, :], edge[:, 0:U], 1.0 / SEG, 0.5 / SEG - 0.5, ALU.mult, ALU.add)
                v.drain()
                v.tensor_copy(base[:, :], base_i[:, :])
                v.drain()
                v.tensor_copy(k.base[:, :], base[:, :])
                v.tensor_tensor(out=seg_f[:, :, :], in0=off[:, :, :], in1=base[:, :].unsqueeze(2).to_broadcast([P, U, NSEG]), op=ALU.add)
                v.scalar_tensor_tensor(out=span[:, :], in0=base[:, :], scalar=-float(SEG), in1=edge[:, U:NB], op0=ALU.mult, op1=ALU.add)
                v.drain()
                v.tensor_copy(seg_i[:, :, :], seg_f[:, :, :])
                v.tensor_reduce(out=span1[:, :], in_=span[:, :], axis=AXX, op=ALU.max)
                v.drain().then_inc(seg_ready, 1)
                dve.wait_ge(span_psum, 1)
                v.tensor_copy(spanT[:, :], ps_h[0:1, 0:P])
                v.drain()
                v.tensor_reduce(out=span1[0:1, :], in_=spanT[:, :], axis=AXX, op=ALU.max)
                v.drain()
                v.tensor_scalar(k.rounds[0:1, :], span1[0:1, :], 1.0 / WIN, 0.5 - 0.5 / WIN, ALU.mult, ALU.add)

                dve.wait_ge(std_done, 1)
                v.reciprocal(rstd[:, :], std[:, :])
                v.drain()
                dve.wait_ge(att_loaded, 32)

                def logits(i):
                    for b, tiles in enumerate(BANKS):
                        dve.wait_ge(z_ready, 3 * i + b + 1)
                        if b == 0:
                            dve.wait_ge(zs_free, 16 * U * (i + 1))
                        for s, u in enumerate(tiles):
                            v.tensor_copy(z[:, u, :, 0:DH],
                                          ps_z[0:P, b, s * F:(s + 1) * F].rearrange("p (h o) -> p h o", h=HEADS))
                        v.drain().then_inc(z_free, 1)
                    v.nop().then_inc(zs_ready, 1)
                    for u in range(U):
                        for j in range(2):
                            v.tensor_tensor(out=prod[:, u, j, :, :], in0=z[:, u, :, 0:DH], in1=att_b[:, j, :, :], op=ALU.mult)
                    v.drain()
                    v.tensor_reduce(out=ered[:, :, :, :].rearrange("p u j h -> p (u j h)"),
                                    in_=prod[:, :, :, :, :].rearrange("p u j h o -> p (u j h) o"), axis=AXX, op=ALU.add)
                    v.drain()
                    v.tensor_copy(k.es[:, bass.ds(i * U, U), :], ered[:, :, 0, :])
                    v.tensor_copy(k.ed[:, bass.ds(i * U, U), :], ered[:, :, 1, :])
                    v.drain()

                normalize_batch(v, X, H, MV, rstd, 0, h_ready, t_ready, dve, True)
                with dve.Fori(1, U) as i:
                    normalize_batch(v, X, H, MV, rstd, i, h_ready, t_ready, dve, False)
                    logits(i - 1)
                logits(U - 1)
                v.nop().then_inc(es_done, 1)
                v.tensor_reduce(out=ends[:, 0, :], in_=k.es[:, :, :].rearrange("p t h -> p h t"), axis=AXX, op=ALU.max)
                v.tensor_reduce(out=ends[:, 1, :], in_=k.es[:, :, :].rearrange("p t h -> p h t"), axis=AXX, op=ALU.min)
                v.drain()
                v.tensor_scalar(ends[:, 1, :], ends[:, 1, :], -1.0, None, ALU.mult)
                v.drain().then_inc(ends_done, 1)
                dve.wait_ge(ends_psum, 1)
                v.tensor_reduce(out=ends8[:, :], in_=ps_w[0:2 * HEADS, 0, 0:P], axis=AXX, op=ALU.max)
                v.drain()
                v.tensor_scalar(diag8[:, :], k.ident[0:2 * HEADS, 0:2 * HEADS], ends8[:, 0:1], None, ALU.mult)
                v.drain().then_inc(diag_done, 1)
                dve.wait_ge(limits_psum, 1)
                v.tensor_copy(limits[:, :, :].rearrange("p j h -> p (j h)"), ps_w[0:P, 0, 0:2 * HEADS])
                v.drain()
                v.tensor_copy(k.top[:, :], limits[:, 0, :])
                v.tensor_tensor(out=wide[:, :], in0=limits[:, 0, :], in1=limits[:, 1, :], op=ALU.add)
                v.drain()
                v.tensor_reduce(out=wide1[:, :], in_=wide[:, :], axis=AXX, op=ALU.max)
                v.drain()
                v.tensor_scalar(wide1[:, :], wide1[:, :], WIDE, 2.0, ALU.is_gt, ALU.mult)
                v.drain()
                v.tensor_tensor(out=k.rounds[0:1, :], in0=k.rounds[0:1, :], in1=wide1[0:1, :], op=ALU.max)
                v.drain()

                dve.wait_ge(win_in, 16 * U * NSEG)
                cut_keys(nc, v, low, win, rel, rq_i, rq, lo)
                v.nop().then_inc(cut_ready, 1)
                dve.wait_ge(cut_psum, 1)
                copy_cuts(v, k, ps_q, ps_l)

            @block.scalar
            def _(act):
                act.sem_inc(zs_free, 16 * U)
                act.wait_ge(wt_psum, 1)
                a.activation(wT[:, :, :], ps_w[:, :, :], ACT.Copy)
                a.drain().then_inc(wt_ready, 1)
                act.wait_ge(stats_done, 1)
                a.activation(std[:, :], MV[:, :, 1], ACT.Sqrt, bias=eps[:, 0:1])
                a.drain().then_inc(std_done, 1)
                copy_transposed(act, a, ps_t, HT, t_ready, z_ready, ht_ready)
                act.wait_ge(esT_psum, 1)
                a.activation(esT[:, :, :].rearrange("r j p -> r (j p)"), ps_t[0:HEADS * T, 0, 0:2 * P], ACT.Copy)
                a.drain().then_inc(esT_done, 1)

            @block.tensor
            def _(pe):
                pe.wait_ge(heads_in, 1)
                t_.matmul(ps_h[0:P, 0:P], k.ones[0:P, 0:P], diag[:, :], start=True, stop=True)
                t_.matmul(ps_h[0:P, P:P + 1], k.ones[0:P, 0:P], nd[:, :], start=True, stop=True)
                t_.drain().then_inc(heads_psum, 1)
                pe.wait_ge(w_loaded, 16)
                for q in range(KF):
                    for r in range(KF):
                        t_.transpose(ps_w[:, q, r * 128:(r + 1) * 128], w_rows[:, r, q * 128:(q + 1) * 128], k.ident[:, :])
                t_.drain().then_inc(wt_psum, 1)
                pe.wait_ge(wt_ready, 1)

                pe.wait_ge(seg_ready, 1)
                t_.transpose(ps_h[0:1, 0:P], span1[:, :], k.ident[0:P, 0:P])
                t_.drain().then_inc(span_psum, 1)

                def products(i):
                    for b, tiles in enumerate(BANKS):
                        pe.wait_ge(ht_ready, 3 * i + b + 1)
                        pe.wait_ge(z_free, 3 * i + b + 1)
                        for s, u in enumerate(tiles):
                            for q in range(KF):
                                last = t_.matmul(ps_z[0:P, b, s * F:(s + 1) * F], HT[:, q, u * P:(u + 1) * P], wT[:, q, :],
                                                 start=(q == 0), stop=(q == KF - 1))
                        last.then_inc(z_ready, 1)

                transpose_batch(pe, t_, k, H, ps_t, h_ready, ht_ready, t_ready, 0, True)
                with pe.Fori(1, U) as i:
                    transpose_batch(pe, t_, k, H, ps_t, h_ready, ht_ready, t_ready, i, False)
                    products(i - 1)
                products(U - 1)
                pe.wait_ge(es_done, 1)
                t_.transpose(ps_t[0:HEADS * T, 0, 0:P], k.es[:, :, :].rearrange("p t h -> p (t h)"), k.ident[0:P, 0:P])
                t_.transpose(ps_t[0:HEADS * T, 0, P:2 * P], k.ed[:, :, :].rearrange("p t h -> p (t h)"), k.ident[0:P, 0:P]).then_inc(esT_psum, 1)
                pe.wait_ge(ends_done, 1)
                t_.transpose(ps_w[0:2 * HEADS, 0, 0:P], ends[:, :, :].rearrange("p j h -> p (j h)"), k.ident[0:P, 0:P])
                t_.drain().then_inc(ends_psum, 1)
                pe.wait_ge(diag_done, 1)
                t_.matmul(ps_w[0:P, 0, 0:2 * HEADS], k.ones[0:2 * HEADS, 0:P], diag8[:, :], start=True, stop=True)
                t_.drain().then_inc(limits_psum, 1)
                pe.wait_ge(cut_ready, 1)
                pe.wait_ge(esT_done, 1)
                transpose_cuts(t_, k, rq, lo, ps_q, ps_l)
                t_.drain().then_inc(cut_psum, 1)


def cut_keys(nc, v, low, win, rel, rq_i, rq, lo):
    for j in range(U):
        v.scalar_tensor_tensor(out=rel[:, j, :], in0=low[:, j:j + 1].to_broadcast([P, WIN]), scalar=-float(G * N),
                               in1=win[:, j, :], op0=ALU.mult, op1=ALU.add)
    v.drain()
    v.tensor_scalar(rq_i[:, :, :], rel[:, :, :], 1.0 / P, 0.5 / P - 0.5, ALU.mult, ALU.add)
    v.drain()
    v.tensor_copy(rq[:, :, :], rq_i[:, :, :])
    v.drain()
    v.scalar_tensor_tensor(out=lo[:, :, :], in0=rq[:, :, :], scalar=-float(P), in1=rel[:, :, :], op0=ALU.mult, op1=ALU.add)
    v.drain()
    v.tensor_scalar(rq[:, :, :], rq[:, :, :], -1.0, float(P), ALU.max, ALU.min)
    v.drain()


def transpose_cuts(t_, k, rq, lo, ps_q, ps_l):
    for j in range(U):
        for c in range(2):
            n = 2 * j + c
            for cut, ps in ((rq, ps_q), (lo, ps_l)):
                t_.transpose(ps[:, n // 4, (n % 4) * P:(n % 4 + 1) * P], cut[:, j, c * 128:(c + 1) * 128], k.ident[0:P, 0:P])


def copy_cuts(v, k, ps_q, ps_l):
    for cut, ps in ((k.rowG, ps_q), (k.colG, ps_l)):
        for j in range(U):
            for c in range(2):
                n = 2 * j + c
                v.tensor_copy(cut[:, j * T:(j + 1) * T, c * U:(c + 1) * U],
                              ps[:, n // 4, (n % 4) * P:(n % 4 + 1) * P].rearrange("p (b g) -> p b g", g=U))
    v.drain()


HB = [(0, 1, 2), (3, 4)]
PAIR = [0, 1, 2, 0, 1]
BACK = [2, 2, 5, 3, 3]
TQ = 4
TR_AFTER = [(0, 1), (2,), (3, 4), (5,), (6,)]
NTB = (T + TQ - 1) // TQ


def zparts(k):
    return k.arena[:, :].rearrange("p (t h e c d) -> p t h e c d", t=T, h=HEADS, e=2, c=3)


def count_phase(k):
    nc = k.nc
    v, a, t_ = nc.vector, nc.scalar, nc.tensor
    with scope(nc) as (sb, pb, sem):
        M = 2 * U
        iota_rep = sb("iota_rep", [128, P, M], BF16)
        row_hot = sb("row_hot", [128, U, P, M], BF16)
        col_hot = sb("col_hot", [128, U, P, M], BF16)
        blk = sb("blk", [P, 2, T, QB], BF16)
        tr = sb("tr", [P, 2, N], BF16)
        u_dst = sb("u_dst", [P, T, HEADS], FP32)
        m_dst = sb("m_dst", [P, T, HEADS], FP32)
        src_exp = sb("src_exp", [P, T, HEADS, 2], FP32)
        z = sb("z_tile_in", [P, HEADS, D1], FP32)
        ex = sb("src_exp_now", [P, HEADS, 2], FP32)
        full = sb("z_full", [P, HEADS, 2, D1], FP32)
        rest = sb("z_rest", [P, HEADS, 2, D1], FP32)
        ps = pb("ps_hist", [128, 3, 2, 512], FP32)
        ps_tr = pb("ps_tr", [128, 2, 512], FP32)
        hot_done, hist_done, blk_done = sem("hot_done"), sem("hist_done"), sem("blk_done")
        tr_psum, tr_done = sem("tr_psum"), sem("tr_done")
        blk_stored, tr_stored = sem("blk_stored"), sem("tr_stored")
        terms_done, exps_done, z_in, z_read = sem("terms_done"), sem("exps_done"), sem("z_in"), sem("z_read")
        with nc.Block() as block:
            @block.vector
            def _(dve):
                v.tensor_copy(iota_rep[:, :, :], k.iota_row[:, :].unsqueeze(2).to_broadcast([128, P, M]))
                v.drain()

                top_b = k.top[:, :].unsqueeze(1).to_broadcast([P, T, HEADS])
                v.tensor_tensor(out=src_exp[:, :, :, 0], in0=k.es[:, :, :], in1=top_b, op=ALU.subtract)
                v.tensor_tensor(out=u_dst[:, :, :], in0=k.ed[:, :, :], in1=top_b, op=ALU.add)
                v.tensor_scalar(k.es_mask[:, :, :], k.es[:, :, :], MASK_SCALE, None, ALU.mult)
                v.drain()
                v.tensor_scalar(src_exp[:, :, :, 1], src_exp[:, :, :, 0], 0.01, None, ALU.mult)
                v.tensor_scalar(k.dst_exp[:, :, :, 1], u_dst[:, :, :], 0.01, None, ALU.mult)
                v.drain()
                v.tensor_tensor(out=m_dst[:, :, :], in0=u_dst[:, :, :], in1=k.dst_exp[:, :, :, 1], op=ALU.max)
                v.drain()
                v.tensor_tensor(out=k.dst_exp[:, :, :, 0], in0=u_dst[:, :, :], in1=m_dst[:, :, :], op=ALU.subtract)
                v.tensor_tensor(out=k.dst_exp[:, :, :, 1], in0=k.dst_exp[:, :, :, 1], in1=m_dst[:, :, :], op=ALU.subtract)
                v.drain().then_inc(terms_done, 1)

                def hots(i, first):
                    for u in range(U):
                        if not first:
                            dve.wait_ge(hist_done, U * (i - 1) + u + 1)
                        for cut, hot in ((k.rowG, row_hot), (k.colG, col_hot)):
                            v.tensor_tensor(out=hot[:, u, :, :], in0=iota_rep[:, :, :],
                                            in1=cut[:, bass.ds(i * U + u, 1), :].to_broadcast([128, P, M]),
                                            op=ALU.is_equal).then_inc(hot_done, 1)

                hots(0, True)
                with dve.Fori(1, T) as i:
                    hots(i, False)

            @block.gpsimd
            def _(pool):
                g = nc.gpsimd
                pool.wait_ge(exps_done, 1)
                with pool.Fori(0, T) as t:
                    g.tensor_copy(ex[:, :, :], src_exp[:, bass.ds(t, 1), :, :].rearrange("p a h e -> p (a h) e"))
                    g.drain()
                    pool.wait_ge(z_in, 16 * (t + 1))
                    part = [zparts(k)[:, bass.ds(t, 1), :, :, c, :].rearrange("p a h e c -> p (a h) e c") for c in range(3)]
                    for e in range(2):
                        factor = ex[:, :, e:e + 1].to_broadcast([P, HEADS, D1])
                        g.tensor_tensor(out=full[:, :, e, :], in0=z[:, :, :], in1=factor, op=ALU.mult)
                        g.tensor_tensor(out=part[0][:, :, e, :], in0=z[:, :, :], in1=factor, op=ALU.mult)
                    g.drain().then_inc(z_read, 1)
                    g.tensor_tensor(out=rest[:, :, :, :], in0=full[:, :, :, :], in1=part[0], op=ALU.subtract)
                    g.tensor_tensor(out=part[1], in0=full[:, :, :, :], in1=part[0], op=ALU.subtract)
                    g.drain()
                    g.tensor_tensor(out=part[2], in0=rest[:, :, :, :], in1=part[1], op=ALU.subtract)
                    g.drain()

            @block.scalar
            def _(act):
                act.sem_inc(tr_done, 2)
                act.sem_inc(blk_done, U)
                act.wait_ge(terms_done, 1)
                a.activation(src_exp[:, :, :, :], src_exp[:, :, :, :], ACT.Exp)
                a.activation(k.dst_exp[:, :, :, :], k.dst_exp[:, :, :, :], ACT.Exp)
                a.drain().then_inc(exps_done, 1)

                def hist_out(i, u):
                    act.wait_ge(hist_done, U * i + u + 1)
                    for b, groups in enumerate(HB):
                        n = len(groups) * G
                        last = a.activation(
                            blk[:, bass.ds((i // U) % 2, 1), :,
                                bass.ds((i % U) * P + u * G * U + groups[0] * G, n)].rearrange("p a t d -> p (a t) d"),
                            ps[0:P, PAIR[u], b, 0:n * T].rearrange("p (d t) -> p t d", t=T), ACT.Copy)
                    last.then_inc(blk_done, 1)

                def tr_out(i, banks):
                    for r in banks:
                        n = min(TQ, T - r * TQ)
                        act.wait_ge(tr_psum, NTB * i + r + 1)
                        a.activation(tr[:, bass.ds(i % 2, 1), r * TQ * P:(r * TQ + n) * P].rearrange("p a c -> p (a c)"),
                                     ps_tr[0:P, r % 2, 0:n * P], ACT.Copy).then_inc(tr_done, 1)

                act.wait_ge(blk_stored, 16)
                for u in range(U):
                    hist_out(0, u)
                with act.Fori(1, T) as i:
                    act.wait_ge(blk_stored, 16 * (i // U + 1))
                    act.wait_ge(tr_stored, 16 * i)
                    for u in range(U):
                        hist_out(i, u)
                        tr_out(i - 1, TR_AFTER[u])
                act.wait_ge(tr_stored, 16 * T)
                tr_out(T - 1, range(NTB))

            @block.tensor
            def _(pe):
                def histogram(i, u):
                    pe.wait_ge(hot_done, 2 * (U * i + u + 1))
                    pe.wait_ge(blk_done, U * i + u + 1 - BACK[u] + U)
                    for b, groups in enumerate(HB):
                        for s, gg in enumerate(groups):
                            for c in range(2):
                                last = t_.matmul(ps[0:P, PAIR[u], b, s * P:(s + 1) * P],
                                                 col_hot[:, u, :, c * U + gg], row_hot[:, u, :, c * U + gg],
                                                 start=(c == 0), stop=(c == 1))
                    last.then_inc(hist_done, 1)

                def transposes(i, banks):
                    for r in banks:
                        pe.wait_ge(tr_done, NTB * i + r + 1 + (1 if r == 0 else 0))
                        for s in range(min(TQ, T - r * TQ)):
                            last = t_.matmul(ps_tr[0:P, r % 2, s * P:(s + 1) * P],
                                             blk[:, bass.ds((i // U) % 2, 1), r * TQ + s, bass.ds((i % U) * P, P)].rearrange("p a d -> p (a d)"),
                                             k.ident_bf[0:P, 0:P], start=True, stop=True)
                        last.then_inc(tr_psum, 1)

                for u in range(U):
                    histogram(0, u)
                with pe.Fori(1, T) as i:
                    for u in range(U):
                        histogram(i, u)
                        if u == 0:
                            pe.wait_ge(blk_done, U * i + U)
                        transposes(i - 1, TR_AFTER[u])
                pe.wait_ge(blk_done, U * T + U)
                transposes(T - 1, range(NTB))

            @block.sync
            def _(sp):
                sp.sem_inc(blk_stored, 32)
                sp.sem_inc(tr_stored, 32)
                sp.sem_inc(z_read, 1)
                with sp.Fori(0, U) as j:
                    with sp.Fori(0, U) as w:
                        i = j * U + w
                        sp.wait_ge(z_read, i + 1)
                        sp.dma_start(z[:, :, :],
                                     k.z_dram[:, bass.ds(i, 1), :, :].rearrange("h a p c -> p (a h) c")).then_inc(z_in, 16)
                        sp.wait_ge(tr_done, NTB * (i + 1) + 2)
                        sp.wait_ge(tr_stored, 16 * i + 32)
                        sp.dma_start(k.countsT.rearrange("(t p) s -> t p s", p=P)[bass.ds(i, 1), :, :].rearrange("a p s -> (a p) s"),
                                     tr[:, bass.ds(i % 2, 1), :].rearrange("p a s -> p (a s)")).then_inc(tr_stored, 16)
                    sp.wait_ge(blk_stored, 16 * j + 32)
                    sp.dma_start(k.counts[:, bass.ds(j * QB, QB)].rearrange("(t p) d -> p t d", p=P),
                                 blk[:, bass.ds(j % 2, 1), :, :].rearrange("p a t d -> p (a t) d")).then_inc(blk_stored, 16)
                sp.wait_ge(blk_stored, 16 * U + 32)
                sp.wait_ge(tr_stored, 16 * T + 32)


def more_windows_phase(k, r):
    nc = k.nc
    v, t_, g = nc.vector, nc.tensor, nc.gpsimd
    with scope(nc) as (sb, pb, sem):
        low_i = sb("w_low_i", [P, U], I32)
        low = sb("w_low", [P, U], FP32)
        off_i = sb("w_off_i", [P, U, NSEG], I32)
        off = sb("w_off", [P, U, NSEG], FP32)
        seg_f = sb("w_seg_f", [P, U, NSEG], FP32)
        seg_i = sb("w_seg_i", [P, U, NSEG], I32)
        win = sb("w_win", [P, U, WIN], FP32)
        rel = sb("w_rel", [P, U, WIN], FP32)
        rq_i = sb("w_rq_i", [P, U, WIN], I32)
        rq = sb("w_rq", [P, U, WIN], FP32)
        lo = sb("w_lo", [P, U, WIN], FP32)
        ps_q = pb("w_ps_q", [128, 3, 512], FP32)
        ps_l = pb("w_ps_l", [128, 3, 512], FP32)
        consts, seg_ready, cut_ready, cut_psum = sem("w_consts"), sem("w_seg"), sem("w_cut"), sem("w_cut_psum")
        with nc.Block() as block:
            @block.gpsimd
            def _(pool):
                g.iota(low_i[:, :], pattern=[[P, U]], base=0, channel_multiplier=1)
                g.iota(off_i[:, :, :], pattern=[[0, U], [1, NSEG]], base=0, channel_multiplier=0)
                g.drain()
                g.tensor_copy(low[:, :], low_i[:, :])
                g.tensor_copy(off[:, :, :], off_i[:, :, :])
                g.drain().then_inc(consts, 1)
                pool.wait_ge(seg_ready, 1)
                for j in range(U):
                    for s in range(NSEG):
                        g.indirect_dma_start(out=win[:, j, s * SEG:(s + 1) * SEG], out_offset=None, in_=k.key_dram,
                                             in_offset=bass.IndirectOffsetOnAxis(ap=seg_i[:, j, s:s + 1], axis=0)).then_inc(k.more_in, 16)

            @block.vector
            def _(dve):
                dve.wait_ge(consts, 1)
                v.tensor_scalar(k.base[:, :], k.base[:, :], float(NSEG), None, ALU.add)
                v.drain()
                v.tensor_tensor(out=seg_f[:, :, :], in0=off[:, :, :], in1=k.base[:, :].unsqueeze(2).to_broadcast([P, U, NSEG]), op=ALU.add)
                v.drain()
                v.tensor_scalar(seg_i[:, :, :], seg_f[:, :, :], float(SROWS - 1), None, ALU.min)
                v.drain().then_inc(seg_ready, 1)
                dve.wait_ge(k.more_in, 16 * U * NSEG * r)
                cut_keys(nc, v, low, win, rel, rq_i, rq, lo)
                v.nop().then_inc(cut_ready, 1)
                dve.wait_ge(cut_psum, 1)
                copy_cuts(v, k, ps_q, ps_l)

            @block.tensor
            def _(pe):
                pe.wait_ge(cut_ready, 1)
                transpose_cuts(t_, k, rq, lo, ps_q, ps_l)
                t_.drain().then_inc(cut_psum, 1)


def clear_low_phase(k):
    nc = k.nc
    with scope(nc) as (sb, pb, sem):
        zero = sb("zero_rows", [P, N], BF16)
        zero_set, cleared = sem("zero_set"), sem("cleared")
        with nc.Block() as block:
            @block.vector
            def _(dve):
                nc.vector.memset(zero[:, :], 0.0)
                nc.vector.drain().then_inc(zero_set, 1)

            @block.sync
            def _(sp):
                sp.wait_ge(zero_set, 1)
                with sp.Fori(0, T) as t:
                    sp.dma_start(k.counts_low[bass.ds(t * P, P), :], zero[:, :]).then_inc(cleared, 16)
                sp.wait_ge(cleared, 16 * T)


def more_counts_phase(k):
    nc = k.nc
    v, t_ = nc.vector, nc.tensor
    M = 2 * U
    with scope(nc) as (sb, pb, sem):
        iota_rep = sb("m_iota", [128, P, M], BF16)
        row_hot = sb("m_row_hot", [128, P, M], BF16)
        col_hot = sb("m_col_hot", [128, P, M], BF16)
        high = sb("m_high", [P, T, P], BF16)
        low = sb("m_low", [P, T, P], BF16)
        acc = sb("m_acc", [P, T, P], FP32)
        ps = pb("m_ps", [128, 2, 512], FP32)
        in_done, hot_done, hist_done, sum_done, stored = sem("m_in"), sem("m_hot"), sem("m_hist"), sem("m_sum"), sem("m_stored")

        def tile(counts, i):
            return counts.rearrange("(t p) d -> p t d", p=P)[:, :, bass.ds(i * P, P)]

        with nc.Block() as block:
            @block.sync
            def _(sp):
                sp.sem_inc(stored, 32)
                with sp.Fori(0, T) as i:
                    sp.wait_ge(stored, 32 * (i + 1))
                    sp.dma_start(high[:, :, :], tile(k.counts, i)).then_inc(in_done, 16)
                    sp.dma_start(low[:, :, :], tile(k.counts_low, i)).then_inc(in_done, 16)
                    sp.wait_ge(sum_done, i + 1)
                    sp.dma_start(tile(k.counts, i), high[:, :, :]).then_inc(stored, 16)
                    sp.dma_start(tile(k.counts_low, i), low[:, :, :]).then_inc(stored, 16)
                sp.wait_ge(stored, 32 * (T + 1))

            @block.vector
            def _(dve):
                v.tensor_copy(iota_rep[:, :, :], k.iota_row[:, :].unsqueeze(2).to_broadcast([128, P, M]))
                v.drain()
                with dve.Fori(0, T) as i:
                    for u in range(U):
                        for cut, hot in ((k.rowG, row_hot), (k.colG, col_hot)):
                            v.tensor_tensor(out=hot[:, :, :], in0=iota_rep[:, :, :],
                                            in1=cut[:, bass.ds(i * U + u, 1), :].to_broadcast([128, P, M]), op=ALU.is_equal)
                        v.drain().then_inc(hot_done, 1)
                        dve.wait_ge(hist_done, U * i + u + 1)
                        for b, groups in enumerate(HB):
                            n = len(groups) * G
                            d0 = u * G * U + groups[0] * G
                            v.tensor_copy(acc[:, :, d0:d0 + n], ps[0:P, b, 0:n * T].rearrange("p (d t) -> p t d", t=T))
                        v.drain()
                    dve.wait_ge(in_done, 32 * (i + 1))
                    for part in (high, low):
                        v.tensor_tensor(out=acc[:, :, :], in0=acc[:, :, :], in1=part[:, :, :], op=ALU.add)
                        v.drain()
                    v.tensor_copy(high[:, :, :], acc[:, :, :])
                    v.drain()
                    v.tensor_tensor(out=low[:, :, :], in0=acc[:, :, :], in1=high[:, :, :], op=ALU.subtract)
                    v.drain().then_inc(sum_done, 1)

            @block.tensor
            def _(pe):
                with pe.Fori(0, T) as i:
                    for u in range(U):
                        pe.wait_ge(hot_done, U * i + u + 1)
                        for b, groups in enumerate(HB):
                            for s, gg in enumerate(groups):
                                for c in range(2):
                                    last = t_.matmul(ps[0:P, b, s * P:(s + 1) * P], col_hot[:, :, c * U + gg], row_hot[:, :, c * U + gg],
                                                     start=(c == 0), stop=(c == 1))
                        last.then_inc(hist_done, 1)


def transpose_counts_phase(k, name, counts, countsT, with_max):
    nc = k.nc
    v, t_ = nc.vector, nc.tensor
    with scope(nc) as (sb, pb, sem):
        tile = sb(name + "tile", [P, T, P], BF16)
        tr = sb(name + "tr", [P, N], BF16)
        absent = sb(name + "absent", [P, N], BF16)
        junk = sb(name + "junk", [P, N], BF16)
        mx1 = sb(name + "mx1", [P, HEADS], FP32)
        ps = pb(name + "ps", [128, NTB, 512], FP32)
        es_row = k.arena[0:P, 0:2 * HEADS * N].bitcast(FP32).rearrange("p (h n) -> p h n", h=HEADS)
        tile_in, tr_psum, tr_done, stored = sem(name + "tile_in"), sem(name + "psum"), sem(name + "done"), sem(name + "stored")
        es_loaded = sem(name + "es_loaded")
        with nc.Block() as block:
            @block.sync
            def _(sp):
                sp.sem_inc(stored, 16)
                if with_max:
                    for h in range(HEADS):
                        sp.dma_start(es_row[:, h, :].rearrange("q (t p) -> q t p", p=P),
                                     k.es_dram[:, h, :].unsqueeze(0).to_broadcast([P, T, P])).then_inc(es_loaded, 16)
                with sp.Fori(0, T) as i:
                    sp.wait_ge(stored, 16 * (i + 1))
                    sp.dma_start(tile[:, :, :], counts.rearrange("(t p) d -> p t d", p=P)[:, :, bass.ds(i * P, P)]).then_inc(tile_in, 16)
                    sp.wait_ge(tr_done, i + 1)
                    sp.dma_start(countsT[bass.ds(i * P, P), :], tr[:, :]).then_inc(stored, 16)
                sp.wait_ge(stored, 16 * (T + 1))

            @block.tensor
            def _(pe):
                with pe.Fori(0, T) as i:
                    pe.wait_ge(tile_in, 16 * (i + 1))
                    for t in range(T):
                        last = t_.matmul(ps[0:P, t // TQ, (t % TQ) * P:(t % TQ + 1) * P], tile[:, t, :], k.ident_bf[0:P, 0:P],
                                         start=True, stop=True)
                    last.then_inc(tr_psum, 1)

            @block.vector
            def _(dve):
                if with_max:
                    dve.wait_ge(es_loaded, 16 * HEADS)
                with dve.Fori(0, T) as i:
                    dve.wait_ge(tr_psum, i + 1)
                    for b in range(NTB):
                        n = min(TQ, T - b * TQ)
                        v.tensor_copy(tr[:, b * TQ * P:(b * TQ + n) * P], ps[0:P, b, 0:n * P])
                    v.drain()
                    if with_max:
                        v.tensor_scalar(absent[:, :], tr[:, :], 0.0, -BIG, ALU.is_equal, ALU.mult)
                        v.drain()
                        for h in range(HEADS):
                            v.tensor_tensor_reduce(out=junk[:, :], in0=es_row[:, h, :], in1=absent[:, :], scale=1.0,
                                                   scalar=-3e38, op0=ALU.add, op1=ALU.max, accum_out=mx1[:, h:h + 1])
                            v.drain()
                        v.tensor_copy(k.mx[:, bass.ds(i, 1), :].rearrange("p a h -> p (a h)"), mx1[:, :])
                        v.drain()
                    v.nop().then_inc(tr_done, 1)


def last_use(u, ring, period):
    if u >= ring:
        return ring
    return period + u - max(x for x in range(period) if x % ring == u % ring)


def gat_attend_phase(k, name, planes):
    nc = k.nc
    v, a, t_ = nc.vector, nc.scalar, nc.tensor
    TT = T * len(planes)
    RC, R1, R2 = 2, 3, 2
    NC = (N + 511) // 512
    NR = (T + 6) // 7
    with scope(nc) as (sb, pb, sem):
        ec = sb(name + "edge_max", [P, T, HEADS], FP32)
        has = sb(name + "has_edge", [P, T, HEADS], FP32)
        rows = sb(name + "row_terms", [P, 2, HEADS, T], FP32)
        rowsT = sb(name + "row_termsT", [HEADS * T, 2, P], FP32)
        es_now = sb(name + "es_now", [P, 2, T], FP32)
        row_b = k.arena[0:P, 0:8 * N].bitcast(FP32).rearrange("p (r j n) -> p r j n", r=2, j=2)
        cnt = k.arena[0:P, 10 * N:(10 + RC) * N].rearrange("p (r n) -> p r n", r=RC)
        zt = sb(name + "z_tile", [P, RC, D1], FP32)
        e1 = sb(name + "exp_full", [P, R1, N], FP32)
        e2 = sb(name + "exp_slope", [P, R2, N], FP32)
        sums = k.arena[0:D1, 8 * N:10 * N].bitcast(FP32)
        ps = pb(name + "ps_sums", [128, NC, 512], FP32)
        ps_t = pb(name + "ps_back", [128, 512], FP32)
        rows_ready, rows_psum = sem(name + "rows_ready"), sem(name + "rows_psum")
        rowsT_ready, rows_stored = sem(name + "rowsT_ready"), sem(name + "rows_stored")
        row_in = sem(name + "row_in")
        cz_in = [sem(name + f"cz_in{s}") for s in range(RC)]
        exp_done, e2_free, w_done, pv_done = sem(name + "exp_done"), sem(name + "e2_free"), sem(name + "w_done"), sem(name + "pv_done")
        head_out, back_psum, back_out = sem(name + "head_out"), sem(name + "back_psum"), sem(name + "back_out")
        act_passed = sem(name + "act_passed")
        uses = [sum(1 for x in range(TT) if x % RC == s) for s in range(RC)]

        with nc.Block() as block:
            @block.sync
            def _(sp):
                sp.wait_ge(rowsT_ready, 1)
                for j in range(2):
                    sp.dma_start(k.rows_dram[j].rearrange("h t p -> (h t) p"), rowsT[:, j, :]).then_inc(rows_stored, 16)
                sp.wait_ge(rows_stored, 32)
                with sp.Fori(0, HEADS) as h:
                    sp.wait_ge(exp_done, 2 * TT * h + 2)
                    for j in range(2):
                        sp.dma_start(row_b[:, bass.ds(h % 2, 1), j, :].rearrange("p a n -> p (a n)"),
                                     k.rows_dram[j, bass.ds(h, 1)].rearrange("a t p -> a (t p)").to_broadcast([P, N])).then_inc(row_in, 16)
                    for t in range(TT):
                        sp.wait_ge(pv_done, TT * h + t + 1 - last_use(t, RC, TT) + TT)
                        sp.dma_start(cnt[:, t % RC, :], planes[t // T][(t % T) * P:(t % T + 1) * P, :]).then_inc(cz_in[t % RC], 16)
                        sp.dma_start(zt[:, t % RC, :], k.z_dram[bass.ds(h, 1), t % T].rearrange("a p c -> (a p) c")).then_inc(cz_in[t % RC], 16)

            @block.vector
            def _(dve):
                v.tensor_scalar(has[:, :, :], k.mx[:, :, :], -0.5 * BIG, None, ALU.is_gt)
                v.drain()
                v.tensor_tensor(out=ec[:, :, :], in0=k.mx[:, :, :], in1=has[:, :, :], op=ALU.mult)
                v.drain()
                v.tensor_tensor(out=ec[:, :, :], in0=ec[:, :, :], in1=k.ed[:, :, :], op=ALU.add)
                v.drain()
                v.tensor_tensor(out=ec[:, :, :], in0=ec[:, :, :], in1=has[:, :, :], op=ALU.mult)
                v.drain()
                v.scalar_tensor_tensor(out=ec[:, :, :], in0=ec[:, :, :], scalar=0.01, in1=ec[:, :, :], op0=ALU.mult, op1=ALU.max)
                v.drain()
                v.tensor_tensor(out=rows[:, 0, :, :].rearrange("p h t -> p t h"), in0=k.ed[:, :, :], in1=ec[:, :, :], op=ALU.subtract)
                v.scalar_tensor_tensor(out=rows[:, 1, :, :].rearrange("p h t -> p t h"), in0=k.ed[:, :, :], scalar=0.01,
                                       in1=ec[:, :, :], op0=ALU.mult, op1=ALU.subtract)
                v.drain().then_inc(rows_ready, 1)

                def back(h, r):
                    n = min(7, T - 7 * r)
                    dve.wait_ge(back_psum, NR * h + r + 2)
                    v.tensor_copy(k.acc[:, bass.ds(h, 1), 7 * r:7 * r + n, :].rearrange("p a t c -> p (a t c)"),
                                  ps_t[0:P, 0:n * D1]).then_inc(back_out, 1)

                def head(h, first):
                    for t in range(TT):
                        dve.wait_ge(exp_done, 2 * (TT * h + t + 1) + 2 * TT + 2)
                        v.tensor_tensor(out=e1[:, t % R1, :], in0=e1[:, t % R1, :], in1=e2[:, t % R2, :], op=ALU.max)
                        v.drain().then_inc(e2_free, 1)
                        dve.wait_ge(cz_in[t % RC], 32 * (uses[t % RC] * h + t // RC + 1))
                        v.scalar_tensor_tensor(out=e1[:, t % R1, :], in0=e1[:, t % R1, :], scalar=1.0, in1=cnt[:, t % RC, :],
                                               op0=ALU.min, op1=ALU.mult).then_inc(w_done, 1)
                        if not first and t >= 3 and (t - 3) % 2 == 0 and (t - 3) // 2 < NR:
                            back(h - 1, (t - 3) // 2)

                head(0, True)
                with dve.Fori(1, HEADS) as h:
                    head(h, False)
                for r in range(NR):
                    back(HEADS - 1, r)

            @block.scalar
            def _(act):
                act.sem_inc(exp_done, 2 * TT + 2)
                act.sem_inc(e2_free, TT)
                act.sem_inc(pv_done, TT)
                act.sem_inc(head_out, NC)
                act.sem_inc(back_psum, 1)
                act.wait_ge(rows_psum, 1)
                a.activation(rowsT[:, :, :], ps[0:HEADS * T, 0:2, 0:P], ACT.Copy)
                a.drain().then_inc(rowsT_ready, 1)

                def head_sums(h):
                    for c in range(NC):
                        if c == 0:
                            act.wait_ge(pv_done, TT * (h + 1) + TT)
                            act.wait_ge(back_psum, NR * h + 1)
                        n = min(512, N - 512 * c)
                        a.activation(sums[:, 512 * c:512 * c + n], ps[0:D1, c, 0:n], ACT.Copy).then_inc(head_out, 1)

                def head(h, first):
                    if not first:
                        a.drain()
                    a.activation(es_now[:, 0, :], k.es[:, :, bass.ds(h, 1)].rearrange("p t a -> p (t a)"), ACT.Copy)
                    a.activation(es_now[:, 1, :], k.es[:, :, bass.ds(h, 1)].rearrange("p t a -> p (t a)"), ACT.Copy, scale=0.01)
                    a.drain()
                    act.wait_ge(row_in, 32 * (h + 1))
                    act.sem_inc(act_passed, 1)
                    for t in range(TT):
                        if t == 2 and not first:
                            head_sums(h - 1)
                        act.wait_ge(pv_done, TT * h + t + 1 - last_use(t, R1, TT) + TT)
                        act.sem_inc(act_passed, 1)
                        a.activation(e1[:, t % R1, :], row_b[:, bass.ds(h % 2, 1), 0, :].rearrange("p a n -> p (a n)"), ACT.Exp,
                                     bias=es_now[:, 0, t % T:t % T + 1]).then_inc(exp_done, 1)
                        act.wait_ge(e2_free, TT * h + t + 1 - last_use(t, R2, TT) + TT)
                        act.sem_inc(act_passed, 1)
                        a.activation(e2[:, t % R2, :], row_b[:, bass.ds(h % 2, 1), 1, :].rearrange("p a n -> p (a n)"), ACT.Exp,
                                     bias=es_now[:, 1, t % T:t % T + 1]).then_inc(exp_done, 1)

                head(0, True)
                with act.Fori(1, HEADS) as h:
                    head(h, False)
                head_sums(HEADS - 1)

            @block.tensor
            def _(pe):
                pe.wait_ge(rows_ready, 1)
                for j in range(2):
                    t_.transpose(ps[0:HEADS * T, j, 0:P], rows[:, j, :, :].rearrange("p h t -> p (h t)"), k.ident[0:P, 0:P])
                t_.drain().then_inc(rows_psum, 1)

                def back(h, r):
                    pe.wait_ge(head_out, NC * (h + 1) + NC)
                    if r > 0:
                        pe.wait_ge(back_out, NR * h + r)
                    for s in range(min(7, T - 7 * r)):
                        t = 7 * r + s
                        last = t_.transpose(ps_t[0:P, s * D1:(s + 1) * D1], sums[:, t * P:(t + 1) * P], k.ident[0:D1, 0:D1])
                    last.then_inc(back_psum, 1)

                def head(h, first):
                    for t in range(TT):
                        pe.wait_ge(w_done, TT * h + t + 1)
                        if first and t == 0:
                            pe.wait_ge(rowsT_ready, 1)
                        for c in range(NC):
                            n = min(512, N - 512 * c)
                            if t == 0:
                                pe.wait_ge(head_out, NC * h + c + 1)
                            last = t_.matmul(ps[0:D1, c, 0:n], zt[:, t % RC, :], e1[:, t % R1, 512 * c:512 * c + n],
                                             start=(t == 0), stop=(t == TT - 1))
                        last.then_inc(pv_done, 1)
                        if not first and t >= 2 and t % 2 == 0 and (t - 2) // 2 < NR:
                            back(h - 1, (t - 2) // 2)

                head(0, True)
                with pe.Fori(1, HEADS) as h:
                    head(h, False)
                for r in range(NR):
                    back(HEADS - 1, r)


def gat_finish_phase(k):
    nc = k.nc
    v = nc.vector
    with scope(nc) as (sb, pb, sem):
        den = sb("den", [P, HEADS, T], FP32)
        st = sb("fin_bn_st", [P, U, 6], FP32)
        mv = sb("fin_bn_mv", [P, U, 2], FP32)
        x_in = sem("x_in_again")
        with nc.Block() as block:
            @block.sync
            def _(sp):
                sp.dma_start(k.X[:, :, :], k.x.rearrange("(t p) f -> p t f", p=P)).then_inc(x_in, 16)

            @block.vector
            def _(dve):
                v.tensor_scalar(den[:, :, :], k.acc[:, :, :, DH], 1e-16, None, ALU.max)
                v.drain()
                v.reciprocal(den[:, :, :], den[:, :, :])
                v.drain()
                for h in range(HEADS):
                    v.tensor_tensor(out=k.acc[:, h, :, 0:DH], in0=k.acc[:, h, :, 0:DH],
                                    in1=den[:, h, :].unsqueeze(2).to_broadcast([P, T, DH]), op=ALU.mult)
                v.drain()
                dve.wait_ge(x_in, 16)
                for h in range(HEADS):
                    v.tensor_tensor(out=k.X[:, :, h * DH:(h + 1) * DH], in0=k.X[:, :, h * DH:(h + 1) * DH],
                                    in1=k.acc[:, h, :, 0:DH], op=ALU.add)
                v.drain()
                layernorm_stats(nc, dve, v, k.X, st, mv, k.MV)


def gat_separable_phase(k):
    nc = k.nc
    v, a, t_, g = nc.vector, nc.scalar, nc.tensor, nc.gpsimd
    R = 2 * U
    CHUNKS = ((0, 1), (2, 3, 4))
    BANK = ((0, 1, 2, 3, 4), (5, 6, 7, 3, 4))
    SHARED, OWN = (3, 4), (0, 1, 2)
    LAST = {3: 2 * U - 1, 4: 2 * U, 0: U * U - 2, 1: U * U - 1, 2: U * U}
    with scope(nc) as (sb, pb, sem):
        cnt = sb("cnt_block", [P, T, QB], BF16)
        ed_b = sb("ed_rows", [P, 2, HEADS, QB], FP32)
        kinds = sb("kinds", [P, R, 2, QB], BF16)
        sums = sb("set_sums", [P, U, 2, 3, D1], FP32)
        tot = sb("set_tot", [P, U, 2, D1], FP32)
        dst_now = sb("dst_now", [P, U, 2], FP32)
        num = sb("set_num", [P, U, D1], FP32)
        st = sb("set_bn_st", [P, U, 6], FP32)
        mv = sb("set_bn_mv", [P, U, 2], FP32)
        x_now = sb("set_x", [P, U, DH], FP32)
        den = sb("set_den", [P, U, 1], FP32)
        ps = pb("ps_sets", [128, 8, 512], FP32)
        x_in = sem("x_in_again")
        cnt_in = [sem(f"cnt_in{i}") for i in range(U)]
        ed_in = sem("ed_in")
        mask_done, kinds_done, pv_done = sem("mask_done"), sem("kinds_done"), sem("pv_done")
        shared_copied, own_copied = sem("set_shared_copied"), sem("set_own_copied")
        combined, act_passed = sem("set_combined"), sem("act_passed")
        num_done, den_done, x_done = sem("num_done"), sem("den_done"), sem("x_done")
        SETS = U * HEADS

        def slot(h, i, s):
            return U * ((h + i) % 2) + s

        with nc.Block() as block:
            @block.sync
            def _(sp):
                sp.sem_inc(pv_done, U * R)
                sp.sem_inc(shared_copied, len(SHARED))
                sp.sem_inc(own_copied, 2 * len(OWN))
                sp.sem_inc(combined, 1)
                sp.sem_inc(kinds_done, T)
                sp.sem_inc(ed_in, 16)

                def load(j):
                    sp.wait_ge(ed_in, 16 * HEADS * j + 16)
                    for h in range(HEADS):
                        sp.dma_start(ed_b[:, bass.ds(j % 2, 1), h, :].rearrange("q a (t p) -> q (a t) p", p=P),
                                     k.ed_dram[bass.ds(j * U, U), h, :].unsqueeze(0).to_broadcast([P, U, P])).then_inc(ed_in, 16)
                    for i in range(U):
                        sp.wait_ge(kinds_done, HEADS * T * j + (i + 1) * U)
                        sp.dma_start(cnt[:, i * U:(i + 1) * U, :],
                                     k.counts.rearrange("(t p) d -> p t d", p=P)[:, i * U:(i + 1) * U, bass.ds(j * QB, QB)]).then_inc(cnt_in[i], 16)

                load(0)
                sp.dma_start(k.X[:, :, :], k.x.rearrange("(t p) f -> p t f", p=P)).then_inc(x_in, 16)
                with sp.Fori(1, U) as j:
                    load(j)

            @block.scalar
            def _(act):
                def masks(j, h, i):
                    q = HEADS * j + h
                    for chunk in CHUNKS:
                        whole = i in (1, 2)
                        act.wait_ge(pv_done, U * (T * q + U * i + (U if whole else chunk[-1] + 1)))
                        act.sem_inc(act_passed, 1)
                        for s in chunk:
                            a.activation(kinds[:, slot(h, i, s), 0, :], ed_b[:, bass.ds(j % 2, 1), h, :].rearrange("p a d -> p (a d)"),
                                         ACT.Relu, scale=MASK_SCALE, bias=k.es_mask[:, U * i + s, h:h + 1]).then_inc(mask_done, 1)

                def copies(q, half):
                    act.wait_ge(combined, q + 1)
                    for u in SHARED:
                        act.wait_ge(pv_done, U * T * q + U * U * (U - 1) + LAST[u] + U * R)
                        a.activation(sums[:, u, :, :, :].rearrange("p e c d -> p (e c d)"), ps[0:P, BANK[half][u], 0:2 * W3],
                                     ACT.Copy).then_inc(shared_copied, 1)

                def block_masks(j, first):
                    act.wait_ge(ed_in, 16 * HEADS * (j + 1) + 16)
                    act.sem_inc(act_passed, 1)
                    for h in range(HEADS):
                        for i in range(U):
                            masks(j, h, i)
                            if i == 0 and not (first and h == 0):
                                copies(HEADS * j + h - 1, (h - 1) % 2)

                block_masks(0, True)
                with act.Fori(1, U) as j:
                    block_masks(j, False)
                copies(SETS - 1, 1)

            @block.vector
            def _(dve):
                def block_kinds(j, first):
                    for h in range(HEADS):
                        q = HEADS * j + h
                        for i in range(U):
                            if h == 0:
                                dve.wait_ge(cnt_in[i], 16 * (j + 1))
                            if i == 3 and not (first and h == 0):
                                reciprocals(q - 1)
                            if i == 4 and h == 1 and not first:
                                stats(j - 1)
                            if i == 1 and not (first and h == 0):
                                copies(q - 1, (h - 1) % 2)
                            for chunk in CHUNKS:
                                dve.wait_ge(mask_done, T * q + U * i + chunk[-1] + 1)
                                lo, n = slot(h, i, chunk[0]), len(chunk)
                                tiles = cnt[:, U * i + chunk[0]:U * i + chunk[0] + n, :]
                                v.tensor_tensor(out=kinds[:, lo:lo + n, 0, :], in0=kinds[:, lo:lo + n, 0, :], in1=tiles, op=ALU.min)
                                v.drain()
                                v.tensor_tensor(out=kinds[:, lo:lo + n, 1, :], in0=tiles, in1=kinds[:, lo:lo + n, 0, :],
                                                op=ALU.subtract).then_inc(kinds_done, n)

                def copies(q, half):
                    dve.wait_ge(combined, q + 1)
                    for u in OWN:
                        dve.wait_ge(pv_done, U * T * q + U * U * (U - 1) + LAST[u] + U * R)
                        v.tensor_copy(sums[:, u, :, :, :].rearrange("p e c d -> p (e c d)"), ps[0:P, BANK[half][u], 0:2 * W3])\
                            .then_inc(own_copied, 1)

                def reciprocals(q):
                    dve.wait_ge(num_done, q + 1)
                    v.tensor_scalar(den[:, :, :], num[:, :, DH:D1], 1e-16, None, ALU.max)
                    v.drain()
                    v.reciprocal(den[:, :, :], den[:, :, :])
                    v.drain().then_inc(den_done, 1)

                def stats(j):
                    dve.wait_ge(x_done, HEADS * (j + 1))
                    batch_stats(v, k.X, st, mv, k.MV, j)

                block_kinds(0, True)
                with dve.Fori(1, U) as j:
                    block_kinds(j, False)
                copies(SETS - 1, 1)
                reciprocals(SETS - 1)
                stats(U - 1)

            @block.tensor
            def _(pe):
                parts = zparts(k)
                with pe.Fori(0, U) as j:
                    for h in range(HEADS):
                        q = HEADS * j + h
                        for i in range(U):
                            banks = [(0, 1, 2), (3, 4)] if i == 0 else [(3, 4), (0, 1, 2)] if i == U - 1 else [range(U)]
                            for turn, some in enumerate(banks):
                                for s in range(U):
                                    t = U * i + s
                                    for chunk in CHUNKS:
                                        if turn == 0 and s == chunk[0]:
                                            pe.wait_ge(kinds_done, T * q + U * i + chunk[-1] + 1 + T)
                                    for u in some:
                                        bank = ps[0:P, BANK[h % 2][u]]
                                        if t == 0:
                                            if u in SHARED:
                                                pe.wait_ge(shared_copied, len(SHARED) * q + SHARED.index(u) + 1)
                                            else:
                                                pe.wait_ge(own_copied, len(OWN) * q + u + 1)
                                        for e in range(2):
                                            last = t_.matmul(bank[:, e * W3:(e + 1) * W3], kinds[:, slot(h, i, s), e, u * P:(u + 1) * P],
                                                             parts[:, t, h, e, :, :].rearrange("p c d -> p (c d)"),
                                                             start=(t == 0 and e == 0), stop=(t == T - 1 and e == 1))
                                        last.then_inc(pv_done, 1)

            @block.gpsimd
            def _(pool):
                pool.wait_ge(x_in, 16)
                with pool.Fori(0, U) as j:
                    with pool.Fori(0, HEADS) as h:
                        pool.wait_ge(shared_copied, len(SHARED) * (HEADS * j + h + 2))
                        pool.wait_ge(own_copied, len(OWN) * (HEADS * j + h + 3))
                        g.tensor_tensor(out=tot[:, :, :, :], in0=sums[:, :, :, 1, :], in1=sums[:, :, :, 2, :], op=ALU.add)
                        g.tensor_copy(dst_now[:, :, :], k.dst_exp[:, bass.ds(U * j, U), bass.ds(h, 1), :].rearrange("p t h e -> p t (h e)"))
                        g.drain()
                        g.tensor_tensor(out=tot[:, :, :, :], in0=tot[:, :, :, :], in1=sums[:, :, :, 0, :], op=ALU.add)
                        g.drain().then_inc(combined, 1)
                        g.tensor_tensor(out=tot[:, :, :, :], in0=tot[:, :, :, :],
                                        in1=dst_now[:, :, :].unsqueeze(3).to_broadcast([P, U, 2, D1]), op=ALU.mult)
                        g.drain()
                        g.tensor_tensor(out=num[:, :, :], in0=tot[:, :, 0, :], in1=tot[:, :, 1, :], op=ALU.add)
                        g.drain().then_inc(num_done, 1)
                        pool.wait_ge(den_done, HEADS * j + h + 1)
                        g.tensor_tensor(out=num[:, :, 0:DH], in0=num[:, :, 0:DH], in1=den[:, :, :].to_broadcast([P, U, DH]), op=ALU.mult)
                        g.drain()
                        g.tensor_copy(x_now[:, :, :], k.X[:, bass.ds(U * j, U), bass.ds(h * DH, DH)])
                        g.drain()
                        g.tensor_tensor(out=num[:, :, 0:DH], in0=num[:, :, 0:DH], in1=x_now[:, :, :], op=ALU.add)
                        g.drain()
                        g.tensor_copy(k.X[:, bass.ds(U * j, U), bass.ds(h * DH, DH)], num[:, :, 0:DH])
                        g.drain().then_inc(x_done, 1)


HALF = (QB + 1) // 2
HALVES = [(0, HALF), (HALF, QB - HALF)]


def column(ap):
    return ap.rearrange("(p a) -> p a", a=1)


def moe_phase(k):
    nc = k.nc
    v, a, t_ = nc.vector, nc.scalar, nc.tensor
    X = k.X
    EX, H2 = 4, 64
    NB1 = 6
    I1, I2 = 2 * NB1, 2 * (EX + 1)
    IT = I1 + I2
    with scope(nc) as (sb, pb, sem):
        H = sb("h_moe", [P, U, F], FP32)
        HT = sb("hT_moe", [128, KF, QB], FP32)
        st = sb("bn_st_m", [P, U, 6], FP32)
        mv = sb("bn_mv_m", [P, U, 2], FP32)
        MV = k.MV
        std = sb("std_m", [P, T], FP32)
        rstd = sb("rstd_m", [P, T], FP32)
        eps = sb("eps_m", [P, 1], FP32)
        w1 = sb("moe_w1", [128, KF, NB1, 128], FP32)
        w2e = sb("moe_w2e", [128, EX, H2], FP32)
        w2s = sb("moe_w2s", [128, KF, 128], FP32)
        w3e = sb("moe_w3e", [H2, EX, F], FP32)
        w3s = sb("moe_w3s", [128, F], FP32)
        b3 = sb("moe_b3", [EX + 1, F], FP32)
        b1 = sb("moe_b1", [128, NB1], FP32)
        b2e = sb("moe_b2e", [H2, EX], FP32)
        b2s = sb("moe_b2s", [128, 1], FP32)
        gw = sb("gate_w", [128, KF, EX], FP32)
        gb = sb("gate_b", [P, EX], FP32)
        A1 = sb("moe_a1", [128, NB1, QB], FP32)
        A2e = sb("moe_a2e", [H2, EX, QB], FP32)
        A2s = sb("moe_a2s", [128, QB], FP32)
        lg = sb("gate_logits", [P, U, EX], FP32)
        ge = sb("gate_exp", [P, U, EX], FP32)
        m1 = sb("gate_m1", [P, U, EX], FP32)
        m2 = sb("gate_m2", [P, U, EX], FP32)
        prio = sb("gate_prio", [P, U, EX], FP32)
        g1 = sb("gate_s1", [P, U], FP32)
        g2 = sb("gate_s2", [P, U], FP32)
        g3 = sb("gate_s3", [P, U], FP32)
        g5 = sb("gate_weights", [P, U, EX + 1], FP32)
        gT = sb("gate_weightsT", [EX + 1, QB], FP32)
        ps_t = pb("ps_tm", [128, 3, 512], FP32)
        ps_f = pb("ps_fm", [128, 2, 512], FP32)
        ps_o = pb("ps_om", [128, 3, 512], FP32)
        w_in, stats_done, std_done = sem("m_w_in"), sem("m_stats"), sem("m_std")
        h_ready, t_ready, ht_ready = sem("m_h_ready"), sem("m_t_ready"), sem("m_ht_ready")
        f_done, f_out, o_done, o_out = sem("m_f_done"), sem("m_f_out"), sem("m_o_done"), sem("m_o_out")
        lg_psum, lg_max, lg_exp, top_done, top_exp = sem("m_lg_psum"), sem("m_lg_max"), sem("m_lg_exp"), sem("m_top"), sem("m_top_exp")
        g_ready, gt_psum, gt_ready, wr = sem("m_g_ready"), sem("m_gt_psum"), sem("m_gt_ready"), k.args
        with nc.Block() as block:
            @block.sync
            def _(sp):
                loads = [
                    (w1[:, :, 0:EX, :], wr["L0_ffn_eW1"].rearrange("e (q i) o -> q i e o", i=128)),
                    (w1[:, :, EX:NB1, :], wr["L0_ffn_sW1"].rearrange("(q i) (b o) -> q i b o", i=128, o=128)),
                ]
                for dst, src in loads:
                    for q in range(KF):
                        sp.dma_start(dst[:, q], src[q]).then_inc(w_in, 16)
                rest = [
                    (w2e[:, :, :], wr["L0_ffn_eW2"].rearrange("e i o -> i e o")),
                    (w2s[:, :, :], wr["L0_ffn_sW2"].rearrange("(q i) o -> i q o", i=128)),
                    (w3e[:, :, :], wr["L0_ffn_eW3"].rearrange("e i o -> i e o")),
                    (w3s[:, :], wr["L0_ffn_sW3"]),
                    (b3[0:EX, :], wr["L0_ffn_eb3"]),
                    (b3[EX:EX + 1, :], wr["L0_ffn_sb3"].rearrange("(a f) -> a f", a=1)),
                    (b2s[:, :], column(wr["L0_ffn_sb2"])),
                    (gw[:, :, :], wr["L0_ffn_gW"].rearrange("(q i) e -> i q e", i=128)),
                    (gb[:, :], wr["L0_ffn_gb"].unsqueeze(0).to_broadcast([P, EX])),
                ]
                for e in range(EX):
                    rest.append((b1[:, e:e + 1], column(wr["L0_ffn_eb1"][e])))
                    rest.append((b2e[:, e:e + 1], column(wr["L0_ffn_eb2"][e])))
                for b in range(2):
                    rest.append((b1[:, EX + b:EX + b + 1], column(wr["L0_ffn_sb1"][b * 128:(b + 1) * 128])))
                for dst, src in rest:
                    sp.dma_start(dst, src).then_inc(w_in, 16)
                k.moe_loads = 2 * KF + len(rest)

            @block.vector
            def _(dve):
                v.memset(eps[:, :], EPS)
                v.memset(g5[:, :, :], 1.0)
                for e in range(EX):
                    v.memset(prio[:, :, e], float(EX - e))
                v.drain().then_inc(stats_done, 1)
                dve.wait_ge(std_done, 1)
                v.reciprocal(rstd[:, :], std[:, :])
                v.drain()

                def bc(s):
                    return s[:, :].unsqueeze(2).to_broadcast([P, U, EX])

                def first_largest(mask, values):
                    v.tensor_reduce(out=g1[:, :], in_=values[:, :, :], axis=AXX, op=ALU.max)
                    v.drain()
                    v.tensor_tensor(out=mask[:, :, :], in0=values[:, :, :], in1=bc(g1), op=ALU.is_equal)
                    v.drain()
                    v.tensor_tensor(out=mask[:, :, :], in0=mask[:, :, :], in1=prio[:, :, :], op=ALU.mult)
                    v.drain()
                    v.tensor_reduce(out=g2[:, :], in_=mask[:, :, :], axis=AXX, op=ALU.max)
                    v.drain()
                    v.tensor_tensor(out=mask[:, :, :], in0=mask[:, :, :], in1=bc(g2), op=ALU.is_equal)
                    v.drain()

                def gates(i):
                    dve.wait_ge(lg_psum, i + 1)
                    v.tensor_tensor(out=lg[:, :, :], in0=ps_t[0:P, 2, 256:256 + U * EX].rearrange("p (u e) -> p u e", e=EX),
                                    in1=gb[:, :].unsqueeze(1).to_broadcast([P, U, EX]), op=ALU.add)
                    v.drain()
                    v.tensor_reduce(out=g1[:, :], in_=lg[:, :, :], axis=AXX, op=ALU.max)
                    v.drain()
                    v.tensor_tensor(out=lg[:, :, :], in0=lg[:, :, :], in1=bc(g1), op=ALU.subtract)
                    v.drain().then_inc(lg_max, 1)
                    dve.wait_ge(lg_exp, i + 1)
                    v.tensor_reduce(out=g1[:, :], in_=ge[:, :, :], axis=AXX, op=ALU.add)
                    v.drain()
                    v.reciprocal(g1[:, :], g1[:, :])
                    v.drain()
                    v.tensor_tensor(out=ge[:, :, :], in0=ge[:, :, :], in1=bc(g1), op=ALU.mult)
                    v.drain()
                    first_largest(m1, ge)
                    v.tensor_copy(g3[:, :], g1[:, :])
                    v.scalar_tensor_tensor(out=ge[:, :, :], in0=m1[:, :, :], scalar=-4.0, in1=ge[:, :, :], op0=ALU.mult, op1=ALU.add)
                    v.drain()
                    first_largest(m2, ge)
                    v.tensor_tensor(out=g3[:, :], in0=g1[:, :], in1=g3[:, :], op=ALU.subtract)
                    v.drain().then_inc(top_done, 1)
                    dve.wait_ge(top_exp, i + 1)
                    v.tensor_scalar(g1[:, :], g3[:, :], 1.0, None, ALU.add)
                    v.drain()
                    v.reciprocal(g1[:, :], g1[:, :])
                    v.drain()
                    v.tensor_tensor(out=g2[:, :], in0=g3[:, :], in1=g1[:, :], op=ALU.mult)
                    v.tensor_tensor(out=m1[:, :, :], in0=m1[:, :, :], in1=bc(g1), op=ALU.mult)
                    v.drain()
                    v.tensor_tensor(out=m2[:, :, :], in0=m2[:, :, :], in1=bc(g2), op=ALU.mult)
                    v.drain()
                    v.tensor_tensor(out=g5[:, :, 0:EX], in0=m1[:, :, :], in1=m2[:, :, :], op=ALU.add)
                    v.drain().then_inc(g_ready, 1)

                def combine(i):
                    for u in range(U):
                        xt = X[:, bass.ds(i * U + u, 1), :].rearrange("p a f -> p (a f)")
                        for b, parts in enumerate([(None, 0), (1, 2), (3,)]):
                            dve.wait_ge(o_done, 3 * (U * i + u) + b + 1)
                            for s, e in enumerate(parts):
                                src = ps_o[0:P, b, s * F:(s + 1) * F]
                                if e is None:
                                    v.tensor_tensor(out=xt, in0=src, in1=xt, op=ALU.add)
                                else:
                                    v.scalar_tensor_tensor(out=xt, in0=src, scalar=g5[:, u, e:e + 1], in1=xt, op0=ALU.mult, op1=ALU.add)
                                d = v.drain()
                            d.then_inc(o_out, 1)

                normalize_batch(v, X, H, MV, rstd, 0, h_ready, t_ready, dve, True)
                dve.wait_ge(w_in, 16 * k.moe_loads)
                with dve.Fori(1, U) as i:
                    normalize_batch(v, X, H, MV, rstd, i, h_ready, t_ready, dve, False)
                    gates(i - 1)
                    combine(i - 1)
                    batch_stats(v, X, st, mv, MV, i - 1)
                gates(U - 1)
                combine(U - 1)
                batch_stats(v, X, st, mv, MV, U - 1)

            @block.scalar
            def _(act):
                act.sem_inc(f_out, 2)
                act.wait_ge(stats_done, 1)
                a.activation(std[:, :], MV[:, :, 1], ACT.Sqrt, bias=eps[:, 0:1])
                a.drain().then_inc(std_done, 1)

                def copies(i):
                    for b, tiles in enumerate(BANKS):
                        act.wait_ge(t_ready, 3 * i + b + 1)
                        n = len(tiles)
                        a.activation(HT[:, :, tiles[0] * P:(tiles[0] + n) * P].rearrange("p q (u c) -> p u q c", c=P),
                                     ps_t[:, b, 0:n * KF * P].rearrange("p (u q c) -> p u q c", u=n, c=P), ACT.Copy).then_inc(ht_ready, 1)

                def layers(i):
                    m = 0
                    for o in range(NB1):
                        for lo, n in HALVES:
                            act.wait_ge(f_done, IT * i + m + 1)
                            a.activation(A1[:, o, lo:lo + n], ps_f[:, m % 2, 0:n], ACT.Relu, bias=b1[:, o:o + 1]).then_inc(f_out, 1)
                            m += 1
                        if o == 0:
                            act.wait_ge(lg_max, i + 1)
                            a.activation(ge[:, :, :], lg[:, :, :], ACT.Exp).then_inc(lg_exp, 1)
                        if o == 2:
                            act.wait_ge(top_done, i + 1)
                            a.activation(g3[:, :], g3[:, :], ACT.Exp).then_inc(top_exp, 1)
                    for e in range(EX + 1):
                        for lo, n in HALVES:
                            act.wait_ge(f_done, IT * i + m + 1)
                            if e < EX:
                                a.activation(A2e[:, e, lo:lo + n], ps_f[0:H2, m % 2, 0:n], ACT.Relu, bias=b2e[:, e:e + 1]).then_inc(f_out, 1)
                            else:
                                a.activation(A2s[:, lo:lo + n], ps_f[:, m % 2, 0:n], ACT.Relu, bias=b2s[:, 0:1]).then_inc(f_out, 1)
                            m += 1
                    act.wait_ge(gt_psum, i + 1)
                    a.activation(gT[:, 0:4 * P], ps_t[0:EX + 1, 0, 0:4 * P], ACT.Copy)
                    a.activation(gT[:, 4 * P:QB], ps_t[0:EX + 1, 1, 0:P], ACT.Copy)
                    a.drain().then_inc(gt_ready, 1)

                copies(0)
                act.wait_ge(w_in, 16 * k.moe_loads)
                with act.Fori(1, U) as i:
                    layers(i - 1)
                    copies(i)
                layers(U - 1)

            @block.tensor
            def _(pe):
                def transposes(i, first):
                    for b, tiles in enumerate(BANKS):
                        if not first and b == 0:
                            pe.wait_ge(gt_ready, i)
                        pe.wait_ge(h_ready, U * i + tiles[-1] + 1)
                        for s, u in enumerate(tiles):
                            for q in range(KF):
                                last = t_.transpose(ps_t[:, b, (s * KF + q) * P:(s * KF + q + 1) * P],
                                                    H[:, u, q * 128:(q + 1) * 128], k.ident[0:P, 0:P])
                        last.then_inc(t_ready, 1)

                def layers(i):
                    pe.wait_ge(ht_ready, 3 * (i + 1))
                    for u in range(U):
                        for q in range(KF):
                            last = t_.matmul(ps_t[0:P, 2, 256 + u * EX:256 + (u + 1) * EX], HT[:, q, u * P:(u + 1) * P], gw[:, q, :],
                                             start=(q == 0), stop=(q == KF - 1))
                    last.then_inc(lg_psum, 1)
                    m = 0
                    for o in range(NB1):
                        for lo, n in HALVES:
                            pe.wait_ge(f_out, IT * i + m + 1)
                            for q in range(KF):
                                last = t_.matmul(ps_f[:, m % 2, 0:n], w1[:, q, o, :], HT[:, q, lo:lo + n], start=(q == 0), stop=(q == KF - 1))
                            last.then_inc(f_done, 1)
                            m += 1
                    for e in range(EX + 1):
                        for lo, n in HALVES:
                            pe.wait_ge(f_out, IT * i + m + 1)
                            if e < EX:
                                last = t_.matmul(ps_f[0:H2, m % 2, 0:n], w2e[:, e, :], A1[:, e, lo:lo + n], start=True, stop=True)
                            else:
                                for q in range(KF):
                                    last = t_.matmul(ps_f[:, m % 2, 0:n], w2s[:, q, :], A1[:, EX + q, lo:lo + n],
                                                     start=(q == 0), stop=(q == KF - 1))
                            last.then_inc(f_done, 1)
                            m += 1
                    pe.wait_ge(g_ready, i + 1)
                    for u in range(U):
                        last = t_.transpose(ps_t[0:EX + 1, u // 4, (u % 4) * P:(u % 4 + 1) * P], g5[:, u, :], k.ident[0:P, 0:P])
                    last.then_inc(gt_psum, 1)

                def outputs(i):
                    pe.wait_ge(f_out, IT * (i + 1) + 2)
                    pe.wait_ge(gt_ready, i + 1)
                    for u in range(U):
                        cols = slice(u * P, (u + 1) * P)
                        for b, parts in enumerate([(None, 0), (1, 2), (3,)]):
                            pe.wait_ge(o_out, 3 * (U * i + u) + b + 1)
                            for s, e in enumerate(parts):
                                dst = ps_o[0:P, b, s * F:(s + 1) * F]
                                if e is None:
                                    t_.matmul(dst, A2s[:, cols], w3s[:, :], start=True, stop=False)
                                    last = t_.matmul(dst, gT[:, cols], b3[:, :], start=False, stop=True)
                                else:
                                    last = t_.matmul(dst, A2e[:, e, cols], w3e[:, e, :], start=True, stop=True)
                            last.then_inc(o_done, 1)

                pe.sem_inc(o_out, 3)
                transposes(0, True)
                pe.wait_ge(w_in, 16 * k.moe_loads)
                with pe.Fori(1, U) as i:
                    layers(i - 1)
                    transposes(i, False)
                    outputs(i - 1)
                layers(U - 1)
                outputs(U - 1)


def row_of(X, t):
    return X[:, bass.ds(t, 1), 0:F].rearrange("p a f -> p (a f)")


def split_rest_dve(dve, v, full, rest, R3, hi_done, rest_done, mid_done, i, before=0):
    rows = R3[:, bass.ds(i * U, U), :]
    dve.wait_ge(hi_done, before + i + 1)
    v.tensor_tensor(out=rest[:, :, :], in0=full[:, :, :], in1=rows[:, :, 0:F], op=ALU.subtract)
    v.drain().then_inc(rest_done, 1)
    dve.wait_ge(mid_done, before + i + 1)
    v.tensor_tensor(out=rows[:, :, PART[2][0]:X3], in0=rest[:, :, :], in1=rows[:, :, PART[1][0]:PART[1][0] + F], op=ALU.subtract)
    v.drain()


def split_batch_act(act, a, full, rest, R3, full_done, hi_done, rest_done, mid_done, i, before=0):
    act.wait_ge(full_done, before + i + 1)
    a.activation(R3[:, bass.ds(i * U, U), 0:F], full[:, :, :], ACT.Copy).then_inc(hi_done, 1)
    act.wait_ge(rest_done, before + i + 1)
    a.activation(R3[:, bass.ds(i * U, U), PART[1][0]:PART[1][0] + F], rest[:, :, :], ACT.Copy).then_inc(mid_done, 1)


def convolutions_phase(k, name, counts, countsT):
    nc = k.nc
    v, a, t_ = nc.vector, nc.scalar, nc.tensor
    X = k.X
    NS = U * len(counts)
    STEPS = [(counts, k.pa), (countsT, k.pb), (counts, k.pa), (countsT, k.pb)]
    PARTS_OF = [k.pa, k.pb, k.pa, k.pb]
    with scope(nc) as (sb, pb, sem):
        ring = sb(name + "ring", [P, U, U, QB], BF16)
        means = sb(name + "means", [P, U, F], FP32)
        meansT = sb(name + "meansT", [128, KF, QB], FP32)
        full = sb(name + "full", [P, U, F], FP32)
        rest = sb(name + "rest", [P, U, F], FP32)
        raw = sb(name + "raw", [P, U, F + 1], FP32)
        std = sb(name + "std", [P, T], FP32)
        rstd = sb(name + "rstd", [P, T], FP32)
        eps = sb(name + "eps", [P, 1], FP32)
        num = sb(name + "num", [P, U], FP32)
        one = sb(name + "one", [P, U], FP32)
        inv = sb(name + "inv", [P, U], FP32)
        W = sb(name + "w", [128, 2, KF, F], FP32)
        bias = sb(name + "bias", [P, 2, F], FP32)
        slope = sb(name + "slope", [P, 1], FP32)
        st = sb(name + "bn_st", [P, U, 6], FP32)
        mv = sb(name + "bn_mv", [P, U, 2], FP32)
        ps = pb(name + "ps", [128, U, 512], FP32)
        ps_w = pb(name + "ps_w", [128, 3, 512], FP32)
        c_in = [sem(name + f"c_in{s}") for s in range(U)]
        c_used, c_out, b_in, w_in = sem(name + "c_used"), sem(name + "c_out"), sem(name + "b_in"), sem(name + "w_in")
        h_ready, t_ready, ht_ready = sem(name + "h_ready"), sem(name + "t_ready"), sem(name + "ht_ready")
        z_ready, z_free, parts_done = sem(name + "z_ready"), sem(name + "z_free"), sem(name + "parts_done")
        full_done, hi_done, rest_done, mid_done = sem(name + "full_d"), sem(name + "hi"), sem(name + "rest_d"), sem(name + "mid")
        eps_set, std_done, next_in = sem(name + "eps_set"), sem(name + "std_done"), sem(name + "next_in")
        with nc.Block() as block:
            @block.sync
            def _(sp):
                def loads(n, i):
                    planes = STEPS[n][0]
                    for s in range(NS):
                        sp.wait_ge(c_used, NS * (U * n + i) + s + 1)
                        sp.dma_start(ring[:, s % U, :, :],
                                     planes[s // U][(s % U) * QB:(s % U + 1) * QB, bass.ds(i * QB, QB)].rearrange("(t p) d -> p t d", p=P))\
                            .then_inc(c_in[s % U], 16)

                for n in range(len(STEPS)):
                    with sp.Fori(0, U) as i:
                        loads(n, i)
                w1, b1 = k.args["L1_ffn_w1"], k.args["L1_ffn_b1"]
                sp.dma_start(k.ffn_w1[:, :, :], w1.rearrange("(q i) o -> i q o", i=128)).then_inc(next_in, 16)
                for o in range(HIDDEN // 128):
                    sp.dma_start(k.ffn_b1[:, o:o + 1], column(b1[o * 128:(o + 1) * 128])).then_inc(next_in, 16)
                sp.wait_ge(next_in, 16 * (1 + HIDDEN // 128))

            @block.gpsimd
            def _(pool):
                for j in range(2):
                    pool.dma_start(W[:, j, :, :], k.args[f"L1_gnn_W{j + 1}"].rearrange("(q i) o -> i q o", i=128)).then_inc(w_in, 16)
                    pool.dma_start(bias[:, j, :], k.args[f"L1_gnn_b{j + 1}"].unsqueeze(0).to_broadcast([P, F])).then_inc(b_in, 16)
                pool.dma_start(slope[:, :], k.args["L1_gnn_a"].unsqueeze(0).to_broadcast([P, 1])).then_inc(b_in, 16)

            @block.tensor
            def _(pe):
                def sums(n, i, after):
                    rows = STEPS[n][1]
                    for s in range(NS):
                        pe.wait_ge(c_in[s % U], 16 * (len(counts) * (U * n + i) + s // U + 1))
                        pe.wait_ge(parts_done, U * n + s % U + 1)
                        for w in range(U):
                            t = s * U + w
                            for kk in range(U):
                                if t == 0:
                                    pe.wait_ge(c_out, U * (U * n + i) + kk + 1)
                                for j, (off, size) in enumerate(PART):
                                    last = t_.matmul(ps[0:P, kk, 0:size], ring[:, s % U, w, kk * P:(kk + 1) * P], rows[:, t % T, off:off + size],
                                                     start=(t == 0 and j == 0), stop=(t == NS * U - 1 and j == 2))
                        last.then_inc(c_used, 1)
                        if s in after:
                            after[s]()

                def transposes(c, i):
                    for b, tiles in enumerate(BANKS):
                        pe.wait_ge(h_ready, U * (U * c + i) + tiles[-1] + 1)
                        pe.wait_ge(z_free, 3 * (U * c + i) + b + 1)
                        for s, u in enumerate(tiles):
                            for q in range(KF):
                                last = t_.transpose(ps_w[:, b, (s * KF + q) * P:(s * KF + q + 1) * P],
                                                    means[:, u, q * 128:(q + 1) * 128], k.ident[0:P, 0:P])
                        last.then_inc(t_ready, 1)

                def products(c, i):
                    for b, tiles in enumerate(BANKS):
                        pe.wait_ge(ht_ready, 3 * (U * c + i) + b + 1)
                        for s, u in enumerate(tiles):
                            for q in range(KF):
                                last = t_.matmul(ps_w[0:P, b, s * F:(s + 1) * F], meansT[:, q, u * P:(u + 1) * P], W[:, c, q, :],
                                                 start=(q == 0), stop=(q == KF - 1))
                        last.then_inc(z_ready, 1)

                for c in range(2):
                    sums(2 * c, 0, {})
                    pe.wait_ge(w_in, 32)
                    with pe.Fori(1, U) as i:
                        sums(2 * c, i, {0: lambda: transposes(c, i - 1), 1: lambda: products(c, i - 1)})
                    sums(2 * c + 1, 0, {0: lambda: transposes(c, U - 1), 1: lambda: products(c, U - 1)})
                    with pe.Fori(1, U) as i:
                        sums(2 * c + 1, i, {})

            @block.vector
            def _(dve):
                v.memset(eps[:, :], EPS)
                v.memset(k.pa[:, :, F:F + 1], 1.0)
                v.memset(k.pb[:, :, F:F + 1], 1.0)
                v.drain().then_inc(eps_set, 1)
                dve.sem_inc(z_free, 3)
                dve.sem_inc(c_out, U)
                dve.sem_inc(c_used, U)

                def means_out(n, i):
                    dve.wait_ge(c_used, NS * (U * n + i + 1) + U)
                    for kk in range(U):
                        v.tensor_copy(raw[:, kk, :], ps[0:P, kk, 0:F + 1]).then_inc(c_out, 1)
                    v.drain()
                    v.tensor_scalar(num[:, :], raw[:, :, F], 1.0, None, ALU.max)
                    v.tensor_scalar(one[:, :], raw[:, :, F], 1.0, None, ALU.min)
                    v.drain()
                    v.reciprocal(num[:, :], num[:, :])
                    v.drain()
                    v.tensor_tensor(out=inv[:, :], in0=num[:, :], in1=one[:, :], op=ALU.mult)
                    v.drain()
                    for kk in range(U):
                        if n % 2 == 0:
                            v.tensor_scalar(means[:, kk, :], raw[:, kk, 0:F], inv[:, kk:kk + 1], None, ALU.mult)
                        else:
                            v.scalar_tensor_tensor(out=full[:, kk, :], in0=raw[:, kk, 0:F], scalar=inv[:, kk:kk + 1], in1=bias[:, n // 2, :],
                                                   op0=ALU.mult, op1=ALU.add)
                    v.drain()
                    if n % 2 == 0:
                        v.nop().then_inc(h_ready, U)

                def split(n, i):
                    split_rest_dve(dve, v, full, rest, PARTS_OF[n + 1], hi_done, rest_done, mid_done, i, U * (n + 1))
                    v.nop().then_inc(parts_done, 1)

                def products_out(n, i):
                    for b, tiles in enumerate(BANKS):
                        dve.wait_ge(z_ready, 3 * (U * (n // 2) + i) + b + 1)
                        m = len(tiles)
                        v.tensor_copy(full[:, tiles[0]:tiles[0] + m, :].rearrange("p u f -> p (u f)"), ps_w[0:P, b, 0:m * F])
                        v.drain().then_inc(z_free, 1)
                    v.nop().then_inc(full_done, 1)
                    split(n, i)

                def rows_out(n, i):
                    rows = bass.ds(i * U, U)
                    if n == 3:
                        v.tensor_tensor(out=full[:, :, :], in0=full[:, :, :], in1=k.LNX[:, rows, :], op=ALU.add)
                        v.drain()
                    v.tensor_scalar(rest[:, :, :], full[:, :, :], 0.0, slope[:, 0:1], ALU.min, ALU.mult)
                    v.drain()
                    v.scalar_tensor_tensor(out=full[:, :, :], in0=full[:, :, :], scalar=0.0, in1=rest[:, :, :], op0=ALU.max, op1=ALU.add)
                    v.drain()
                    if n == 3:
                        v.tensor_tensor(out=X[:, rows, :], in0=X[:, rows, :], in1=full[:, :, :], op=ALU.add)
                        v.drain()
                        batch_stats(v, X, st, mv, k.MV, i)
                    else:
                        v.nop().then_inc(full_done, 1)
                        split(n, i)

                dve.wait_ge(std_done, 1)
                v.reciprocal(rstd[:, :], std[:, :])
                v.drain()
                with dve.Fori(0, U) as i:
                    for u in range(U):
                        t = i * U + u
                        v.tensor_scalar(full[:, u, :], row_of(X, t), k.MV[:, bass.ds(t, 1), 0:1].rearrange("p a b -> p (a b)"),
                                        rstd[:, bass.ds(t, 1)], ALU.subtract, ALU.mult)
                    v.drain().then_inc(full_done, 1)
                    v.tensor_copy(k.LNX[:, bass.ds(i * U, U), :], full[:, :, :])
                    split(-1, i)
                dve.wait_ge(b_in, 48)
                for n in range(len(STEPS)):
                    with dve.Fori(0, U) as i:
                        means_out(n, i)
                        if n % 2 == 0:
                            products_out(n, i)
                        else:
                            rows_out(n, i)

            @block.scalar
            def _(act):
                act.wait_ge(eps_set, 1)
                a.activation(std[:, :], k.MV[:, :, 1], ACT.Sqrt, bias=eps[:, 0:1])
                a.drain().then_inc(std_done, 1)
                for n in range(-1, 3):
                    with act.Fori(0, U) as i:
                        if n in (0, 2):
                            for b, tiles in enumerate(BANKS):
                                act.wait_ge(t_ready, 3 * (U * (n // 2) + i) + b + 1)
                                m = len(tiles)
                                a.activation(meansT[:, :, tiles[0] * P:(tiles[0] + m) * P].rearrange("p q (u c) -> p u q c", c=P),
                                             ps_w[:, b, 0:m * KF * P].rearrange("p (u q c) -> p u q c", u=m, c=P), ACT.Copy).then_inc(ht_ready, 1)
                        split_batch_act(act, a, full, rest, PARTS_OF[n + 1], full_done, hi_done, rest_done, mid_done, i, U * (n + 1))


def ffn_phase(k):
    nc = k.nc
    v, a, t_ = nc.vector, nc.scalar, nc.tensor
    X, wr = k.X, k.args
    HB8 = HIDDEN // 128
    I1 = 2 * HB8
    TOPK = N // 2 - 1
    with scope(nc) as (sb, pb, sem):
        H = sb("f_h", [P, U, F], FP32)
        HT = sb("f_hT", [128, KF, QB], FP32)
        MV = k.MV
        std = sb("f_std", [P, T], FP32)
        rstd = sb("f_rstd", [P, T], FP32)
        eps = sb("f_eps", [P, 1], FP32)
        w1, b1 = k.ffn_w1, k.ffn_b1
        w2 = sb("f_w2", [128, HB8, F], FP32)
        b2 = sb("f_b2", [P, F], FP32)
        wr_b = sb("f_wr", [P, F], FP32)
        br_b = sb("f_br", [P, 1], FP32)
        A = sb("f_a", [128, HB8, QB], FP32)
        Y = k.arena[0:P, 0:2 * T * F].bitcast(FP32).rearrange("p (t f) -> p t f", t=T)
        R = k.arena[0:P, 2 * T * F:4 * T * F].bitcast(FP32).rearrange("p (t f) -> p t f", t=T)
        wt5 = sb("f_wt5", [P, U], FP32)
        wt = sb("f_wt", [P, T], FP32)
        wtT = sb("f_wtT", [T, P], FP32)
        w_row = sb("f_w_row", [P, N], FP32)
        junk = sb("f_junk", [P, N], BF16)
        prod = sb("f_prod", [P, U, F], FP32)
        before = sb("f_before", [P, P], FP32)
        gt = sb("f_gt", [P, T], FP32)
        ge = sb("f_ge", [P, T], FP32)
        tie = sb("f_tie", [P, T], FP32)
        ws = sb("f_ws", [P, T], FP32)
        ps_t = pb("f_ps_t", [128, 3, 512], FP32)
        ps_f = pb("f_ps_f", [128, 2, 512], FP32)
        ps_o = pb("f_ps_o", [128, 3, 512], FP32)
        w_in, s_in, stats_done, std_done = sem("f_w_in"), sem("f_s_in"), sem("f_stats"), sem("f_std_done")
        h_ready, t_ready, ht_ready = sem("f_h_ready"), sem("f_t_ready"), sem("f_ht_ready")
        f_done, f_out, o_done, y_done = sem("f_done"), sem("f_out"), sem("f_o_done"), sem("f_y_done")
        wt_done, wt_psum, wt_copied, wt_stored, row_in, tri_done = (sem("f_wt_done"), sem("f_wt_psum"), sem("f_wt_copied"),
                                                                    sem("f_wt_stored"), sem("f_row_in"), sem("f_tri"))
        out_ready, out_stored = sem("f_out_ready"), sem("f_out_stored")
        with nc.Block() as block:
            @block.sync
            def _(sp):
                sp.dma_start(wr_b[:, :], wr["L1_ffn_wr"].rearrange("f a -> a f").to_broadcast([P, F])).then_inc(s_in, 16)
                sp.dma_start(br_b[:, :], wr["L1_ffn_br"].unsqueeze(0).to_broadcast([P, 1])).then_inc(s_in, 16)
                sp.dma_start(b2[:, :], wr["L1_ffn_b2"].unsqueeze(0).to_broadcast([P, F])).then_inc(s_in, 16)
                sp.dma_start(w2[:, :, :], wr["L1_ffn_w2"].rearrange("(q i) o -> i q o", i=128)).then_inc(w_in, 16)
                sp.wait_ge(wt_copied, 1)
                sp.dma_start(k.wt_dram, wtT[:, :]).then_inc(wt_stored, 16)
                sp.wait_ge(wt_stored, 16)
                sp.dma_start(w_row[:, :], k.wt_dram.rearrange("(a t) p -> a (t p)", a=1).to_broadcast([P, N])).then_inc(row_in, 16)
                for i in range(U):
                    sp.wait_ge(out_ready, i + 1)
                    sp.dma_start(k.out.rearrange("(t p) f -> p t f", p=P)[:, i * U:(i + 1) * U, :],
                                 R[:, i * U:(i + 1) * U, :]).then_inc(out_stored, 16)
                sp.wait_ge(out_stored, 16 * U)

            @block.gpsimd
            def _(pool):
                nc.gpsimd.affine_select(out=before[:, :], in_=k.ones[0:P, 0:P], compare_op=ALU.is_gt, fill=0.0, base=0,
                                        pattern=[[-1, P]], channel_multiplier=1)
                nc.gpsimd.drain().then_inc(tri_done, 1)

            @block.vector
            def _(dve):
                v.memset(eps[:, :], EPS)
                v.drain().then_inc(stats_done, 1)
                dve.wait_ge(std_done, 1)
                v.reciprocal(rstd[:, :], std[:, :])
                v.drain()
                normalize_batch(v, X, H, MV, rstd, 0, h_ready, t_ready, dve, True)
                normalize_batch(v, X, H, MV, rstd, 1, h_ready, t_ready, dve, False)
                dve.wait_ge(s_in, 48)
                with dve.Fori(0, U) as i:
                    for u in range(U):
                        t = i * U + u
                        v.tensor_scalar(prod[:, u, :], row_of(X, t), MV[:, bass.ds(t, 1), 0:1].rearrange("p a b -> p (a b)"),
                                        rstd[:, bass.ds(t, 1)], ALU.subtract, ALU.mult)
                    v.drain()
                    v.tensor_tensor(out=prod[:, :, :], in0=prod[:, :, :], in1=wr_b[:, :].unsqueeze(1).to_broadcast([P, U, F]), op=ALU.mult)
                    v.drain()
                    v.tensor_reduce(out=wt5[:, :], in_=prod[:, :, :], axis=AXX, op=ALU.add)
                    v.drain()
                    v.tensor_scalar(wt[:, bass.ds(i * U, U)], wt5[:, :], br_b[:, 0:1], None, ALU.add)
                    v.drain()
                v.nop().then_inc(wt_done, 1)
                with dve.Fori(0, U) as i:
                    for u in range(U):
                        t = i * U + u
                        v.tensor_scalar(prod[:, u, :], row_of(X, t), MV[:, bass.ds(t, 1), 0:1].rearrange("p a b -> p (a b)"),
                                        rstd[:, bass.ds(t, 1)], ALU.subtract, ALU.mult)
                    v.drain()
                    v.tensor_tensor(out=R[:, bass.ds(i * U, U), :], in0=X[:, bass.ds(i * U, U), :], in1=prod[:, :, :], op=ALU.add)
                    v.drain()

                normalize_batch(v, X, H, MV, rstd, 2, h_ready, t_ready, dve, False)

                for i in range(U):
                    if i == 0:
                        dve.wait_ge(row_in, 16)
                        dve.wait_ge(tri_done, 1)
                        v.memset(ge[:, 0:1], 0.0)
                    for t in range(i * U, (i + 1) * U):
                        c = t * P
                        if t:
                            v.tensor_scalar(junk[:, 0:c], w_row[:, 0:c], wt[:, t:t + 1], 0.0, ALU.is_ge, ALU.add, accum_out=ge[:, t:t + 1])
                            v.drain()
                        v.tensor_scalar(junk[:, c:N], w_row[:, c:N], wt[:, t:t + 1], 0.0, ALU.is_gt, ALU.add, accum_out=gt[:, t:t + 1])
                        v.drain()
                        v.scalar_tensor_tensor(out=junk[:, c:c + P], in0=w_row[:, c:c + P], scalar=wt[:, t:t + 1], in1=before[:, :],
                                               op0=ALU.is_equal, op1=ALU.mult, accum_out=tie[:, t:t + 1])
                        v.drain()
                    if i + 3 < U:
                        normalize_batch(v, X, H, MV, rstd, i + 3, h_ready, t_ready, dve, False)
                v.tensor_tensor(out=gt[:, :], in0=gt[:, :], in1=ge[:, :], op=ALU.add)
                v.drain()
                v.tensor_tensor(out=gt[:, :], in0=gt[:, :], in1=tie[:, :], op=ALU.add)
                v.drain()
                v.scalar_tensor_tensor(out=ws[:, :], in0=gt[:, :], scalar=float(TOPK), in1=wt[:, :], op0=ALU.is_lt, op1=ALU.mult)
                v.drain()

                with dve.Fori(0, U) as i:
                    rows = bass.ds(i * U, U)
                    dve.wait_ge(y_done, 3 * (i + 1))
                    v.tensor_tensor(out=Y[:, rows, :], in0=Y[:, rows, :], in1=b2[:, :].unsqueeze(1).to_broadcast([P, U, F]), op=ALU.add)
                    v.drain()
                    for u in range(U):
                        t = i * U + u
                        v.scalar_tensor_tensor(out=row_of(R, t), in0=row_of(Y, t), scalar=ws[:, bass.ds(t, 1)], in1=row_of(R, t),
                                               op0=ALU.mult, op1=ALU.add)
                    v.drain().then_inc(out_ready, 1)

            @block.scalar
            def _(act):
                act.sem_inc(f_out, 2)
                act.wait_ge(stats_done, 1)
                a.activation(std[:, :], MV[:, :, 1], ACT.Sqrt, bias=eps[:, 0:1])
                a.drain().then_inc(std_done, 1)

                def copies(i):
                    for b, tiles in enumerate(BANKS):
                        act.wait_ge(t_ready, 3 * i + b + 1)
                        n = len(tiles)
                        a.activation(HT[:, :, tiles[0] * P:(tiles[0] + n) * P].rearrange("p q (u c) -> p u q c", c=P),
                                     ps_t[:, b, 0:n * KF * P].rearrange("p (u q c) -> p u q c", u=n, c=P), ACT.Copy).then_inc(ht_ready, 1)

                def hidden(i):
                    m = 0
                    for o in range(HB8):
                        for lo, n in HALVES:
                            act.wait_ge(f_done, I1 * i + m + 1)
                            a.activation(A[:, o, lo:lo + n], ps_f[:, m % 2, 0:n], ACT.Gelu_apprx_tanh, bias=b1[:, o:o + 1]).then_inc(f_out, 1)
                            m += 1

                def results(i):
                    for b, tiles in enumerate(BANKS):
                        act.wait_ge(o_done, 3 * i + b + 1)
                        n = len(tiles)
                        a.activation(Y[:, bass.ds(i * U + tiles[0], n), :].rearrange("p t f -> p (t f)"), ps_o[0:P, b, 0:n * F], ACT.Copy)
                        a.drain().then_inc(y_done, 1)

                copies(0)
                hidden(0)
                copies(1)
                results(0)
                act.wait_ge(wt_psum, 1)
                a.activation(wtT[:, :], ps_t[0:T, 0, 0:P], ACT.Copy)
                a.drain().then_inc(wt_copied, 1)
                with act.Fori(2, U) as i:
                    hidden(i - 1)
                    copies(i)
                    results(i - 1)
                hidden(U - 1)
                results(U - 1)

            @block.tensor
            def _(pe):
                def hidden(i):
                    pe.wait_ge(ht_ready, 3 * (i + 1))
                    m = 0
                    for o in range(HB8):
                        for lo, n in HALVES:
                            pe.wait_ge(f_out, I1 * i + m + 1)
                            for q in range(KF):
                                last = t_.matmul(ps_f[:, m % 2, 0:n], w1[:, q, o * 128:(o + 1) * 128], HT[:, q, lo:lo + n],
                                                 start=(q == 0), stop=(q == KF - 1))
                            last.then_inc(f_done, 1)
                            m += 1

                def results(i, first):
                    pe.wait_ge(f_out, I1 * (i + 1) + 2)
                    for b, tiles in enumerate(BANKS):
                        if not first:
                            pe.wait_ge(y_done, 3 * (i - 1) + b + 1)
                        for s, u in enumerate(tiles):
                            for o in range(HB8):
                                last = t_.matmul(ps_o[0:P, b, s * F:(s + 1) * F], A[:, o, u * P:(u + 1) * P], w2[:, o, :],
                                                 start=(o == 0), stop=(o == HB8 - 1))
                        last.then_inc(o_done, 1)

                transpose_batch(pe, t_, k, H, ps_t, h_ready, ht_ready, t_ready, 0, True)
                hidden(0)
                transpose_batch(pe, t_, k, H, ps_t, h_ready, ht_ready, t_ready, 1, False)
                pe.wait_ge(w_in, 16)
                results(0, True)
                pe.wait_ge(wt_done, 1)
                pe.wait_ge(ht_ready, 6)
                t_.transpose(ps_t[0:T, 0, 0:P], wt[:, :], k.ident[0:P, 0:P]).then_inc(wt_psum, 1)
                pe.wait_ge(wt_copied, 1)
                with pe.Fori(2, U) as i:
                    hidden(i - 1)
                    transpose_batch(pe, t_, k, H, ps_t, h_ready, ht_ready, t_ready, i, False)
                    results(i - 1, False)
                hidden(U - 1)
                results(U - 1, False)


def enter_branch(nc):
    for engine in (nc.sync, nc.gpsimd, nc.vector, nc.scalar, nc.tensor):
        engine.nop()


def program(nc, **args):
    k = Env()
    k.nc = nc
    (k.x, k.src, k.dst, k.L0_gnn_W, k.L0_gnn_att) = (args[n] for n in ("x", "src", "dst", "L0_gnn_W", "L0_gnn_att"))
    k.args = args
    k.out = args["out"]

    def dram(name, shape, dt):
        return nc.dram_tensor(name, shape, dt, kind="Internal").ap()

    k.z_dram = dram("z_dram", [HEADS, T, P, DH + 1], FP32)
    k.es_dram = dram("es_dram", [T, HEADS, P], FP32)
    k.ed_dram = dram("ed_dram", [T, HEADS, P], FP32)
    k.key_dram = dram("key_dram", [SROWS, SEG], FP32)
    k.rows_dram = dram("rows_dram", [2, HEADS, T, P], FP32)
    k.wt_dram = dram("wt_dram", [T, P], FP32)
    k.counts = dram("counts", [N, N], BF16)
    k.countsT = dram("countsT", [N, N], BF16)
    k.counts_low = dram("counts_low", [N, N], BF16)
    k.countsT_low = dram("countsT_low", [N, N], BF16)
    with scope(nc) as (sb, pb, sem):
        k.rows_in, k.win_in, k.more_in = sem("rows_in"), sem("win_in"), sem("more_in")
        k.ident = sb("ident", [128, 128], FP32)
        k.ident_bf = sb("ident_bf", [128, 128], BF16)
        k.ones = sb("ones", [128, 128], FP32)
        k.iota_row = sb("iota_row", [128, P], BF16)
        k.es = sb("es", [P, T, HEADS], FP32)
        k.ed = sb("ed", [P, T, HEADS], FP32)
        k.mx = sb("mx", [P, T, HEADS], FP32)
        k.base = sb("base_seg", [P, U], FP32)
        k.rounds = sb("rounds", [1, 1], I32)
        k.rowG = sb("rowG", [128, NG // U, 2 * U], BF16)
        k.colG = sb("colG", [128, NG // U, 2 * U], BF16)
        k.MV = sb("row_stats", [P, T, 2], FP32)
        k.top = sb("es_top", [P, HEADS], FP32)
        k.es_mask = sb("es_mask", [P, T, HEADS], FP32)
        k.dst_exp = sb("dst_exp", [P, T, HEADS, 2], FP32)
        k.arena = sb("arena", [P, ARENA], BF16)
        setup_phase(k)
        edges_and_projection_phase(k)
        rounds = nc.values_load(k.rounds[0:1, 0:1], min_val=1, max_val=(SROWS * SEG) // WIN)
        count_phase(k)

        k.X = sb("X", [P, T, F], FP32)
        with nc.If_cmp(rounds.val, 2, "IS_GE"):
            enter_branch(nc)
            clear_low_phase(k)
            with nc.Fori(1, rounds) as r:
                more_windows_phase(k, r)
                more_counts_phase(k)
            transpose_counts_phase(k, "th_", k.counts, k.countsT, True)
            transpose_counts_phase(k, "tl_", k.counts_low, k.countsT_low, False)
            with nc.sbuf_tensor("gat_sums", [P, HEADS, T, DH + 1], FP32) as acc:
                k.acc = acc
                gat_attend_phase(k, "two_", [k.counts, k.counts_low])
                gat_finish_phase(k)
        with nc.Else():
            enter_branch(nc)
            gat_separable_phase(k)
        nc.end_all_ifs()
        moe_phase(k)
        k.pa, k.pb = (k.arena[:, n * T * X3:(n + 1) * T * X3].rearrange("p (t c) -> p t c", t=T) for n in range(2))
        k.ffn_w1 = sb("ffn_w1", [128, KF, HIDDEN], FP32)
        k.ffn_b1 = sb("ffn_b1", [128, HIDDEN // 128], FP32)
        with nc.sbuf_tensor("LNX", [P, T, F], FP32) as k.LNX:
            with nc.If_cmp(rounds.val, 2, "IS_GE"):
                enter_branch(nc)
                convolutions_phase(k, "two", [k.counts, k.counts_low], [k.countsT, k.countsT_low])
            with nc.Else():
                enter_branch(nc)
                convolutions_phase(k, "one", [k.counts], [k.countsT])
            nc.end_all_ifs()
        ffn_phase(k)


_INS = ['x', 'src', 'dst', 'L0_gnn_W', 'L0_gnn_att', 'L0_ffn_sW1', 'L0_ffn_sb1', 'L0_ffn_sW2', 'L0_ffn_sb2', 'L0_ffn_sW3',
        'L0_ffn_sb3', 'L0_ffn_eW1', 'L0_ffn_eb1', 'L0_ffn_eW2', 'L0_ffn_eb2', 'L0_ffn_eW3', 'L0_ffn_eb3', 'L0_ffn_gW',
        'L0_ffn_gb', 'L1_gnn_W1', 'L1_gnn_b1', 'L1_gnn_W2', 'L1_gnn_b2', 'L1_gnn_a', 'L1_ffn_wr', 'L1_ffn_br', 'L1_ffn_w1',
        'L1_ffn_b1', 'L1_ffn_w2', 'L1_ffn_b2']


def kernel(**inputs):
    import numpy as _np
    import concourse.bacc as _bacc
    from concourse import mybir as _mybir
    from concourse.bass_utils import run_bass_kernel_spmd as _run

    nc = _bacc.Bacc("TRN2", target_bir_lowering=False, num_devices=1)
    arrays, args = {}, {}
    for name in _INS:
        a = _np.ascontiguousarray(inputs[name])
        arrays[f"in_{name}_dram"] = a
        args[name] = nc.dram_tensor(f"in_{name}_dram", a.shape, _mybir.dt.from_np(a.dtype), kind="ExternalInput").ap()
    args["out"] = nc.dram_tensor("out_0_dram", (3125, 256), _mybir.dt.float32, kind="ExternalOutput").ap()
    program(nc, **args)
    r = _run(nc, [arrays], core_ids=[0])
    return r.results[0]["out_0_dram"]
```
